# Optimizing a Trainium2 kernel written in Bass

```python
import numpy as np
import jax
import jax.numpy as jnp

def _softmax(x, axis=-1):
    return jax.nn.softmax(x, axis=axis)

def _gelu(x):
    return jax.nn.gelu(x, approximate=True)

def _silu(x):
    return jax.nn.silu(x)

def _sigmoid(x):
    return jax.nn.sigmoid(x)

def _layernorm(x, axis=-1, eps=1e-05):
    m = jnp.mean(x, axis=axis, keepdims=True)
    v = jnp.var(x, axis=axis, keepdims=True)
    return (x - m) / jnp.sqrt(v + eps)

def _scatter_add(tgt, idx, src, axis=0):
    return tgt.at[idx].add(src)

def _segment_sum(src, seg, n):
    return jax.ops.segment_sum(src, seg, n)
kernel_name = 'mk_adj_ffn_d2_adj_r2_6a599c'

def setup_inputs(seed: int=0):
    np.random.seed(seed)
    _w = jnp.asarray

    def _rec_inputs():
        import jax
        import jax.numpy as jnp
        _gk = jax.random.key(seed)
        x = -0.0005207 + 1.001 * jax.random.normal(jax.random.fold_in(_gk, 1), (128, 128, 128), jnp.float32)
        _w = (1.0 + jnp.arange(128, dtype=jnp.float32)) ** (-0.5)
        _w = _w / _w.mean()
        _pij = jnp.clip(0.0625 * _w[:, None] * _w[None, :], 0.0, 1.0)
        _a = jax.random.uniform(jax.random.fold_in(_gk, 2), (128, 128, 128)) < _pij
        adj = _a.astype(jnp.int32)
        return (x, adj)
    x, adj = _rec_inputs()

    def _L0_gnn_setup():
        import jax, jax.numpy as jnp
        import numpy as np
        B, N, F_IN, F_OUT = (1, 4096, 128, 128)
        ALPHA = 0.2
        NEG_INF = -9000000000000000.0
        key = jax.random.key(seed)
        ks = jax.random.split(key, 8)
        feat = jax.random.normal(ks[0], (B, N, F_IN), dtype=jnp.float32)
        adj = jax.random.randint(ks[1], (B, N, N), 0, 2, dtype=jnp.int32)
        s = 1.414 * (6.0 / (F_IN + F_OUT)) ** 0.5
        W = jax.random.uniform(ks[2], (F_IN, F_OUT), minval=-s, maxval=s, dtype=jnp.float32)
        a_1 = jax.random.normal(ks[3], (F_OUT, 1), dtype=jnp.float32) * 0.1
        a_2 = jax.random.normal(ks[4], (F_OUT, 1), dtype=jnp.float32) * 0.1
        a_12 = jax.random.normal(ks[5], (F_OUT, F_OUT), dtype=jnp.float32) * (1.0 / F_OUT ** 0.5)
        W_1 = jax.random.uniform(ks[6], (F_IN, F_OUT), minval=-s, maxval=s, dtype=jnp.float32)
        W_2 = jax.random.uniform(ks[7], (F_IN, F_OUT), minval=-s, maxval=s, dtype=jnp.float32)
        return {'feat': feat, 'adj': adj, 'W': W, 'a_1': a_1, 'a_2': a_2, 'a_12': a_12, 'W_1': W_1, 'W_2': W_2}
    _L0_gnn_all = _L0_gnn_setup()
    _L0_gnn_in = {k: v for k, v in _L0_gnn_all.items() if k in ('W', 'a_1', 'a_2', 'a_12', 'W_1', 'W_2')}
    del _L0_gnn_all

    def _L0_ffn_setup():
        import math
        import jax, jax.numpy as jnp
        import numpy as np
        CAPACITY_FACTOR = 1.25
        key = jax.random.key(seed)
        ks = jax.random.split(key, 5)
        B, L, D, F, E = (8, 4096, 128, 512, 8)
        h = jax.random.normal(ks[0], (B, L, D), dtype=jnp.float32)
        gate_w = jax.random.normal(ks[1], (D, E), dtype=jnp.float32) * 0.02
        gate_b = jnp.zeros((E,), dtype=jnp.float32)
        w1 = jax.random.normal(ks[2], (E, D, F), dtype=jnp.float32) * (1.0 / math.sqrt(D))
        b1 = jnp.zeros((E, F), dtype=jnp.float32)
        w2 = jax.random.normal(ks[3], (E, F, D), dtype=jnp.float32) * (1.0 / math.sqrt(F))
        b2 = jnp.zeros((E, D), dtype=jnp.float32)
        return {'h': h, 'gate_w': gate_w, 'gate_b': gate_b, 'w1': w1, 'b1': b1, 'w2': w2, 'b2': b2}
    _L0_ffn_all = _L0_ffn_setup()
    _L0_ffn_in = {k: v for k, v in _L0_ffn_all.items() if k in ('gate_w', 'gate_b', 'w1', 'b1', 'w2', 'b2')}
    del _L0_ffn_all

    def _L1_gnn_setup():
        import jax, jax.numpy as jnp
        import numpy as np
        NEG_INF = -1000000000000.0
        ALPHA = 0.2
        key = jax.random.key(seed)
        k1, k2, k3, k4, k5 = jax.random.split(key, 5)
        B, N, Cin, Cout = (8, 1024, 128, 128)
        x = jax.random.normal(k1, (B, N, Cin), dtype=jnp.float32)
        mask = jax.random.randint(k2, (B, N, N), 0, 2, dtype=jnp.int32)
        W = jax.random.normal(k3, (Cout, Cin), dtype=jnp.float32) * Cin ** (-0.5)
        a = jax.random.normal(k4, (2, Cout), dtype=jnp.float32) * Cout ** (-0.5)
        bias = jax.random.normal(k5, (Cout,), dtype=jnp.float32)
        return {'x': x, 'mask': mask, 'W': W, 'a': a, 'bias': bias}
    _L1_gnn_all = _L1_gnn_setup()
    _L1_gnn_in = {k: v for k, v in _L1_gnn_all.items() if k in ('W', 'a', 'bias')}
    del _L1_gnn_all

    def _L1_ffn_setup():
        import jax, jax.numpy as jnp
        import numpy as np
        B, N, D = (16, 2048, 128)
        NUM_EXPERTS, TOP_K, HEADS = (4, 2, 4)
        N_EDGES = 524288
        LN_EPS = 1e-05

        def _layernorm(x, g, b):
            mu = x.mean(-1, keepdims=True)
            var = ((x - mu) ** 2).mean(-1, keepdims=True)
            return (x - mu) * jax.lax.rsqrt(var + LN_EPS) * g + b

        def _forward(x, edge_index, W_gat, att_src, att_dst, b_gat, ln_gamma, ln_beta, W1, b1, W2, b2):
            Bc, Nc, Dc = x.shape
            M = Bc * Nc
            x_flat = x.reshape(M, Dc)
            h = (x_flat @ W_gat).reshape(M, HEADS, NUM_EXPERTS)
            loops = jnp.arange(M, dtype=edge_index.dtype)
            src = jnp.concatenate([edge_index[0], loops])
            dst = jnp.concatenate([edge_index[1], loops])
            a_src = (h * att_src).sum(-1)
            a_dst = (h * att_dst).sum(-1)
            e = jax.nn.leaky_relu(a_src[src] + a_dst[dst], negative_slope=0.2)
            e_max = jax.ops.segment_max(e, dst, num_segments=M)
            ee = jnp.exp(e - e_max[dst])
            denom = jax.ops.segment_sum(ee, dst, num_segments=M)
            alpha = ee / (denom[dst] + 1e-16)
            msg = h[src] * alpha[:, :, None]
            agg = jax.ops.segment_sum(msg, dst, num_segments=M).reshape(M, HEADS * NUM_EXPERTS) + b_gat
            scores = _layernorm(agg, ln_gamma, ln_beta).reshape(M, HEADS, NUM_EXPERTS).mean(1)
            scores = scores.reshape(Bc, Nc, NUM_EXPERTS)
            topk_s, topk_i = jax.lax.top_k(scores, TOP_K)
            w = jax.nn.softmax(topk_s, axis=-1)
            out = jnp.zeros_like(x)
            for ei in range(NUM_EXPERTS):
                g = jnp.where(topk_i == ei, w, 0.0).sum(-1)
                hh = jax.nn.gelu(x @ W1[ei] + b1[ei], approximate=False)
                out = out + g[..., None] * (hh @ W2[ei] + b2[ei])
            return out
        key = jax.random.key(seed)
        ks = jax.random.split(key, 8)
        s = 0.05
        return {'x': jax.random.normal(ks[0], (B, N, D), jnp.float32), 'W_gat': jax.random.normal(ks[1], (D, HEADS * NUM_EXPERTS), jnp.float32) * s, 'att_src': jax.random.normal(ks[2], (HEADS, NUM_EXPERTS), jnp.float32) * s, 'att_dst': jax.random.normal(ks[3], (HEADS, NUM_EXPERTS), jnp.float32) * s, 'b_gat': jnp.zeros((HEADS * NUM_EXPERTS,), jnp.float32), 'ln_gamma': jnp.ones((HEADS * NUM_EXPERTS,), jnp.float32), 'ln_beta': jnp.zeros((HEADS * NUM_EXPERTS,), jnp.float32), 'W1': jax.random.normal(ks[4], (NUM_EXPERTS, D, 2 * D), jnp.float32) * s, 'b1': jnp.zeros((NUM_EXPERTS, 2 * D), jnp.float32), 'W2': jax.random.normal(ks[5], (NUM_EXPERTS, 2 * D, D), jnp.float32) * s, 'b2': jnp.zeros((NUM_EXPERTS, D), jnp.float32), 'edge_index': jax.random.randint(ks[6], (2, N_EDGES), 0, B * N, jnp.int32)}
    _L1_ffn_all = _L1_ffn_setup()
    _L1_ffn_in = {k: v for k, v in _L1_ffn_all.items() if k in ('W_gat', 'att_src', 'att_dst', 'b_gat', 'ln_gamma', 'ln_beta', 'W1', 'b1', 'W2', 'b2', 'edge_index')}
    del _L1_ffn_all
    return {'x': x, 'adj': adj, 'L0_gnn_W': _L0_gnn_in['W'], 'L0_gnn_a_1': _L0_gnn_in['a_1'], 'L0_gnn_a_2': _L0_gnn_in['a_2'], 'L0_gnn_a_12': _L0_gnn_in['a_12'], 'L0_gnn_W_1': _L0_gnn_in['W_1'], 'L0_gnn_W_2': _L0_gnn_in['W_2'], 'L0_ffn_gate_w': _L0_ffn_in['gate_w'], 'L0_ffn_gate_b': _L0_ffn_in['gate_b'], 'L0_ffn_w1': _L0_ffn_in['w1'], 'L0_ffn_b1': _L0_ffn_in['b1'], 'L0_ffn_w2': _L0_ffn_in['w2'], 'L0_ffn_b2': _L0_ffn_in['b2'], 'L1_gnn_W': _L1_gnn_in['W'], 'L1_gnn_a': _L1_gnn_in['a'], 'L1_gnn_bias': _L1_gnn_in['bias'], 'L1_ffn_W_gat': _L1_ffn_in['W_gat'], 'L1_ffn_att_src': _L1_ffn_in['att_src'], 'L1_ffn_att_dst': _L1_ffn_in['att_dst'], 'L1_ffn_b_gat': _L1_ffn_in['b_gat'], 'L1_ffn_ln_gamma': _L1_ffn_in['ln_gamma'], 'L1_ffn_ln_beta': _L1_ffn_in['ln_beta'], 'L1_ffn_W1': _L1_ffn_in['W1'], 'L1_ffn_b1': _L1_ffn_in['b1'], 'L1_ffn_W2': _L1_ffn_in['W2'], 'L1_ffn_b2': _L1_ffn_in['b2'], 'L1_ffn_edge_index': _L1_ffn_in['edge_index']}

def reference(x, adj, L0_gnn_W, L0_gnn_a_1, L0_gnn_a_2, L0_gnn_a_12, L0_gnn_W_1, L0_gnn_W_2, L0_ffn_gate_w, L0_ffn_gate_b, L0_ffn_w1, L0_ffn_b1, L0_ffn_w2, L0_ffn_b2, L1_gnn_W, L1_gnn_a, L1_gnn_bias, L1_ffn_W_gat, L1_ffn_att_src, L1_ffn_att_dst, L1_ffn_b_gat, L1_ffn_ln_gamma, L1_ffn_ln_beta, L1_ffn_W1, L1_ffn_b1, L1_ffn_W2, L1_ffn_b2, L1_ffn_edge_index):
    import jax
    import jax.numpy as jnp

    def _L0_gnn_ref(feat, adj, W, a_1, a_2, a_12, W_1, W_2):
        import jax, jax.numpy as jnp
        import numpy as np
        B, N, F_IN, F_OUT = (1, 4096, 128, 128)
        ALPHA = 0.2
        NEG_INF = -9000000000000000.0
        h = jnp.matmul(feat, W)
        Ax = jnp.matmul(h, a_1)
        Ay = jnp.matmul(h, a_2)
        A_xy = jnp.matmul(jnp.matmul(h, a_12), jnp.swapaxes(h, 1, 2))
        logits = jnp.swapaxes(Ax, 1, 2) + Ay + A_xy
        e = jax.nn.leaky_relu(logits, negative_slope=ALPHA)
        e = jnp.where(adj > 0, e, NEG_INF)
        attention = jax.nn.softmax(e, axis=-1)
        h_prime = jnp.matmul(attention, feat)
        h_out = jnp.matmul(feat, W_1) + jnp.matmul(h_prime, W_2)
        return jax.nn.elu(h_out)

    def _L0_ffn_ref(h, gate_w, gate_b, w1, b1, w2, b2):
        import math
        import jax, jax.numpy as jnp
        import numpy as np
        CAPACITY_FACTOR = 1.25
        B, L, D = h.shape
        E = gate_w.shape[1]
        T = B * L
        C = max(1, math.ceil(CAPACITY_FACTOR * T / E))
        x = h.reshape(T, D)
        logits = x @ gate_w + gate_b
        probs = jax.nn.softmax(logits, axis=-1)
        idx = jnp.argmax(probs, axis=-1)
        prb = jnp.take_along_axis(probs, idx[:, None], axis=1)[:, 0]
        one_hot = jax.nn.one_hot(idx, E, dtype=jnp.float32)
        pos = (jnp.cumsum(one_hot, axis=0) * one_hot).sum(-1).astype(jnp.int32) - 1
        kept = pos < C
        pos_safe = jnp.where(kept, pos, C)
        buf = jnp.zeros((E, C, D), dtype=h.dtype).at[idx, pos_safe].set(x, mode='drop')
        hmid = jax.nn.relu(jnp.einsum('ecd,edf->ecf', buf, w1) + b1[:, None, :])
        ybuf = jnp.einsum('ecf,efd->ecd', hmid, w2) + b2[:, None, :]
        pos_g = jnp.minimum(pos, C - 1)
        y_tok = ybuf[idx, pos_g] * (prb * kept)[:, None]
        y = y_tok.reshape(B, L, D)
        y = jnp.nan_to_num(y, nan=0.0, posinf=10000.0, neginf=-10000.0)
        return y

    def _L1_gnn_ref(x, mask, W, a, bias):
        import jax, jax.numpy as jnp
        import numpy as np
        NEG_INF = -1000000000000.0
        ALPHA = 0.2
        hidden = jnp.einsum('bni,oi->bno', x, W)
        av = jnp.einsum('bno,ko->bnk', hidden, a)
        attn1, attn2 = (av[..., 0], av[..., 1])
        attn = attn1[:, :, None] + attn2[:, None, :]
        attn = jax.nn.leaky_relu(attn, negative_slope=ALPHA)
        attn = jnp.where(mask > 0, attn, attn + NEG_INF)
        attn = jax.nn.softmax(attn, axis=-1)
        out = jnp.einsum('bnm,bmo->bno', attn, hidden) + bias
        return out

    def _L1_ffn_ref(x, W_gat, att_src, att_dst, b_gat, ln_gamma, ln_beta, W1, b1, W2, b2, edge_index):
        import jax, jax.numpy as jnp
        import numpy as np
        B, N, D = (16, 2048, 128)
        NUM_EXPERTS, TOP_K, HEADS = (4, 2, 4)
        N_EDGES = 524288
        LN_EPS = 1e-05

        def _layernorm(x, g, b):
            mu = x.mean(-1, keepdims=True)
            var = ((x - mu) ** 2).mean(-1, keepdims=True)
            return (x - mu) * jax.lax.rsqrt(var + LN_EPS) * g + b

        def _forward(x, edge_index, W_gat, att_src, att_dst, b_gat, ln_gamma, ln_beta, W1, b1, W2, b2):
            Bc, Nc, Dc = x.shape
            M = Bc * Nc
            x_flat = x.reshape(M, Dc)
            h = (x_flat @ W_gat).reshape(M, HEADS, NUM_EXPERTS)
            loops = jnp.arange(M, dtype=edge_index.dtype)
            src = jnp.concatenate([edge_index[0], loops])
            dst = jnp.concatenate([edge_index[1], loops])
            a_src = (h * att_src).sum(-1)
            a_dst = (h * att_dst).sum(-1)
            e = jax.nn.leaky_relu(a_src[src] + a_dst[dst], negative_slope=0.2)
            e_max = jax.ops.segment_max(e, dst, num_segments=M)
            ee = jnp.exp(e - e_max[dst])
            denom = jax.ops.segment_sum(ee, dst, num_segments=M)
            alpha = ee / (denom[dst] + 1e-16)
            msg = h[src] * alpha[:, :, None]
            agg = jax.ops.segment_sum(msg, dst, num_segments=M).reshape(M, HEADS * NUM_EXPERTS) + b_gat
            scores = _layernorm(agg, ln_gamma, ln_beta).reshape(M, HEADS, NUM_EXPERTS).mean(1)
            scores = scores.reshape(Bc, Nc, NUM_EXPERTS)
            topk_s, topk_i = jax.lax.top_k(scores, TOP_K)
            w = jax.nn.softmax(topk_s, axis=-1)
            out = jnp.zeros_like(x)
            for ei in range(NUM_EXPERTS):
                g = jnp.where(topk_i == ei, w, 0.0).sum(-1)
                hh = jax.nn.gelu(x @ W1[ei] + b1[ei], approximate=False)
                out = out + g[..., None] * (hh @ W2[ei] + b2[ei])
            return out
        return _forward(x, edge_index, W_gat, att_src, att_dst, b_gat, ln_gamma, ln_beta, W1, b1, W2, b2)
    x = x + _L0_gnn_ref(_layernorm(x, axis=-1), adj, L0_gnn_W, L0_gnn_a_1, L0_gnn_a_2, L0_gnn_a_12, L0_gnn_W_1, L0_gnn_W_2)
    x = x + _L0_ffn_ref(_layernorm(x, axis=-1), L0_ffn_gate_w, L0_ffn_gate_b, L0_ffn_w1, L0_ffn_b1, L0_ffn_w2, L0_ffn_b2)
    x = x + _L1_gnn_ref(_layernorm(x, axis=-1), adj, L1_gnn_W, L1_gnn_a, L1_gnn_bias)
    x = x + _L1_ffn_ref(_layernorm(x, axis=-1), L1_ffn_W_gat, L1_ffn_att_src, L1_ffn_att_dst, L1_ffn_b_gat, L1_ffn_ln_gamma, L1_ffn_ln_beta, L1_ffn_W1, L1_ffn_b1, L1_ffn_W2, L1_ffn_b2, L1_ffn_edge_index)
    return x

_drawn_inputs = setup_inputs


def setup_inputs(seed=0):
    import zlib

    import numpy as np

    out = dict(_drawn_inputs(seed))
    spreads = {'L0_ffn_gate_b': (0.0, 0.1),
     'L0_ffn_b1': (0.0, 0.8),
     'L0_ffn_b2': (0.0, 0.8),
     'L1_ffn_b_gat': (0.0, 0.1),
     'L1_ffn_ln_gamma': (1.0, 0.6),
     'L1_ffn_ln_beta': (0.0, 0.1),
     'L1_ffn_b1': (0.0, 0.478),
     'L1_ffn_b2': (0.0, 0.1)}
    factors = {'L0_gnn_a_2': 6.842, 'L1_ffn_att_src': 8.0, 'L1_ffn_att_dst': 8.0}
    for name, (base, spread) in spreads.items():
        noise = np.random.default_rng([zlib.crc32(name.encode()), seed]).standard_normal(out[name].shape)
        drawn = base * np.exp(spread * noise) if base else spread * noise
        out[name] = jnp.asarray(drawn.astype(out[name].dtype))
    for name, factor in factors.items():
        out[name] = (out[name] * factor).astype(out[name].dtype)
    return out
```

```python
from contextlib import ExitStack

import concourse.bass as bass
from concourse import mybir

ALU = mybir.AluOpType
ACT = mybir.ActivationFunctionType
F32 = mybir.dt.float32
BF16 = mybir.dt.bfloat16
I32 = mybir.dt.int32
U32 = mybir.dt.uint32
AX_X = mybir.AxisListType.X

P = 128
GRAPHS = NODES = FEAT = 128
PER = 4
GROUPS = GRAPHS // PER
WIDE = PER * FEAT
EPS = 1e-5
SLOPE = 0.2
TOKENS = GRAPHS * NODES

EXPERTS = 8
HIDDEN = 512
HC = HIDDEN // P
CAPACITY = (5 * TOKENS + 4 * EXPERTS - 1) // (4 * EXPERTS)
SLOT_GROUPS = CAPACITY // WIDE

EDGES = 524288
COLS = EDGES // P
LOG_COLS = COLS.bit_length() - 1
LOG_EDGES = EDGES.bit_length() - 1
NODE_BIT = TOKENS
LOG_NODES = TOKENS.bit_length() - 1
KEY_INSIDE = 1 << 28
KEY_CLAMPED = 2 << 28
KEY_DROPPED = 3 << 28
FAN = 64
SEARCHES = 2 * NODES
PER_SEARCH = SEARCHES // GROUPS
HEADS = 4
TOP_EXPERTS = 4
GAT = HEADS * TOP_EXPERTS
ROW = GAT + HEADS
TAB = ROW + HEADS
WINDOW = 24
EDGE_TILES = 8
EDGE_STEP = EDGE_TILES * P
CLEAR = 2560
HIDDEN1 = 256
HC1 = HIDDEN1 // P
BIG = 1e30


def ge(engine, semaphore, value):
    if isinstance(value, int) and value <= 0:
        return
    engine.wait_ge(semaphore, value)


def across(ap, n):
    return bass.AP(ap.tensor, 0, [[0, P], [1, n]])


def pipeline(engine, first, step, total=GROUPS):
    for n in range(first, 4):
        step(n, n % 4)
    with engine.Fori(1, total // 4 - 1) as turn:
        for u in range(4):
            step(turn * 4 + u, u)
    for n in range(total - 4, total):
        step(n, n % 4)


def live(n, total=GROUPS):
    return not isinstance(n, int) or 0 <= n < total


def sort_edges(nc, sem, edge_index, keys_dram, coarse_dram, starts, counted, source_ids, ident, row_id, clear):
    HALF = COLS // 2
    BLOCKS = COLS // P
    with ExitStack() as ctx:
        ping = ctx.enter_context(nc.sbuf_tensor("sort_ping", [P, COLS], F32))
        pong = ctx.enter_context(nc.sbuf_tensor("sort_pong", [P, COLS], F32))
        sense = ctx.enter_context(nc.sbuf_tensor("sort_sense", [P, 8], F32))
        bits = ctx.enter_context(nc.sbuf_tensor("sort_bits", [P, 8], I32))
        small = ctx.enter_context(nc.sbuf_tensor("sort_small", [P, 2 * FAN], F32))
        zeros = ctx.enter_context(nc.sbuf_tensor("zeros", [P, CLEAR], F32))
        zeroed, cleared = sem("zeroed"), sem("tables_cleared")
        turned = ctx.enter_context(nc.psum_tensor("sort_turned", [P, 8, 512], F32))
        edges_in, made, half_ready = sem("edges_in"), sem("sort_step"), sem("half_ready")
        half_turned, half_copied, keys_out = sem("half_turned"), sem("half_copied"), sem("keys_out")
        sorted_s, coarse_s, starts_turned, starts_s = sem("sorted"), sem("coarse"), sem("starts_turned"), sem("starts")
        turns = [(k, back, h) for k in range(LOG_COLS + 1, LOG_EDGES + 1) for back in (0, 1) for h in (0, 1)]
        source = ping[:, :].bitcast(I32)
        target = pong[:, :].bitcast(I32)
        from_to = {}
        block = ctx.enter_context(nc.Block())

        @block.sync
        def _(sp):
            sp.dma_start(source, edge_index[0, :].rearrange("(p f) -> p f", p=P)).then_inc(edges_in, 16)
            sp.dma_start(target, edge_index[1, :].rearrange("(p f) -> p f", p=P)).then_inc(edges_in, 16)
            sp.wait_ge(zeroed, 1)
            sent = 0
            for table in clear:
                flat = table.rearrange("(p r) d -> p (r d)", p=P)
                for c in range(0, flat.shape[1], CLEAR):
                    width = min(CLEAR, flat.shape[1] - c)
                    sp.dma_start(flat[:, c:c + width], zeros[:, 0:width]).then_inc(cleared, 16)
                    sent += 16
            sp.wait_ge(cleared, sent)

        @block.vector
        def _(dve):
            steps = [0]

            def step(ins):
                ins.then_inc(made, 1)
                steps[0] += 1

            def join():
                dve.wait_ge(made, steps[0])

            def link(ins):
                step(ins)
                join()

            for b in range(7):
                step(dve.tensor_scalar(bits[:, b:b + 1], row_id, b, 1, ALU.logical_shift_right, ALU.bitwise_and))
            join()
            link(dve.tensor_scalar(sense[:, 0:7], bits[:, 0:7], -2.0, 1.0, ALU.mult, ALU.add))
            dve.wait_ge(edges_in, 32)
            with nc.sbuf_tensor("sort_part", [P, COLS], I32) as part, nc.sbuf_tensor("sort_key", [P, COLS], I32) as key:
                beyond = NODE_BIT
                inner = NODE_BIT - 1
                link(dve.tensor_scalar(part[:, :], target, inner, LOG_NODES, ALU.bitwise_and, ALU.logical_shift_left))
                link(dve.scalar_tensor_tensor(key[:, :], source, inner, part[:, :], ALU.bitwise_and, ALU.bitwise_or))
                link(dve.tensor_tensor(part[:, :], source, target, ALU.bitwise_or))
                link(dve.tensor_scalar(part[:, :], part[:, :], beyond, 15, ALU.bitwise_and, ALU.logical_shift_left))
                link(dve.tensor_tensor(key[:, :], key[:, :], part[:, :], ALU.bitwise_or))
                link(dve.scalar_tensor_tensor(part[:, :], source, beyond, target, ALU.bitwise_xor, ALU.bitwise_or))
                link(dve.tensor_scalar(part[:, :], part[:, :], beyond, 14, ALU.bitwise_and, ALU.logical_shift_left))
                link(dve.tensor_tensor(source, key[:, :], part[:, :], ALU.bitwise_or))

            def both_ways(k, j, a, b):
                c, m, n = 1 << j, 1 << (k - 1 - j), COLS >> (k + 1)
                va = a[:, :].rearrange("p (n d m t c) -> p n d m t c", n=n, d=2, m=m, t=2, c=c)
                vb = b[:, :].rearrange("p (n d m t c) -> p n d m t c", n=n, d=2, m=m, t=2, c=c)
                for d in (0, 1):
                    ops = (ALU.max, ALU.min) if d else (ALU.min, ALU.max)
                    for t in (0, 1):
                        step(dve.tensor_tensor(vb[:, :, d, :, t, :], va[:, :, d, :, 0, :], va[:, :, d, :, 1, :], ops[t]))
                join()

            def upwards(a, b, c):
                va = a.rearrange("p (m t c) -> p m t c", t=2, c=c)
                vb = b.rearrange("p (m t c) -> p m t c", t=2, c=c)
                for t, op in ((0, ALU.min), (1, ALU.max)):
                    step(dve.tensor_tensor(vb[:, :, t, :], va[:, :, 0, :], va[:, :, 1, :], op))
                join()

            a, b = ping, pong
            for k in range(1, LOG_COLS):
                for j in range(k - 1, -1, -1):
                    both_ways(k, j, a, b)
                    a, b = b, a
            n = 0
            for k in range(LOG_COLS, LOG_EDGES + 1):
                if k > LOG_COLS:
                    link(dve.tensor_scalar(b[:, :], a[:, :], sense[:, k - 1 - LOG_COLS:k - LOG_COLS], None, ALU.mult))
                    a, b = b, a
                if k < LOG_EDGES:
                    link(dve.tensor_scalar(b[:, :], a[:, :], sense[:, k - LOG_COLS:k - LOG_COLS + 1], None, ALU.mult))
                    a, b = b, a
                if k > LOG_COLS:
                    from_to[n] = from_to[n + 1] = (a, b)
                    dve.tensor_copy(bits[:, 7:8], bits[:, 0:1]).then_inc(half_ready, 2)
                    a, b = b, a
                    for h in (0, 1):
                        cols = slice(h * HALF, (h + 1) * HALF)
                        dve.wait_ge(half_copied, n + h + 1)
                        x, y = a, b
                        for j in range(k - 1, LOG_COLS - 1, -1):
                            upwards(x[:, cols], y[:, cols], 1 << (j - LOG_COLS))
                            x, y = y, x
                        from_to[n + 2 + h] = (x, y)
                        dve.tensor_copy(bits[:, 7:8], bits[:, 0:1]).then_inc(half_ready, 1)
                    a, b = y, x
                    n += 4
                    dve.wait_ge(half_copied, n)
                for j in range(LOG_COLS - 1, -1, -1):
                    upwards(a[:, :], b[:, :], 1 << j)
                    a, b = b, a
            from_to["sorted"] = from_to[n] = from_to[n + 1] = (a, b)
            link(dve.tensor_copy(small[:, 0:FAN], a[:, 0:COLS:FAN]))
            dve.tensor_copy(bits[:, 7:8], bits[:, 0:1]).then_inc(sorted_s, 1)
            link(dve.tensor_scalar(bits[:, 6:7], row_id, 0, KEY_DROPPED, ALU.bitwise_and, ALU.bitwise_or))
            link(dve.tensor_scalar(pong[:, :] if a is ping else ping[:, :], a[:, :], bits[:, 6:7].bitcast(F32), None, ALU.is_lt))
            link(dve.tensor_reduce(counted, (pong if a is ping else ping)[:, :], AX_X, ALU.add))
            dve.tensor_copy(bits[:, 7:8], bits[:, 0:1]).then_inc(half_ready, 2)
            dve.wait_ge(starts_turned, 1)
            link(dve.tensor_copy(starts[:, :], turned[:, 0, 0:P]))
            dve.tensor_copy(bits[:, 7:8], bits[:, 0:1]).then_inc(starts_s, 1)
            dve.wait_ge(half_copied, n + 2)
            tiles = (pong if a is ping else ping)[:, :].bitcast(U32)
            link(dve.tensor_scalar(source_ids[:, 0:COLS].rearrange("q (p b) -> q b p", b=BLOCKS),
                                   tiles.rearrange("q (b p) -> q b p", p=P), NODE_BIT - 1, None, ALU.bitwise_and))

        @block.tensor
        def _(pe):
            total = len(turns)
            for n in range(total + 2):
                if n == total:
                    pe.wait_ge(sorted_s, 1)
                    pe.wait_ge(half_copied, total)
                    pe.transpose(turned[:, 0, 0:P], from_to["sorted"][0][:, 0:1].to_broadcast([P, P]), ident).then_inc(starts_turned, 1)
                    pe.wait_ge(starts_s, 1)
                pe.wait_ge(half_ready, n + 1 if n % 4 else n + 2)
                ge(pe, half_copied, n - 1)
                h = n % 2
                for blk in range(h * BLOCKS // 2, (h + 1) * BLOCKS // 2):
                    last = pe.transpose(turned[:, blk // 4, (blk % 4) * P:(blk % 4 + 1) * P],
                                        from_to[n][0][:, blk * P:(blk + 1) * P], ident)
                last.then_inc(half_turned, 1)

        @block.scalar
        def _(act):
            for n in range(len(turns) + 2):
                act.wait_ge(half_turned, n + 1)
                for bank in range(4 * (n % 2), 4 * (n % 2) + 4):
                    last = act.activation(from_to[n][1][:, bank * 512:bank * 512 + 512], turned[:, bank, :], ACT.Copy)
                last.then_inc(half_copied, 1)

        @block.gpsimd
        def _(pool):
            pool.memset(zeros[:, :], 0.0).then_inc(zeroed, 1)
            pool.wait_ge(sorted_s, 1)
            pool.dma_start(keys_dram.rearrange("(p b) f -> p (b f)", p=P), from_to["sorted"][0][:, :]).then_inc(keys_out, 16)
            pool.dma_start(coarse_dram, small[:, 0:FAN]).then_inc(keys_out, 16)
            pool.wait_ge(keys_out, 32)


def finish_norm(nc, sem, stats, scratch, rstd, shift, tag):
    made, rooted = sem(f"norm_step_{tag}"), sem(f"norm_root_{tag}")
    even, odd = stats[:, :, 1], stats[:, :, 4]
    with nc.Block() as block:
        @block.vector
        def _(dve):
            steps = [0]

            def link(ins):
                ins.then_inc(made, 1)
                steps[0] += 1
                dve.wait_ge(made, steps[0])

            link(dve.tensor_tensor(scratch[:, 0, :], even, odd, ALU.subtract))
            link(dve.scalar_tensor_tensor(scratch[:, 1, :], scratch[:, 0, :], 0.25, scratch[:, 0, :], ALU.mult, ALU.mult))
            link(dve.tensor_tensor(scratch[:, 0, :], stats[:, :, 2], stats[:, :, 5], ALU.add))
            link(dve.scalar_tensor_tensor(scratch[:, 2, :], scratch[:, 0, :], 1.0 / FEAT, scratch[:, 1, :], ALU.mult, ALU.add))
            link(dve.tensor_scalar(scratch[:, 2, :], scratch[:, 2, :], EPS, None, ALU.add))
            dve.wait_ge(rooted, 1)
            link(dve.reciprocal(rstd[:, :], scratch[:, 1, :]))
            link(dve.tensor_tensor(scratch[:, 0, :], even, odd, ALU.add))
            link(dve.scalar_tensor_tensor(shift[:, :], scratch[:, 0, :], -0.5, rstd[:, :], ALU.mult, ALU.mult))

        @block.scalar
        def _(act):
            act.wait_ge(made, 5)
            act.activation(scratch[:, 1, :], scratch[:, 2, :], ACT.Sqrt).then_inc(rooted, 1)


def normalise(act, out, x, rstd, shift, g):
    for u in range(PER):
        b = g * PER + u
        last = act.activation(out[:, u, :], x[:, bass.ds(b, 1), :].rearrange("p o f -> p (o f)"), ACT.Identity,
                              bias=shift[:, bass.ds(b, 1)], scale=rstd[:, bass.ds(b, 1)])
    return last


def graph_attention(nc, sem, layer, x, masked, stats, rstd, shift, ident, w, search):
    first = layer == 0
    fill = -9e15 if first else -1e12
    with ExitStack() as ctx:
        def sb(name, shape, dt=F32):
            return ctx.enter_context(nc.sbuf_tensor(f"{name}{layer}", shape, dt))

        def bank(name):
            return ctx.enter_context(nc.psum_tensor(f"{name}{layer}", [P, PER, P], F32))

        def s(name):
            return sem(f"g{layer}_{name}")

        feat = sb("feat", [P, 2, PER, FEAT])
        featT = sb("featT", [P, 4, PER, NODES])
        right = sb("right", [P, 4, PER, FEAT])
        queries = sb("queries", [P, 2, PER, NODES])
        low = sb("low", [P, PER, NODES])
        score = sb("score", [P, PER, NODES])
        probs = sb("probs", [P, 2, PER, NODES])
        probsT = sb("probsT", [P, PER, NODES])
        row = sb("row", [P, 3, PER])
        under = sb("under", [P, PER, FEAT])
        grown = sb("grown", [P, PER, FEAT])
        summed = sb("summed", [P, PER, FEAT])
        chosen = sb("chosen", [P, 2, PER_SEARCH], U32)
        fetched = sb("fetched", [P, 2, PER_SEARCH, FAN])
        before = sb("before", [P, PER_SEARCH, FAN])
        b_featT, b_queries, b_right, b_score, b_probsT, b_out = map(
            bank, ("b_featT", "b_queries", "b_right", "b_score", "b_probsT", "b_out"))
        normed, turned, featT_s, asked, queries_s, righted, right_s = map(
            s, ("normed", "turned", "featT", "asked", "queries", "righted", "right"))
        scored, low_s, score_s, shifted, exped, probs_s, probs_turned, probsT_s, out_s = map(
            s, ("scored", "low", "score", "shifted", "exped", "probs", "probs_turned", "probsT", "out"))
        under_s, grown_s, out_read, updated, stats_s = map(s, ("under", "grown", "out_read", "updated", "stats"))
        chain_b, chain_s, begun = s("chain_b"), s("chain_s"), s("begun")
        chosen_s, fetched_s, looked = s("chosen"), (s("fetched_even"), s("fetched_odd")), s("looked")
        table, row_ids, wanted, counts = search
        block = ctx.enter_context(nc.Block())

        @block.scalar
        def _(act):
            def step(n, u):
                b, a, f = n + 1, n + 2, n + 3
                if live(b):
                    act.wait_ge(scored, b + 1)
                    ge(act, score_s, b)
                    act.activation(low[:, :, :], b_score[:, :, :], ACT.Copy, scale=SLOPE).then_inc(low_s, 1)
                if live(n):
                    act.wait_ge(probs_turned, n + 1)
                    ge(act, out_s, n)
                    act.activation(probsT[:, :, :], b_probsT[:, :, :], ACT.Copy).then_inc(probsT_s, 1)
                if live(a):
                    act.wait_ge(turned, a + 1)
                    ge(act, out_s, a - 3)
                    act.activation(featT[:, (u + 2) % 4, :, :], b_featT[:, :, :], ACT.Copy).then_inc(featT_s, 1)
                if live(n) and first:
                    act.wait_ge(under_s, n + 1)
                    ge(act, updated, n)
                    act.activation(grown[:, :, :], under[:, :, :], ACT.Exp).then_inc(grown_s, 1)
                if live(b):
                    act.wait_ge(shifted, b + 1)
                    ge(act, probs_turned, b - 1)
                    act.activation(probs[:, (u + 1) % 2, :, :], score[:, :, :], ACT.Exp).then_inc(exped, 1)
                if live(a) and first:
                    act.wait_ge(righted, a + 1)
                    ge(act, out_s, a - 3)
                    act.activation(right[:, (u + 2) % 4, :, :], b_right[:, :, :], ACT.Copy).then_inc(right_s, 1)
                if live(f):
                    ge(act, turned, f - 1)
                    normalise(act, feat[:, (u + 3) % 2, :, :], x, rstd, shift, f).then_inc(normed, 1)

            pipeline(act, -3, step)

        @block.tensor
        def _(pe):
            def step(n, u):
                b, a = n + 1, n + 2
                if live(n):
                    pe.wait_ge(probs_s, n + 1)
                    ge(pe, probsT_s, n)
                    for v in range(PER):
                        last = pe.transpose(b_probsT[:, v, :], probs[:, u % 2, v, :], ident)
                    last.then_inc(probs_turned, 1)
                if live(b):
                    f = featT[:, (u + 1) % 4, :, :]
                    ge(pe, score_s, b)
                    if first:
                        pe.wait_ge(queries_s, b + 1)
                    else:
                        pe.wait_ge(featT_s, b + 1)
                    for v in range(PER):
                        pe.matmul(b_score[:, v, :], queries[:, (u + 1) % 2, v, :] if first else w["key_side"], f[:, v, :],
                                  start=True, stop=False)
                        last = pe.matmul(b_score[:, v, :], f[:, v, :], w["query_side"], start=False, stop=True)
                    last.then_inc(scored, 1)
                if live(a):
                    pe.wait_ge(normed, a + 1)
                    ge(pe, featT_s, a)
                    for v in range(PER):
                        last = pe.transpose(b_featT[:, v, :], feat[:, (u + 2) % 2, v, :], ident)
                    last.then_inc(turned, 1)
                if live(n):
                    pe.wait_ge(probsT_s, n + 1)
                    pe.wait_ge(right_s, n + 1)
                    ge(pe, out_read, n)
                    for v in range(PER):
                        if first:
                            pe.matmul(b_out[:, v, :], featT[:, u, v, :], w["own"], start=True, stop=False)
                        last = pe.matmul(b_out[:, v, :], probsT[:, v, :], right[:, u, v, :], start=not first, stop=True)
                    last.then_inc(out_s, 1)
                if live(a):
                    f = featT[:, (u + 2) % 4, :, :]
                    pe.wait_ge(featT_s, a + 1)
                    if first:
                        ge(pe, queries_s, a)
                        pe.matmul(b_queries[:, :, :], w["bilinear"], f, start=True, stop=True).then_inc(asked, 1)
                    ge(pe, right_s, a)
                    for v in range(PER):
                        last = pe.matmul(b_right[:, v, :], f[:, v, :], w["other"], start=True, stop=True)
                    last.then_inc(righted, 1)

            pipeline(pe, -2, step)

        @block.vector
        def _(dve):
            def step(n, u):
                b, a = n + 1, n + 2
                if live(b):
                    at = b * 4
                    dve.wait_ge(low_s, b + 1)
                    ge(dve, exped, b)
                    dve.tensor_tensor(score[:, :, :], b_score[:, :, :], low[:, :, :], ALU.max).then_inc(score_s, 1)
                    dve.wait_ge(score_s, b + 1)
                    dve.scalar_tensor_tensor(score[:, :, :], masked[:, bass.ds(b * PER, PER), :], fill, score[:, :, :],
                                             ALU.mult, ALU.add).then_inc(chain_b, 1)
                    dve.wait_ge(chain_b, at + 1)
                    dve.tensor_reduce(row[:, 0, :], score[:, :, :], AX_X, ALU.max).then_inc(chain_b, 1)
                    dve.wait_ge(chain_b, at + 2)
                    dve.tensor_tensor(score[:, :, :], score[:, :, :], row[:, 0, :].unsqueeze(2).to_broadcast([P, PER, NODES]),
                                      ALU.subtract).then_inc(shifted, 1)
                if live(n) and first:
                    dve.wait_ge(out_s, n + 1)
                    ge(dve, grown_s, n)
                    dve.tensor_scalar(under[:, :, :], b_out[:, :, :], 0.0, None, ALU.min).then_inc(under_s, 1)
                if live(b):
                    p = probs[:, (u + 1) % 2, :, :]
                    dve.wait_ge(exped, b + 1)
                    dve.tensor_reduce(row[:, 1, :], p, AX_X, ALU.add).then_inc(chain_b, 1)
                    dve.wait_ge(chain_b, at + 3)
                    dve.reciprocal(row[:, 2, :], row[:, 1, :]).then_inc(chain_b, 1)
                    dve.wait_ge(chain_b, at + 4)
                    dve.tensor_tensor(p, p, row[:, 2, :].unsqueeze(2).to_broadcast([P, PER, NODES]), ALU.mult).then_inc(probs_s, 1)
                if live(n):
                    mine = x[:, bass.ds(n * PER, PER), :]
                    if first:
                        dve.wait_ge(grown_s, n + 1)
                        dve.scalar_tensor_tensor(summed[:, :, :], b_out[:, :, :], 0.0, grown[:, :, :], ALU.max, ALU.add).then_inc(out_read, 1)
                        dve.wait_ge(out_read, n + 1)
                        dve.scalar_tensor_tensor(mine, summed[:, :, :], -1.0, mine, ALU.add, ALU.add).then_inc(updated, 1)
                    else:
                        dve.wait_ge(out_s, n + 1)
                        dve.tensor_tensor(mine, b_out[:, :, :], mine, ALU.add).then_inc(out_read, 1)
                if live(a):
                    if first:
                        dve.wait_ge(asked, a + 1)
                        ge(dve, scored, a - 1)
                        dve.tensor_scalar(queries[:, (u + 2) % 2, :, :], b_queries[:, :, :], w["key_side"], None, ALU.add).then_inc(queries_s, 1)
                    else:
                        dve.wait_ge(righted, a + 1)
                        ge(dve, out_s, a - 3)
                        dve.tensor_tensor(right[:, (u + 2) % 4, :, :], b_right[:, :, :],
                                          w["bias"].unsqueeze(1).to_broadcast([P, PER, FEAT]), ALU.add).then_inc(right_s, 1)
                if live(n):
                    dve.wait_ge(updated if first else out_read, n + 1)
                    for v in range(PER):
                        q = n * PER + v
                        dve.bn_stats(stats[:, bass.ds(q, 1), :].rearrange("p o s -> p (o s)"),
                                     x[:, bass.ds(q, 1), :].rearrange("p o f -> p (o f)"))
                    dve.wait_ge(fetched_s[u % 2], (n - u % 2) * (8 * PER_SEARCH) + 16 * PER_SEARCH)
                    dve.tensor_tensor(before[:, :, :], fetched[:, u % 2, :, :],
                                      wanted[:, bass.ds(n * PER_SEARCH, PER_SEARCH)].unsqueeze(2).to_broadcast([P, PER_SEARCH, FAN]),
                                      ALU.is_lt).then_inc(chain_s, 1)
                    dve.wait_ge(chain_s, n + 1)
                    dve.tensor_reduce(counts[:, bass.ds(n * PER_SEARCH, PER_SEARCH)], before[:, :, :], AX_X, ALU.add).then_inc(looked, 1)
                    dve.wait_ge(looked, n + 1)

            pipeline(dve, -2, step)

        @block.gpsimd
        def _(pool):
            def step(n, u):
                if not isinstance(n, int) or n >= 2:
                    pool.wait_ge(looked, n - 1)
                pool.tensor_copy(chosen[:, u % 2, :], row_ids[:, bass.ds(n * PER_SEARCH, PER_SEARCH)]).then_inc(chosen_s, 1)
                pool.wait_ge(chosen_s, n + 1)
                pool.sem_inc(begun, 1)
                for c in range(PER_SEARCH):
                    pool.indirect_dma_start(fetched[:, u % 2, c, :], None, table,
                                            bass.IndirectOffsetOnAxis(chosen[:, u % 2, c:c + 1], 0)).then_inc(fetched_s[u % 2], 16)

            pipeline(pool, 0, step)


def project(nc, sem, tag, x, rstd, shift, ident, weight, cols, into):
    with ExitStack() as ctx:
        feat = ctx.enter_context(nc.sbuf_tensor(f"feat_{tag}", [P, 2, PER, FEAT], F32))
        featT = ctx.enter_context(nc.sbuf_tensor(f"featT_{tag}", [P, 2, PER, NODES], F32))
        b_featT = ctx.enter_context(nc.psum_tensor(f"b_featT_{tag}", [P, 2, PER, P], F32))
        b_out = ctx.enter_context(nc.psum_tensor(f"b_out_{tag}", [P, 2, PER, P], F32))
        normed, turned, featT_s, projected, kept = (sem(f"{tag}_{n}") for n in ("normed", "turned", "featT", "projected", "kept"))
        block = ctx.enter_context(nc.Block())

        @block.scalar
        def _(act):
            def step(n, u):
                a, f = n + 1, n + 2
                if live(a):
                    act.wait_ge(turned, a + 1)
                    ge(act, projected, a - 1)
                    act.activation(featT[:, (u + 1) % 2, :, :], b_featT[:, (u + 1) % 2, :, :], ACT.Copy).then_inc(featT_s, 1)
                if live(f):
                    ge(act, turned, f - 1)
                    normalise(act, feat[:, u % 2, :, :], x, rstd, shift, f).then_inc(normed, 1)

            pipeline(act, -2, step)

        @block.tensor
        def _(pe):
            def step(n, u):
                a = n + 1
                if live(a):
                    pe.wait_ge(normed, a + 1)
                    ge(pe, featT_s, a - 1)
                    for v in range(PER):
                        last = pe.transpose(b_featT[:, (u + 1) % 2, v, :], feat[:, (u + 1) % 2, v, :], ident)
                    last.then_inc(turned, 1)
                if live(n):
                    pe.wait_ge(featT_s, n + 1)
                    ge(pe, kept, n - 1)
                    for v in range(PER):
                        last = pe.matmul(b_out[:, u % 2, v, 0:cols], featT[:, u % 2, v, :], weight, start=True, stop=True)
                    last.then_inc(projected, 1)

            pipeline(pe, -1, step)

        @block.vector
        def _(dve):
            def step(n, u):
                dve.wait_ge(projected, n + 1)
                dve.tensor_scalar(into[:, bass.ds(n * PER, PER), :], b_out[:, u % 2, :, 0:cols], 1.0, None, ALU.mult).then_inc(kept, 1)

            pipeline(dve, 0, step)


def experts0(nc, sem, a, x, stats, rstd, shift, ident, ones, upto, slots_dram, rows_dram):
    with ExitStack() as outer:
        def kp(name, shape, dt=F32):
            return outer.enter_context(nc.sbuf_tensor(name, shape, dt))

        send = kp("send", [P, GRAPHS], U32)
        fetch = kp("fetch", [P, GRAPHS], U32)
        weight = kp("gate_weight", [P, GRAPHS])

        with ExitStack() as ctx:
            def sb(name, shape, dt=F32):
                return ctx.enter_context(nc.sbuf_tensor(name, shape, dt))

            gate_w, gate_b, logits = sb("gate_w", [P, EXPERTS]), sb("gate_b", [P, EXPERTS]), sb("gate_logits", [P, GRAPHS, EXPERTS])
            loaded = sem("gate_loaded")
            with nc.Block() as block:
                @block.sync
                def _(sp):
                    sp.dma_start(gate_w[:, :], a["gate_w"]).then_inc(loaded, 16)
                    sp.dma_start(gate_b[:, :], across(a["gate_b"], EXPERTS)).then_inc(loaded, 16)
                    sp.wait_ge(loaded, 32)
            project(nc, sem, "gate", x, rstd, shift, ident, gate_w[:, :], EXPERTS, logits)

            grown, chosen, tot, scan, work = (sb(n, [P, GRAPHS, EXPERTS]) for n in ("gate_grown", "gate_chosen", "gate_tot", "gate_scan", "gate_work"))
            best, prob, pos, base, kept = (sb(n, [P, GRAPHS]) for n in ("gate_best", "gate_prob", "gate_pos", "gate_base", "gate_kept"))
            order_i, order = sb("order_i", [P, 2, EXPERTS], I32), sb("order", [P, 2, EXPERTS])
            incl = ctx.enter_context(nc.psum_tensor("gate_incl", [P, GRAPHS, EXPERTS], F32))
            total = ctx.enter_context(nc.psum_tensor("gate_total", [P, GRAPHS, EXPERTS], F32))
            made, exped, ranked, ordered = sem("route_step"), sem("route_exp"), sem("route_ranked"), sem("route_order")
            block = ctx.enter_context(nc.Block())

            def wide(ap):
                return ap.unsqueeze(2).to_broadcast([P, GRAPHS, EXPERTS])

            def each(ap):
                return ap.unsqueeze(1).to_broadcast([P, GRAPHS, EXPERTS])

            @block.gpsimd
            def _(pool):
                pool.iota(order_i[:, 0, :], [[-1, EXPERTS]], base=EXPERTS, channel_multiplier=0).then_inc(ordered, 1)
                pool.iota(order_i[:, 1, :], [[CAPACITY, EXPERTS]], base=0, channel_multiplier=0).then_inc(ordered, 1)

            @block.vector
            def _(dve):
                n = [0]

                def link(ins):
                    ins.then_inc(made, 1)
                    n[0] += 1
                    dve.wait_ge(made, n[0])

                dve.wait_ge(ordered, 2)
                link(dve.tensor_copy(order[:, :, :], order_i[:, :, :]))
                L = logits[:, :, :]
                link(dve.tensor_tensor(L, L, each(gate_b[:, :]), ALU.add))
                link(dve.tensor_reduce(best[:, :], L, AX_X, ALU.max))
                link(dve.tensor_tensor(work[:, :, :], L, wide(best[:, :]), ALU.subtract))
                link(dve.tensor_tensor(chosen[:, :, :], L, wide(best[:, :]), ALU.is_equal))
                link(dve.tensor_tensor(chosen[:, :, :], chosen[:, :, :], each(order[:, 0, :]), ALU.mult))
                link(dve.tensor_reduce(pos[:, :], chosen[:, :, :], AX_X, ALU.max))
                link(dve.tensor_tensor(chosen[:, :, :], chosen[:, :, :], wide(pos[:, :]), ALU.is_equal))
                dve.wait_ge(exped, 1)
                link(dve.tensor_reduce(pos[:, :], grown[:, :, :], AX_X, ALU.add))
                link(dve.reciprocal(prob[:, :], pos[:, :]))
                link(dve.tensor_tensor(work[:, :, :], chosen[:, :, :], each(order[:, 1, :]), ALU.mult))
                link(dve.tensor_reduce(base[:, :], work[:, :, :], AX_X, ALU.add))
                dve.wait_ge(ranked, 4)
                link(dve.tensor_copy(tot[:, :, :], total[:, :, :]))
                for e in range(EXPERTS):
                    link(dve.tensor_tensor_scan(scan[:, :, e], ones[:, :], tot[:, :, e], 0.0, ALU.mult, ALU.add))
                link(dve.tensor_tensor(scan[:, :, :], scan[:, :, :], tot[:, :, :], ALU.subtract))
                link(dve.tensor_tensor(scan[:, :, :], incl[:, :, :], scan[:, :, :], ALU.add))
                link(dve.tensor_tensor(scan[:, :, :], scan[:, :, :], chosen[:, :, :], ALU.mult))
                link(dve.tensor_reduce(pos[:, :], scan[:, :, :], AX_X, ALU.add))
                link(dve.tensor_scalar(pos[:, :], pos[:, :], -1.0, None, ALU.add))
                link(dve.tensor_scalar(kept[:, :], pos[:, :], float(CAPACITY), None, ALU.is_lt))
                link(dve.scalar_tensor_tensor(base[:, :], pos[:, :], float(CAPACITY - 1), base[:, :], ALU.min, ALU.add))
                link(dve.tensor_copy(fetch[:, :], base[:, :]))
                link(dve.tensor_tensor(weight[:, :], prob[:, :], kept[:, :], ALU.mult))
                link(dve.tensor_scalar(kept[:, :], kept[:, :], -float(1 << 20), float(1 << 20), ALU.mult, ALU.add))
                link(dve.tensor_tensor(base[:, :], base[:, :], kept[:, :], ALU.add))
                link(dve.tensor_copy(send[:, :], base[:, :]))

            @block.scalar
            def _(act):
                act.wait_ge(made, 4)
                act.activation(grown[:, :, :], work[:, :, :], ACT.Exp).then_inc(exped, 1)

            @block.tensor
            def _(pe):
                pe.wait_ge(made, 8)
                half = GRAPHS // 2
                for lhs, to in ((upto, incl), (ones, total)):
                    for h in (0, 1):
                        cols = slice(h * half, (h + 1) * half)
                        pe.matmul(to[:, cols, :], lhs[:, :], chosen[:, cols, :], start=True, stop=True).then_inc(ranked, 1)

        with ExitStack() as ctx:
            feat = ctx.enter_context(nc.sbuf_tensor("sent_feat", [P, 2, PER, FEAT], F32))
            ids = ctx.enter_context(nc.sbuf_tensor("sent_ids", [P, 2, PER], U32))
            normed, ids_s, paced = sem("sent_normed"), sem("sent_ids_s"), sem("sent_paced")
            sent = (sem("sent_even"), sem("sent_odd"))
            block = ctx.enter_context(nc.Block())

            @block.scalar
            def _(act):
                def step(n, u):
                    if not isinstance(n, int) or n >= 2:
                        act.wait_ge(sent[u % 2], (n - u % 2) * (8 * PER))
                    normalise(act, feat[:, u % 2, :, :], x, rstd, shift, n).then_inc(normed, 1)

                pipeline(act, 0, step)

            @block.gpsimd
            def _(pool):
                def step(n, u):
                    if not isinstance(n, int) or n >= 2:
                        pool.wait_ge(sent[u % 2], (n - u % 2) * (8 * PER))
                    pool.tensor_copy(ids[:, u % 2, :], send[:, bass.ds(n * PER, PER)]).then_inc(ids_s, 1)
                    pool.wait_ge(ids_s, n + 1)
                    pool.wait_ge(normed, n + 1)
                    pool.sem_inc(paced, 1)
                    for v in range(PER):
                        pool.indirect_dma_start(slots_dram, bass.IndirectOffsetOnAxis(ids[:, u % 2, v:v + 1], 0),
                                                feat[:, u % 2, v, :], None, bounds_check=EXPERTS * CAPACITY - 1,
                                                oob_is_err=False).then_inc(sent[u % 2], 16)

                pipeline(pool, 0, step)
                for s in sent:
                    pool.wait_ge(s, 8 * PER * GROUPS)

        with ExitStack() as ctx:
            def sb(name, shape, dt=F32):
                return ctx.enter_context(nc.sbuf_tensor(name, shape, dt))

            w1, w2 = sb("w1", [P, 2, HIDDEN]), sb("w2", [P, 2, HC, FEAT])
            b1, b2 = sb("b1", [P, 2, HC]), sb("b2", [P, 2, FEAT])
            rows, rowsT = sb("rows", [P, 2, PER, FEAT]), sb("rowsT", [P, 2, WIDE])
            hid, res = sb("hid", [P, 2, HC, WIDE]), sb("res", [P, 2, PER, FEAT])
            b_rowsT = ctx.enter_context(nc.psum_tensor("b_rowsT", [P, PER, P], F32))
            b_hid = ctx.enter_context(nc.psum_tensor("b_hid", [P, HC, WIDE], F32))
            b_res = ctx.enter_context(nc.psum_tensor("b_res", [P, 2, PER, P], F32))
            w_in = (sem("x0_w_even"), sem("x0_w_odd"))
            rows_in = (sem("x0_rows_even"), sem("x0_rows_odd"))
            turned, rowsT_s, hid_mm, hid_act, hid_dve, res_mm, res_s = (sem(f"x0_{n}") for n in (
                "turned", "rowsT", "hid_mm", "hid_act", "hid_dve", "res_mm", "res"))
            res_out = (sem("x0_out_even"), sem("x0_out_odd"))
            block = ctx.enter_context(nc.Block())
            STEPS = EXPERTS * SLOT_GROUPS
            TURN = 2 * SLOT_GROUPS
            slots_v = slots_dram.rearrange("(k p r) d -> k p r d", p=P, r=PER)
            rows_v = rows_dram.rearrange("(k p r) d -> k p r d", p=P, r=PER)

            def turns(engine, first, step):
                for n in range(first, TURN):
                    step(n, n % TURN)
                with engine.Fori(1, STEPS // TURN - 1) as turn:
                    for u in range(TURN):
                        step(turn * TURN + u, u)
                for n in range(STEPS - TURN, STEPS):
                    step(n, n % TURN)

            def there(n):
                return not isinstance(n, int) or 0 <= n < STEPS

            @block.sync
            def _(sp):
                def load(n, u):
                    ge(sp, turned, n - 1)
                    sp.dma_start(rows[:, u % 2, :, :], slots_v[bass.ds(n, 1)].rearrange("o p r d -> p (o r) d")).then_inc(rows_in[u % 2], 16)

                def store(n, u):
                    sp.wait_ge(res_s, n + 1)
                    sp.dma_start(rows_v[bass.ds(n, 1)].rearrange("o p r d -> p (o r) d"), res[:, u % 2, :, :]).then_inc(res_out[u % 2], 16)

                def step(n, u):
                    if there(n + 2):
                        load(n + 2, (u + 2) % TURN)
                    if there(n):
                        store(n, u)

                turns(sp, -2, step)
                for s in res_out:
                    sp.wait_ge(s, 8 * STEPS)

            @block.gpsimd
            def _(pool):
                def load(e, h):
                    for to, of in ((w1[:, h, :], a["w1"]), (w2[:, h, :, :], a["w2"]), (b1[:, h, :], a["b1T"])):
                        pool.dma_start(to, of[e]).then_inc(w_in[h], 16)
                    pool.dma_start(b2[:, h, :], bass.AP(a["b2"].tensor, e * FEAT, [[0, P], [1, FEAT]])).then_inc(w_in[h], 16)

                for e in range(EXPERTS):
                    if e >= 2:
                        pool.wait_ge(res_s, (e - 1) * SLOT_GROUPS)
                    load(e, e % 2)

            @block.tensor
            def _(pe):
                def step(n, u, pair):
                    m = n + 2
                    if there(m):
                        pe.wait_ge(rows_in[u % 2], (m - u % 2) * 8 + 16)
                        ge(pe, rowsT_s, m)
                        for r in range(PER):
                            last = pe.transpose(b_rowsT[:, r, :], rows[:, u % 2, r, :], ident)
                        last.then_inc(turned, 1)
                    m, mu = n + 1, (u + 1) % TURN
                    if there(m):
                        h = mu // SLOT_GROUPS
                        pe.wait_ge(w_in[h], (pair + (1 if u == TURN - 1 else 0)) * 64 + 64)
                        pe.wait_ge(rowsT_s, m + 1)
                        ge(pe, hid_act, m)
                        ge(pe, hid_dve, m)
                        for c in range(HC):
                            last = pe.matmul(b_hid[:, c, :], w1[:, h, c * P:(c + 1) * P], rowsT[:, (u + 1) % 2, :], start=True, stop=True)
                        last.then_inc(hid_mm, 1)
                    if there(n):
                        pe.wait_ge(hid_act, n + 1)
                        pe.wait_ge(hid_dve, n + 1)
                        ge(pe, res_s, n - 1)
                        h = u // SLOT_GROUPS
                        for r in range(PER):
                            for c in range(HC):
                                last = pe.matmul(b_res[:, u % 2, r, :], hid[:, u % 2, c, r * P:(r + 1) * P], w2[:, h, c, :],
                                                 start=(c == 0), stop=(c == HC - 1))
                        last.then_inc(res_mm, 1)

                for n in range(-2, TURN):
                    step(n, n % TURN, n // TURN)
                with pe.Fori(1, STEPS // TURN - 1) as turn:
                    for u in range(TURN):
                        step(turn * TURN + u, u, turn)
                for n in range(STEPS - TURN, STEPS):
                    step(n, n % TURN, n // TURN)

            @block.scalar
            def _(act):
                def step(n, u):
                    m = n + 1
                    if there(m):
                        act.wait_ge(turned, m + 1)
                        ge(act, hid_mm, m - 1)
                        act.activation(rowsT[:, (u + 1) % 2, :], b_rowsT[:, :, :].rearrange("p r i -> p (r i)"), ACT.Copy).then_inc(rowsT_s, 1)
                    if there(n):
                        act.wait_ge(hid_mm, n + 1)
                        ge(act, res_mm, n - 1)
                        h = u // SLOT_GROUPS
                        for c in (0, 1):
                            last = act.activation(hid[:, u % 2, c, :], b_hid[:, c, :], ACT.Relu, bias=b1[:, h, c:c + 1])
                        last.then_inc(hid_act, 1)

                turns(act, -1, step)

            @block.vector
            def _(dve):
                def step(n, u):
                    m, mu = n + 1, (u + 1) % TURN
                    if there(m):
                        dve.wait_ge(hid_mm, m + 1)
                        ge(dve, res_mm, m - 1)
                        h = mu // SLOT_GROUPS
                        for c in (2, 3):
                            last = dve.tensor_scalar(hid[:, (u + 1) % 2, c, :], b_hid[:, c, :], b1[:, h, c:c + 1], 0.0, ALU.add, ALU.max)
                        last.then_inc(hid_dve, 1)
                    if there(n):
                        h = u // SLOT_GROUPS
                        dve.wait_ge(res_mm, n + 1)
                        if not isinstance(n, int) or n >= 2:
                            dve.wait_ge(res_out[u % 2], (n - u % 2) * 8)
                        dve.tensor_tensor(res[:, u % 2, :, :], b_res[:, u % 2, :, :],
                                          b2[:, h, :].unsqueeze(1).to_broadcast([P, PER, FEAT]), ALU.add).then_inc(res_s, 1)

                turns(dve, -1, step)

        with ExitStack() as ctx:
            got = ctx.enter_context(nc.sbuf_tensor("got", [P, 2, PER, FEAT], F32))
            ids = ctx.enter_context(nc.sbuf_tensor("got_ids", [P, 2, PER], U32))
            ids_s, paced, added = sem("got_ids_s"), sem("got_paced"), sem("got_added")
            came = (sem("got_even"), sem("got_odd"))
            block = ctx.enter_context(nc.Block())

            @block.gpsimd
            def _(pool):
                def step(n, u):
                    if not isinstance(n, int) or n >= 2:
                        pool.wait_ge(added, n - 1)
                    pool.tensor_copy(ids[:, u % 2, :], fetch[:, bass.ds(n * PER, PER)]).then_inc(ids_s, 1)
                    pool.wait_ge(ids_s, n + 1)
                    pool.sem_inc(paced, 1)
                    for v in range(PER):
                        pool.indirect_dma_start(got[:, u % 2, v, :], None, rows_dram,
                                                bass.IndirectOffsetOnAxis(ids[:, u % 2, v:v + 1], 0)).then_inc(came[u % 2], 16)

                pipeline(pool, 0, step)

            @block.vector
            def _(dve):
                def step(n, u):
                    dve.wait_ge(came[u % 2], (n - u % 2) * (8 * PER) + 16 * PER)
                    for v in range(PER):
                        q = n * PER + v
                        mine = x[:, bass.ds(q, 1), :].rearrange("p o f -> p (o f)")
                        last = dve.scalar_tensor_tensor(mine, got[:, u % 2, v, :], weight[:, bass.ds(q, 1)], mine, ALU.mult, ALU.add)
                    last.then_inc(added, 1)
                    dve.wait_ge(added, n + 1)
                    for v in range(PER):
                        q = n * PER + v
                        dve.bn_stats(stats[:, bass.ds(q, 1), :].rearrange("p o s -> p (o s)"),
                                     x[:, bass.ds(q, 1), :].rearrange("p o f -> p (o f)"))

                pipeline(dve, 0, step)


def prepare_nodes(nc, sem, tab, table_dram, node, last_node, ident, ones, wanted, found, counted, first_edge, degree, clamped, loops):
    with ExitStack() as ctx:
        def sb(name, shape, dt=F32):
            return ctx.enter_context(nc.sbuf_tensor(name, shape, dt))

        beside, at_end, total_at_end = sb("beside", [P, P]), sb("at_end", [P, P]), sb("total_at_end", [P, P])
        ends, most, flag = sb("ends", [P, 2]), sb("most", [P, 1]), sb("most_row", [P, 4])
        ps = ctx.enter_context(nc.psum_tensor("ends_ps", [P, 512], F32))
        wrote, read, drawn, made, shifted, turned = (sem(f"nodes_{n}") for n in ("wrote", "read", "drawn", "made", "shifted", "turned"))
        block = ctx.enter_context(nc.Block())

        @block.sync
        def _(sp):
            sp.dma_start(table_dram.rearrange("(b i) c -> i b c", i=NODES), tab[:, :, :]).then_inc(wrote, 16)
            sp.wait_ge(wrote, 16)
            sp.dma_start(node[:, :, :], table_dram.rearrange("(b i) c -> b i c", i=NODES)).then_inc(read, 16)
            sp.dma_start(last_node[:, :], bass.AP(table_dram.tensor, (TOKENS - 1) * TAB, [[0, P], [1, TAB]])).then_inc(read, 16)
            sp.wait_ge(read, 32)

        @block.gpsimd
        def _(pool):
            pool.affine_select(out=total_at_end[:, :], in_=ones[:, :], compare_op=ALU.is_ge, fill=0.0, base=-(P - 1),
                               pattern=[[1, P]], channel_multiplier=0).then_inc(drawn, 1)
            pool.memset(beside[:, :], 0.0).then_inc(drawn, 1)
            pool.wait_ge(drawn, 2)
            pool.affine_select(out=beside[:, :], in_=beside[:, :], compare_op=ALU.not_equal, fill=1.0, base=-1,
                               pattern=[[-1, P]], channel_multiplier=1).then_inc(drawn, 1)
            pool.affine_select(out=at_end[:, :], in_=total_at_end[:, :], compare_op=ALU.is_ge, fill=0.0, base=0,
                               pattern=[[0, P]], channel_multiplier=-1).then_inc(drawn, 1)

        @block.tensor
        def _(pe):
            pe.wait_ge(drawn, 4)
            pe.matmul(ps[:, 0:1], beside[:, :], found[:, 0, 0:1], start=True, stop=False)
            pe.matmul(ps[:, 0:1], at_end[:, :], found[:, 0, NODES:NODES + 1], start=False, stop=True)
            pe.matmul(ps[:, 1:2], beside[:, :], found[:, 0, NODES:NODES + 1], start=True, stop=False)
            pe.matmul(ps[:, 1:2], total_at_end[:, :], counted, start=False, stop=True).then_inc(shifted, 1)
            pe.wait_ge(made, 6)
            pe.transpose(ps[:, 128:256], most[:, :].to_broadcast([P, P]), ident).then_inc(turned, 1)

        @block.vector
        def _(dve):
            n = [0]

            def link(ins):
                ins.then_inc(made, 1)
                n[0] += 1
                dve.wait_ge(made, n[0])

            dve.wait_ge(shifted, 1)
            link(dve.tensor_copy(ends[:, :], ps[:, 0:2]))
            for c, to in ((0, degree), (1, clamped)):
                s = found[:, 0, c * NODES:(c + 1) * NODES]
                link(dve.tensor_tensor(to[:, 0:NODES - 1], s[:, 1:NODES], s[:, 0:NODES - 1], ALU.subtract))
                link(dve.tensor_tensor(to[:, NODES - 1:NODES], ends[:, c:c + 1], s[:, NODES - 1:NODES], ALU.subtract))
            link(dve.tensor_reduce(most[:, :], degree[:, :], AX_X, ALU.max))
            link(dve.tensor_copy(first_edge[:, :], found[:, 0, 0:NODES]))
            dve.wait_ge(turned, 1)
            link(dve.tensor_reduce(flag[:, 0:1], ps[:, 128:256], AX_X, ALU.max))
            link(dve.tensor_scalar(flag[:, 0:1], flag[:, 0:1], 1.0, None, ALU.max))
            link(dve.tensor_scalar(flag[:, 1:2], found[:, 0, NODES:NODES + 1], float(WINDOW + EDGE_STEP), None, ALU.add))
            link(dve.tensor_copy(loops[:, 0:2], flag[:, 0:2]))
            link(dve.tensor_scalar(loops[:, 1:2], loops[:, 1:2], EDGE_STEP.bit_length() - 1, None, ALU.logical_shift_right))


def gather_edges(nc, sem, source_ids, table_dram, edges_dram, loops):
    with ExitStack() as ctx:
        ids = ctx.enter_context(nc.sbuf_tensor("edge_ids", [P, 2, EDGE_TILES], U32))
        rows = ctx.enter_context(nc.sbuf_tensor("edge_rows", [P, 2, EDGE_TILES, ROW], F32))
        ids_s, paced, freed = sem("edge_ids_s"), sem("edge_paced"), sem("edge_freed")
        came = (sem("edge_rows_even"), sem("edge_rows_odd"))
        gone = (sem("edge_out_even"), sem("edge_out_odd"))
        out_v = edges_dram.rearrange("(s c q) w -> s q c w", c=EDGE_TILES, q=P)
        block = ctx.enter_context(nc.Block())

        def turns(engine):
            return (engine.value_load(loops[0:1, 1:2], min_val=1, max_val=EDGES // EDGE_STEP + 1) + 1) // 2

        @block.gpsimd
        def _(pool):
            with pool.Fori(0, turns(pool)) as turn:
                for u in (0, 1):
                    n = turn * 2 + u
                    pool.wait_ge(freed, n + 1)
                    pool.tensor_copy(ids[:, u, :], source_ids[:, bass.ds(n * EDGE_TILES, EDGE_TILES)]).then_inc(ids_s, 1)
                    pool.wait_ge(ids_s, n + 1)
                    pool.sem_inc(paced, 1)
                    for c in range(EDGE_TILES):
                        pool.indirect_dma_start(rows[:, u, c, :], None, table_dram,
                                                bass.IndirectOffsetOnAxis(ids[:, u, c:c + 1], 0)).then_inc(came[u], 16)

        @block.sync
        def _(sp):
            sp.sem_inc(freed, 2)
            with sp.Fori(0, turns(sp)) as turn:
                for u in (0, 1):
                    n = turn * 2 + u
                    sp.wait_ge(came[u], turn * (16 * EDGE_TILES) + 16 * EDGE_TILES)
                    sp.dma_start(out_v[bass.ds(n, 1)].rearrange("o q c w -> q (o c) w"), rows[:, u, :, :]).then_inc(gone[u], 16)
                    sp.wait_ge(gone[u], turn * 16 + 16)
                    sp.sem_inc(freed, 1)


def attend_edges(nc, sem, a, edges_dram, node, last_node, first_edge, degree, clamped, loops, gates, ident):
    HALL = NODES * HEADS
    with ExitStack() as ctx:
        def sb(name, shape, dt=F32):
            return ctx.enter_context(nc.sbuf_tensor(name, shape, dt))

        top, total = sb("top", [P, NODES, HEADS]), sb("total", [P, NODES, HEADS])
        acc = sb("acc", [P, NODES, GAT])
        self_w, clamp_w = sb("self_w", [P, NODES, HEADS]), sb("clamp_w", [P, NODES, HEADS])
        wide = sb("wide", [P, NODES, GAT])
        left = sb("left", [P, NODES])
        order_i, order = sb("window_order_i", [P, WINDOW], I32), sb("window_order", [P, WINDOW])
        made, exped, drawn = sem("attend_step"), sem("attend_exp"), sem("attend_drawn")

        def heads(ap):
            return ap.unsqueeze(2).to_broadcast([P, NODES, HEADS])

        with nc.Block() as block:
            @block.gpsimd
            def _(pool):
                pool.iota(order_i[:, :], [[1, WINDOW]], base=0, channel_multiplier=0).then_inc(drawn, 1)

            @block.vector
            def _(dve):
                n = [0]

                def link(ins):
                    ins.then_inc(made, 1)
                    n[0] += 1
                    dve.wait_ge(made, n[0])

                S, C = self_w[:, :, :], clamp_w[:, :, :]
                to = node[:, :, ROW:TAB]
                link(dve.tensor_tensor(S, node[:, :, GAT:ROW], to, ALU.add))
                link(dve.scalar_tensor_tensor(S, S, SLOPE, S, ALU.mult, ALU.max))
                link(dve.tensor_tensor(C, to, last_node[:, GAT:ROW].unsqueeze(1).to_broadcast([P, NODES, HEADS]), ALU.add))
                link(dve.scalar_tensor_tensor(C, C, SLOPE, C, ALU.mult, ALU.max))
                link(dve.tensor_scalar(left[:, :], clamped[:, :], 0.0, -BIG, ALU.is_equal, ALU.mult))
                link(dve.tensor_tensor(C, C, heads(left[:, :]), ALU.add))
                link(dve.tensor_tensor(top[:, :, :], S, C, ALU.max))
                link(dve.tensor_tensor(S, S, top[:, :, :], ALU.subtract))
                link(dve.tensor_tensor(C, C, top[:, :, :], ALU.subtract))
                dve.wait_ge(exped, 2)
                link(dve.tensor_tensor(C, C, heads(clamped[:, :]), ALU.mult))
                link(dve.tensor_tensor(total[:, :, :], S, C, ALU.add))
                rows_h = node[:, :, 0:GAT].rearrange("p n (h e) -> p n h e", h=HEADS)
                acc_h = acc[:, :, :].rearrange("p n (h e) -> p n h e", h=HEADS)
                wide_h = wide[:, :, :].rearrange("p n (h e) -> p n h e", h=HEADS)
                link(dve.tensor_tensor(acc_h, rows_h, S.unsqueeze(3).to_broadcast([P, NODES, HEADS, TOP_EXPERTS]), ALU.mult))
                last_h = last_node[:, 0:GAT].rearrange("p (h e) -> p h e", h=HEADS)
                link(dve.tensor_tensor(wide_h, last_h.unsqueeze(1).to_broadcast([P, NODES, HEADS, TOP_EXPERTS]),
                                       C.unsqueeze(3).to_broadcast([P, NODES, HEADS, TOP_EXPERTS]), ALU.mult))
                link(dve.tensor_tensor(acc[:, :, :], acc[:, :, :], wide[:, :, :], ALU.add))
                link(dve.tensor_copy(left[:, :], degree[:, :]))
                dve.wait_ge(drawn, 1)
                link(dve.tensor_copy(order[:, :], order_i[:, :]))

            @block.scalar
            def _(act):
                act.wait_ge(made, 9)
                act.activation(self_w[:, :, :], self_w[:, :, :], ACT.Exp).then_inc(exped, 1)
                act.activation(clamp_w[:, :, :], clamp_w[:, :, :], ACT.Exp).then_inc(exped, 1)

        with ExitStack() as inner:
            def sb(name, shape, dt=F32):
                return inner.enter_context(nc.sbuf_tensor(name, shape, dt))

            win = sb("win", [P, 2, PER, WINDOW * ROW])
            ids = sb("win_ids", [P, 2, PER], U32)
            sc, low = sb("win_score", [P, 2, PER, WINDOW, HEADS]), sb("win_low", [P, PER * WINDOW * HEADS])
            hide = sb("win_hide", [P, PER, WINDOW])
            newtop, fade = sb("win_top", [P, 2, PER, HEADS]), sb("win_fade", [P, 2, PER, HEADS])
            msg, got = sb("win_msg", [P, PER, WINDOW, GAT]), sb("win_got", [P, PER, GAT])
            sums, adv = sb("win_sums", [P, PER, HEADS]), sb("win_adv", [P, PER])
            ids_s, paced, exp_s, scored, used, chain, advanced = (sem(f"win_{n}") for n in ("ids_s", "paced", "exp", "scored", "used", "chain", "advanced"))
            came = (sem("win_even"), sem("win_odd"))
            block = inner.enter_context(nc.Block())
            FULL = [P, PER, WINDOW, HEADS]

            def rounds(engine):
                return (engine.value_load(loops[0:1, 0:1], min_val=1, max_val=EDGES) + (WINDOW - 1)) // WINDOW

            @block.gpsimd
            def _(pool):
                with pool.Fori(0, rounds(pool)) as r:
                    with pool.Fori(0, GROUPS // 2) as turn:
                        for u in (0, 1):
                            g = turn * 2 + u
                            n = r * GROUPS + g
                            pool.wait_ge(used, n + 1)
                            pool.tensor_copy(ids[:, u, :], first_edge[:, bass.ds(g * PER, PER)]).then_inc(ids_s, 1)
                            pool.wait_ge(ids_s, n + 1)
                            pool.sem_inc(paced, 1)
                            for v in range(PER):
                                pool.indirect_dma_start(win[:, u, v, :], None, edges_dram,
                                                        bass.IndirectOffsetOnAxis(ids[:, u, v:v + 1], 0)).then_inc(came[u], 16)

            @block.scalar
            def _(act):
                with act.Fori(0, rounds(act)) as r:
                    with act.Fori(0, GROUPS // 2) as turn:
                        for u in (0, 1):
                            n = r * GROUPS + turn * 2 + u
                            act.wait_ge(scored, n + 1)
                            act.activation(fade[:, u, :, :], fade[:, u, :, :], ACT.Exp).then_inc(exp_s, 1)
                            act.activation(sc[:, u, :, :, :], sc[:, u, :, :, :], ACT.Exp).then_inc(exp_s, 1)

            @block.vector
            def _(dve):
                def look(g, n, u, r):
                    at = n * 12
                    mine = bass.ds(g * PER, PER)
                    w = win[:, u, :, :].rearrange("p t (k c) -> p t k c", c=ROW)
                    s = sc[:, u, :, :, :]
                    flat = s.rearrange("p t k h -> p (t k h)")
                    dve.wait_ge(came[u], (n - u) * (8 * PER) + 16 * PER)
                    dve.tensor_tensor(s, w[:, :, :, GAT:ROW], node[:, mine, ROW:TAB].unsqueeze(2).to_broadcast(FULL), ALU.add).then_inc(chain, 1)
                    dve.tensor_tensor(hide[:, :, :], order[:, :].unsqueeze(1).to_broadcast([P, PER, WINDOW]),
                                      left[:, mine].unsqueeze(2).to_broadcast([P, PER, WINDOW]), ALU.is_ge).then_inc(chain, 1)
                    dve.wait_ge(chain, at + 2)
                    dve.tensor_scalar(hide[:, :, :], hide[:, :, :], -BIG, None, ALU.mult).then_inc(chain, 1)
                    dve.scalar_tensor_tensor(flat, flat, SLOPE, flat, ALU.mult, ALU.max).then_inc(chain, 1)
                    dve.wait_ge(chain, at + 4)
                    dve.tensor_tensor(s, s, hide[:, :, :].unsqueeze(3).to_broadcast(FULL), ALU.add).then_inc(chain, 1)
                    dve.wait_ge(chain, at + 5)
                    dve.tensor_reduce(newtop[:, u, :, :], s.rearrange("p t k h -> p t h k"), AX_X, ALU.max).then_inc(chain, 1)
                    dve.wait_ge(chain, at + 6)
                    dve.tensor_tensor(newtop[:, u, :, :], newtop[:, u, :, :], top[:, mine, :], ALU.max).then_inc(chain, 1)
                    dve.wait_ge(chain, at + 7)
                    dve.tensor_tensor(fade[:, u, :, :], top[:, mine, :], newtop[:, u, :, :], ALU.subtract).then_inc(chain, 1)
                    dve.tensor_tensor(s, s, newtop[:, u, :, :].unsqueeze(2).to_broadcast(FULL), ALU.subtract).then_inc(chain, 1)
                    dve.wait_ge(chain, at + 9)
                    dve.tensor_scalar(top[:, mine, :], newtop[:, u, :, :], 1.0, None, ALU.mult).then_inc(scored, 1)
                    dve.tensor_scalar(left[:, mine], left[:, mine], -float(WINDOW), None, ALU.add).then_inc(chain, 1)
                    dve.wait_ge(chain, at + 10)
                    dve.tensor_scalar(adv[:, :], left[:, mine], 0.0, float(WINDOW), ALU.is_gt, ALU.mult).then_inc(chain, 1)
                    dve.wait_ge(chain, at + 11)
                    dve.tensor_tensor(first_edge[:, mine], first_edge[:, mine], adv[:, :], ALU.add).then_inc(chain, 1)

                def gather(g, n, u):
                    at = n * 6
                    mine = bass.ds(g * PER, PER)
                    w = win[:, u, :, :].rearrange("p t (k c) -> p (t k) c", c=ROW)
                    s = sc[:, u, :, :, :]
                    dve.wait_ge(exp_s, n * 2 + 2)
                    dve.tensor_reduce(sums[:, :, :], s.rearrange("p t k h -> p t h k"), AX_X, ALU.add).then_inc(advanced, 1)
                    dve.tensor_tensor(total[:, mine, :], total[:, mine, :], fade[:, u, :, :], ALU.mult).then_inc(advanced, 1)
                    dve.tensor_tensor(msg[:, :, :, :].rearrange("p t k (h e) -> p (t k) h e", h=HEADS),
                                      w[:, :, 0:GAT].rearrange("p k (h e) -> p k h e", h=HEADS),
                                      s.rearrange("p t k h -> p (t k) h").unsqueeze(3).to_broadcast([P, PER * WINDOW, HEADS, TOP_EXPERTS]),
                                      ALU.mult).then_inc(used, 1)
                    a4 = acc[:, mine, :].rearrange("p t (h e) -> p t h e", h=HEADS)
                    dve.tensor_tensor(a4, a4, fade[:, u, :, :].unsqueeze(3).to_broadcast([P, PER, HEADS, TOP_EXPERTS]), ALU.mult).then_inc(advanced, 1)
                    dve.wait_ge(advanced, at + 3)
                    dve.tensor_tensor(total[:, mine, :], total[:, mine, :], sums[:, :, :], ALU.add).then_inc(advanced, 1)
                    dve.wait_ge(used, n + 3)
                    dve.tensor_reduce(got[:, :, :], msg[:, :, :, :].rearrange("p t k c -> p t c k"), AX_X, ALU.add).then_inc(advanced, 1)
                    dve.wait_ge(advanced, at + 5)
                    dve.tensor_tensor(acc[:, mine, :], acc[:, mine, :], got[:, :, :], ALU.add).then_inc(advanced, 1)

                dve.tensor_copy(adv[:, 0:1], left[:, 0:1]).then_inc(used, 2)
                with dve.Fori(0, rounds(dve)) as r:
                    with dve.Fori(0, GROUPS // 2) as turn:
                        g = turn * 2
                        n = r * GROUPS + g
                        look(g, n, 0, r)
                        look(g + 1, n + 1, 1, r)
                        gather(g, n, 0)
                        gather(g + 1, n + 1, 1)

        with ExitStack() as inner:
            def sb(name, shape, dt=F32):
                return inner.enter_context(nc.sbuf_tensor(name, shape, dt))

            gat_b, gamma, beta = sb("gat_b", [P, GAT]), sb("gat_gamma", [P, GAT]), sb("gat_beta", [P, GAT])
            mean, var, root = sb("gat_mean", [P, NODES]), sb("gat_var", [P, NODES]), sb("gat_root", [P, NODES])
            s4, one, two, val = (sb(n, [P, NODES, TOP_EXPERTS]) for n in ("s4", "one", "two", "val"))
            first, second, w1, w2 = (sb(n, [P, NODES]) for n in ("first_best", "second_best", "first_w", "second_w"))
            pref_i, pref = sb("pref_i", [P, TOP_EXPERTS], I32), sb("pref", [P, TOP_EXPERTS])
            ps = inner.enter_context(nc.psum_tensor("gates_ps", [P, TOP_EXPERTS, P], F32))
            loaded, made, act_s, drawn, turned = (sem(f"top_{n}") for n in ("loaded", "made", "act", "drawn", "turned"))
            block = inner.enter_context(nc.Block())

            @block.sync
            def _(sp):
                for to, of in ((gat_b, "gat_b"), (gamma, "gamma"), (beta, "beta")):
                    sp.dma_start(to[:, :], across(a[of], GAT)).then_inc(loaded, 16)

            @block.gpsimd
            def _(pool):
                pool.iota(pref_i[:, :], [[-1, TOP_EXPERTS]], base=TOP_EXPERTS, channel_multiplier=0).then_inc(drawn, 1)

            marks = {}

            @block.vector
            def _(dve):
                n = [0]

                def link(ins, mark=None):
                    ins.then_inc(made, 1)
                    n[0] += 1
                    dve.wait_ge(made, n[0])
                    if mark:
                        marks[mark] = n[0]

                def nodes16(ap):
                    return ap.unsqueeze(2).to_broadcast([P, NODES, GAT])

                def each16(ap):
                    return ap.unsqueeze(1).to_broadcast([P, NODES, GAT])

                def nodes4(ap):
                    return ap.unsqueeze(2).to_broadcast([P, NODES, TOP_EXPERTS])

                A, B = acc[:, :, :], wide[:, :, :]
                link(dve.tensor_scalar(total[:, :, :], total[:, :, :], 1e-16, None, ALU.add))
                link(dve.reciprocal(total[:, :, :], total[:, :, :]))
                A4 = A.rearrange("p n (h e) -> p n h e", h=HEADS)
                link(dve.tensor_tensor(A4, A4, total[:, :, :].unsqueeze(3).to_broadcast([P, NODES, HEADS, TOP_EXPERTS]), ALU.mult))
                dve.wait_ge(loaded, 48)
                link(dve.tensor_tensor(A, A, each16(gat_b[:, :]), ALU.add))
                link(dve.tensor_reduce(mean[:, :], A, AX_X, ALU.add))
                link(dve.tensor_scalar(mean[:, :], mean[:, :], 1.0 / GAT, None, ALU.mult))
                link(dve.tensor_tensor(A, A, nodes16(mean[:, :]), ALU.subtract))
                link(dve.tensor_tensor(B, A, A, ALU.mult))
                link(dve.tensor_reduce(var[:, :], B, AX_X, ALU.add))
                link(dve.tensor_scalar(var[:, :], var[:, :], 1.0 / GAT, EPS, ALU.mult, ALU.add), "var")
                dve.wait_ge(act_s, 1)
                link(dve.reciprocal(var[:, :], root[:, :]))
                link(dve.tensor_tensor(A, A, nodes16(var[:, :]), ALU.mult))
                link(dve.tensor_tensor(A, A, each16(gamma[:, :]), ALU.mult))
                link(dve.tensor_tensor(A, A, each16(beta[:, :]), ALU.add))
                link(dve.tensor_reduce(s4[:, :, :], A.rearrange("p n (h e) -> p n e h", h=HEADS), AX_X, ALU.add))
                link(dve.tensor_scalar(s4[:, :, :], s4[:, :, :], 1.0 / HEADS, None, ALU.mult))
                dve.wait_ge(drawn, 1)
                link(dve.tensor_copy(pref[:, :], pref_i[:, :]))
                pref4 = pref[:, :].unsqueeze(1).to_broadcast([P, NODES, TOP_EXPERTS])
                for best, hot in ((first, one), (second, two)):
                    link(dve.tensor_reduce(best[:, :], s4[:, :, :], AX_X, ALU.max))
                    link(dve.tensor_tensor(val[:, :, :], s4[:, :, :], nodes4(best[:, :]), ALU.is_equal))
                    link(dve.tensor_tensor(val[:, :, :], val[:, :, :], pref4, ALU.mult))
                    link(dve.tensor_reduce(w1[:, :], val[:, :, :], AX_X, ALU.max))
                    link(dve.tensor_tensor(hot[:, :, :], val[:, :, :], nodes4(w1[:, :]), ALU.is_equal))
                    if hot is one:
                        link(dve.scalar_tensor_tensor(s4[:, :, :], one[:, :, :], -BIG, s4[:, :, :], ALU.mult, ALU.add))
                link(dve.tensor_tensor(w2[:, :], second[:, :], first[:, :], ALU.subtract), "gap")
                dve.wait_ge(act_s, 2)
                link(dve.tensor_scalar(w1[:, :], w2[:, :], 1.0, None, ALU.add))
                link(dve.reciprocal(w1[:, :], w1[:, :]))
                link(dve.tensor_tensor(w2[:, :], w2[:, :], w1[:, :], ALU.mult))
                link(dve.tensor_tensor(one[:, :, :], one[:, :, :], nodes4(w1[:, :]), ALU.mult))
                link(dve.tensor_tensor(two[:, :, :], two[:, :, :], nodes4(w2[:, :]), ALU.mult))
                link(dve.tensor_tensor(one[:, :, :], one[:, :, :], two[:, :, :], ALU.add), "gates")
                dve.wait_ge(turned, 1)
                link(dve.tensor_copy(gates[:, :, :].rearrange("i b e -> i e b"), ps[:, :, :]))

            @block.scalar
            def _(act):
                act.wait_ge(made, marks["var"])
                act.activation(root[:, :], var[:, :], ACT.Sqrt).then_inc(act_s, 1)
                act.wait_ge(made, marks["gap"])
                act.activation(w2[:, :], w2[:, :], ACT.Exp).then_inc(act_s, 1)

            @block.tensor
            def _(pe):
                pe.wait_ge(made, marks["gates"])
                for e in range(TOP_EXPERTS):
                    last = pe.transpose(ps[:, e, :], one[:, :, e], ident)
                last.then_inc(turned, 1)


def experts1(nc, sem, a, x, rstd, shift, gates, ident, out):
    with ExitStack() as ctx:
        def sb(name, shape, dt=F32):
            return ctx.enter_context(nc.sbuf_tensor(name, shape, dt))

        w1, b1 = sb("x1_w1", [P, TOP_EXPERTS, HIDDEN1]), sb("x1_b1", [P, TOP_EXPERTS * HC1])
        w2, b2 = sb("x1_w2", [P, TOP_EXPERTS * HC1, FEAT]), sb("x1_b2", [TOP_EXPERTS, FEAT])
        feat, featT = sb("x1_feat", [P, 2, PER, FEAT]), sb("x1_featT", [P, 2, WIDE])
        gates_now = sb("x1_gates_now", [P, 2, PER, TOP_EXPERTS])
        gatesT = sb("x1_gatesT", [TOP_EXPERTS, 2, WIDE])
        hid = sb("x1_hid", [P, 2, HC1, WIDE])
        b_featT = ctx.enter_context(nc.psum_tensor("x1_b_featT", [P, PER, P], F32))
        b_gates = ctx.enter_context(nc.psum_tensor("x1_b_gates", [P, PER, P], F32))
        b_hid = ctx.enter_context(nc.psum_tensor("x1_b_hid", [P, 2, HC1, WIDE], F32))
        b_res = ctx.enter_context(nc.psum_tensor("x1_b_res", [P, 2, PER, P], F32))
        loaded, normed, turned, featT_s, gatesT_s, hid_mm, hid_s, res_mm, added = (sem(f"x1_{n}") for n in (
            "loaded", "normed", "turned", "featT", "gatesT", "hid_mm", "hid", "res_mm", "added"))
        gone, gates_in = sem("x1_out"), sem("x1_gates_in")
        block = ctx.enter_context(nc.Block())
        E = TOP_EXPERTS
        RES = E + 1

        @block.sync
        def _(sp):
            for to, of in ((w1[:, :, :], "w1b"), (b1[:, :], "b1b"), (w2[:, :, :], "w2b"), (b2[:, :], "b2b")):
                sp.dma_start(to, a[of]).then_inc(loaded, 16)

            def step(n, u):
                sp.wait_ge(added, n * RES + RES)
                sp.dma_start(out[:, bass.ds(n * PER, PER), :], x[:, bass.ds(n * PER, PER), :]).then_inc(gone, 16)

            pipeline(sp, 0, step)
            sp.wait_ge(gone, 16 * GROUPS)

        @block.gpsimd
        def _(pool):
            def step(n, u):
                ge(pool, turned, n - 1)
                pool.tensor_copy(gates_now[:, u % 2, :, :], gates[:, bass.ds(n * PER, PER), :]).then_inc(gates_in, 1)

            pipeline(pool, 0, step)

        @block.scalar
        def _(act):
            def step(n, u):
                if live(n + 1):
                    m = n + 1
                    act.wait_ge(turned, m + 1)
                    ge(act, hid_mm, (m - 1) * E)
                    act.activation(featT[:, (u + 1) % 2, :], b_featT[:, :, :].rearrange("p v i -> p (v i)"), ACT.Copy).then_inc(featT_s, 1)
                    ge(act, res_mm, (m - 2) * RES + 1)
                    act.activation(gatesT[:, (u + 1) % 2, :], b_gates[0:E, :, :].rearrange("p v i -> p (v i)"), ACT.Copy).then_inc(gatesT_s, 1)
                if live(n):
                    for e in range(E):
                        act.wait_ge(hid_mm, n * E + e + 1)
                        if e >= 2:
                            act.wait_ge(res_mm, n * RES + e)
                        else:
                            ge(act, res_mm, (n - 1) * RES + e + E)
                        for c in range(HC1):
                            last = act.activation(hid[:, e % 2, c, :], b_hid[:, e % 2, c, :], ACT.Gelu, bias=b1[:, e * HC1 + c:e * HC1 + c + 1])
                        last.then_inc(hid_s, 1)
                if live(n + 2):
                    ge(act, turned, n + 1)
                    normalise(act, feat[:, u % 2, :, :], x, rstd, shift, n + 2).then_inc(normed, 1)

            act.wait_ge(loaded, 64)
            pipeline(act, -2, step)

        @block.tensor
        def _(pe):
            def hidden(n, u, e):
                pe.wait_ge(featT_s, n + 1)
                ge(pe, hid_s, n * E + e - 1)
                for c in range(HC1):
                    last = pe.matmul(b_hid[:, e % 2, c, :], w1[:, e, c * P:(c + 1) * P], featT[:, u % 2, :], start=True, stop=True)
                last.then_inc(hid_mm, 1)

            def result(n, u, e):
                k = e + 1
                ge(pe, added, n * RES + k - 1)
                to = b_res[:, (u * RES + k) % 2, :, :]
                if e < 0:
                    pe.wait_ge(gatesT_s, n + 1)
                else:
                    pe.wait_ge(hid_s, n * E + e + 1)
                for v in range(PER):
                    cols = slice(v * P, (v + 1) * P)
                    if e < 0:
                        last = pe.matmul(to[:, v, :], gatesT[:, u % 2, cols], b2[:, :], start=True, stop=True)
                    else:
                        for c in range(HC1):
                            last = pe.matmul(to[:, v, :], hid[:, e % 2, c, cols], w2[:, e * HC1 + c, :], start=(c == 0), stop=(c == HC1 - 1))
                last.then_inc(res_mm, 1)

            def step(n, u):
                if live(n + 1):
                    m = n + 1
                    pe.wait_ge(normed, m + 1)
                    pe.wait_ge(gates_in, m + 1)
                    ge(pe, featT_s, m)
                    ge(pe, gatesT_s, m)
                    for v in range(PER):
                        pe.transpose(b_featT[:, v, :], feat[:, (u + 1) % 2, v, :], ident)
                    for v in range(PER):
                        last = pe.transpose(b_gates[0:E, v, :], gates_now[:, (u + 1) % 2, v, :], ident)
                    last.then_inc(turned, 1)
                if live(n):
                    hidden(n, u, 0)
                    result(n, u, -1)
                    for e in range(1, E):
                        hidden(n, u, e)
                        result(n, u, e - 1)
                    result(n, u, E - 1)

            pe.wait_ge(loaded, 64)
            pipeline(pe, -1, step)

        @block.vector
        def _(dve):
            def step(n, u):
                for k in range(RES):
                    r = b_res[:, (u * RES + k) % 2, :, :]
                    dve.wait_ge(res_mm, n * RES + k + 1)
                    if k == 0:
                        mine = x[:, bass.ds(n * PER, PER), :]
                        dve.tensor_tensor(mine, r, mine, ALU.add).then_inc(added, 1)
                        continue
                    dve.wait_ge(added, n * RES + k)
                    for v in range(PER):
                        q = n * PER + v
                        mine = x[:, bass.ds(q, 1), :].rearrange("p o f -> p (o f)")
                        last = dve.scalar_tensor_tensor(mine, r[:, v, :], gates[:, bass.ds(q, 1), k - 1:k].rearrange("p o e -> p (o e)"), mine, ALU.mult, ALU.add)
                    last.then_inc(added, 1)

            pipeline(dve, 0, step)


def build(nc, a, out):
    keys_dram = nc.dram_tensor("keys", (EDGES // FAN, FAN), F32).ap()
    slots_dram = nc.dram_tensor("slots", (EXPERTS * CAPACITY, FEAT), F32).ap()
    rows_dram = nc.dram_tensor("slot_results", (EXPERTS * CAPACITY, FEAT), F32).ap()
    table_dram = nc.dram_tensor("node_table", (TOKENS, TAB), F32).ap()
    edges_dram = nc.dram_tensor("edge_table", (EDGES + 2 * EDGE_STEP, ROW), F32).ap()
    coarse_dram = nc.dram_tensor("coarse", (P * COLS // FAN // FAN, FAN), F32).ap()
    with ExitStack() as top:
        in_use = []

        def sem(name):
            in_use.append(nc.alloc_semaphore(name))
            return in_use[-1]

        def renew_semaphores():
            nc.all_engine_barrier()
            nc.clear_and_free_semaphores(in_use)
            in_use.clear()
            nc.all_engine_barrier()

        def keep(name, shape, dt=F32):
            return top.enter_context(nc.sbuf_tensor(name, shape, dt))

        x = keep("x", [P, GRAPHS, FEAT])
        stats = keep("stats", [P, GRAPHS, 6])
        rstd = keep("rstd", [P, GRAPHS])
        shift = keep("shift", [P, GRAPHS])
        scratch = keep("scratch", [P, 3, P])
        ident = keep("ident", [P, P])
        ones = keep("ones", [P, P])
        upto = keep("upto", [P, P])
        row_id = keep("row_id", [P, 1], I32)
        source_ids = keep("source_ids", [P, COLS + 2 * EDGE_TILES], U32)
        wanted = keep("wanted", [P, SEARCHES])
        starts = keep("starts", [P, P])
        counted = keep("counted", [P, 1])
        row_ids = keep("row_ids", [P, SEARCHES], U32)
        counts = keep("counts", [P, SEARCHES])
        found = keep("found", [P, 2, SEARCHES])
        W = {n: keep(n, [P, k]) for n, k in (("bilinear", P), ("key_col", 1), ("query_row0", P), ("own", P), ("other0", P),
                                             ("query_row1", P), ("key_row1", P), ("other1", P), ("bias1", P))}

        with ExitStack() as ctx:
            def sb(name, shape, dt=F32):
                return ctx.enter_context(nc.sbuf_tensor(name, shape, dt))

            w0T, a12, cols0, w1, cols1 = sb("w0T", [P, P]), sb("a12", [P, P]), sb("cols0", [P, 2]), sb("w1g", [P, P]), sb("cols1", [P, 2])
            m1 = sb("m1", [P, P])
            vec = sb("vec", [P, 4])
            ps = ctx.enter_context(nc.psum_tensor("setup_ps", [P, 2, 512], F32))
            loaded, drawn, prod, made = sem("loaded"), sem("drawn"), sem("setup_product"), sem("setup_step")
            block = ctx.enter_context(nc.Block())

            @block.sync
            def _(sp):
                for to, of in ((w0T, a["gnn0_wT"]), (a12, a["gnn0_a12"]), (cols0, a["gnn0_a"]), (w1, a["gnn1_w"]), (cols1, a["gnn1_aT"]),
                               (W["own"], a["gnn0_w1"]), (W["other0"], a["gnn0_w2"]), (W["other1"], a["gnn1_wT"]), (W["bias1"], across(a["gnn1_bias"], P))):
                    sp.dma_start(to[:, :], of).then_inc(loaded, 16)
                sp.dma_start(x[:, :, :], a["x"]).then_inc(loaded, 16)

            @block.gpsimd
            def _(pool):
                pool.memset(ident[:, :], 0.0).then_inc(drawn, 1)
                pool.memset(ones[:, :], 1.0).then_inc(drawn, 1)
                pool.memset(source_ids[:, COLS:], 0).then_inc(drawn, 1)
                pool.iota(row_id[:, :], [[0, 1]], base=0, channel_multiplier=1).then_inc(drawn, 1)
                for c, base in enumerate((KEY_INSIDE, KEY_CLAMPED)):
                    pool.iota(wanted[:, c * NODES:(c + 1) * NODES].bitcast(I32), [[1 << LOG_NODES, NODES]], base=base,
                              channel_multiplier=NODES << LOG_NODES).then_inc(drawn, 1)
                pool.wait_ge(drawn, 6)
                pool.affine_select(out=ident[:, :], in_=ident[:, :], compare_op=ALU.not_equal, fill=1.0, base=0,
                                   pattern=[[-1, P]], channel_multiplier=1).then_inc(drawn, 1)
                pool.affine_select(out=upto[:, :], in_=ones[:, :], compare_op=ALU.is_ge, fill=0.0, base=0,
                                   pattern=[[1, P]], channel_multiplier=-1).then_inc(drawn, 1)
                pool.wait_ge(drawn, 8)

            @block.tensor
            def _(pe):
                pe.wait_ge(loaded, 160)
                pe.matmul(ps[:, 0, 0:P], a12[:, :], w0T[:, :], start=True, stop=True).then_inc(prod, 1)
                pe.matmul(ps[:, 0, 128:130], w0T[:, :], cols0[:, :], start=True, stop=True).then_inc(prod, 1)
                pe.matmul(ps[:, 0, 130:132], w1[:, :], cols1[:, :], start=True, stop=True).then_inc(prod, 1)
                pe.wait_ge(made, 1)
                pe.matmul(ps[:, 1, 0:P], m1[:, :], w0T[:, :], start=True, stop=True).then_inc(prod, 1)

            @block.vector
            def _(dve):
                dve.wait_ge(prod, 3)
                dve.tensor_copy(m1[:, :], ps[:, 0, 0:P]).then_inc(made, 1)
                dve.tensor_copy(vec[:, :], ps[:, 0, 128:132]).then_inc(made, 1)
                dve.wait_ge(made, 2)
                dve.tensor_copy(W["key_col"][:, :], vec[:, 0:1])
                dve.tensor_copy(W["query_row0"][:, :], vec[:, 1:2].to_broadcast([P, P]))
                dve.tensor_copy(W["query_row1"][:, :], vec[:, 2:3].to_broadcast([P, P]))
                dve.tensor_copy(W["key_row1"][:, :], vec[:, 3:4].to_broadcast([P, P]))
                dve.wait_ge(prod, 4)
                dve.tensor_copy(W["bilinear"][:, :], ps[:, 1, 0:P])
                with dve.Fori(0, GROUPS) as g:
                    for v in range(PER):
                        q = g * PER + v
                        dve.bn_stats(stats[:, bass.ds(q, 1), :].rearrange("p o s -> p (o s)"),
                                     x[:, bass.ds(q, 1), :].rearrange("p o f -> p (o f)"))

        sort_edges(nc, sem, a["edges"], keys_dram, coarse_dram, starts, counted[:, :], source_ids, ident[:, :], row_id[:, :],
                   (slots_dram, edges_dram))

        def descend(level, base_in, base_out):
            made = sem(f"descend_{level}")
            with ExitStack() as ctx:
                lower = ctx.enter_context(nc.sbuf_tensor(f"lower_{level}", [P, SEARCHES], F32))
                tmp = ctx.enter_context(nc.sbuf_tensor(f"firsts_before_{level}", [P, 64, P], BF16))
                block = ctx.enter_context(nc.Block())

                @block.vector
                def _(dve):
                    n = [0]

                    def link(ins):
                        ins.then_inc(made, 1)
                        n[0] += 1
                        dve.wait_ge(made, n[0])

                    if level == 1:
                        for c in range(0, SEARCHES, 64):
                            link(dve.tensor_tensor(tmp[:, :, :], starts[:, :].unsqueeze(1).to_broadcast([P, 64, P]),
                                                   wanted[:, c:c + 64].unsqueeze(2).to_broadcast([P, 64, P]), ALU.is_lt))
                            link(dve.tensor_reduce(counts[:, c:c + 64], tmp[:, :, :], AX_X, ALU.add))
                    if level < 3:
                        link(dve.tensor_scalar(lower[:, :], counts[:, :], -1.0, 0.0, ALU.add, ALU.max))
                    else:
                        link(dve.tensor_copy(lower[:, :], counts[:, :]))
                    if level > 1:
                        link(dve.scalar_tensor_tensor(base_out, base_in, float(FAN), lower[:, :], ALU.mult, ALU.add))
                    else:
                        link(dve.tensor_copy(base_out, lower[:, :]))
                    if level < 3:
                        link(dve.tensor_copy(row_ids[:, :], base_out))

        descend(1, None, found[:, 0, :])
        masked_ctx = top.enter_context(ExitStack())
        masked = masked_ctx.enter_context(nc.sbuf_tensor("masked", [P, GRAPHS, NODES], BF16))
        with nc.sbuf_tensor("adjacent", [P, 4, NODES * GRAPHS // 16], I32) as adjacent, nc.Block() as block:
            adj_in, adj_used = [sem(f"adj_in{c}") for c in range(4)], sem("adj_used")

            @block.sync
            def _(sp):
                for c in range(16):
                    ge(sp, adj_used, c - 3)
                    sp.dma_start(adjacent[:, c % 4, :], a["adj"][:, c * 1024:(c + 1) * 1024]).then_inc(adj_in[c % 4], 16)

            @block.vector
            def _(dve):
                flat = masked[:, :, :].rearrange("p b j -> p (b j)")
                for c in range(16):
                    dve.wait_ge(adj_in[c % 4], 16 * (c // 4 + 1))
                    dve.tensor_scalar(flat[:, c * 1024:(c + 1) * 1024], adjacent[:, c % 4, :], 0, None, ALU.is_le).then_inc(adj_used, 1)

        finish_norm(nc, sem, stats, scratch, rstd, shift, "gnn0")
        graph_attention(nc, sem, 0, x, masked, stats, rstd, shift, ident[:, :],
                        {"bilinear": W["bilinear"][:, :], "key_side": W["key_col"][:, :], "query_side": W["query_row0"][:, :],
                         "own": W["own"][:, :], "other": W["other0"][:, :]},
                        (coarse_dram, row_ids, wanted, counts))
        descend(2, found[:, 0, :], found[:, 1, :])
        renew_semaphores()
        finish_norm(nc, sem, stats, scratch, rstd, shift, "x0")
        experts0(nc, sem, a, x, stats, rstd, shift, ident[:, :], ones, upto, slots_dram, rows_dram)
        renew_semaphores()
        finish_norm(nc, sem, stats, scratch, rstd, shift, "gnn1")
        graph_attention(nc, sem, 1, x, masked, stats, rstd, shift, ident[:, :],
                        {"key_side": W["key_row1"][:, :], "query_side": W["query_row1"][:, :],
                         "bias": W["bias1"][:, :], "other": W["other1"][:, :]},
                        (keys_dram, row_ids, wanted, counts))
        descend(3, found[:, 1, :], found[:, 0, :])
        masked_ctx.close()
        renew_semaphores()
        finish_norm(nc, sem, stats, scratch, rstd, shift, "gat")
        gates = keep("gates", [P, GRAPHS, TOP_EXPERTS])
        with ExitStack() as ctx:
            def sb(name, shape, dt=F32):
                return ctx.enter_context(nc.sbuf_tensor(name, shape, dt))

            node, last_node = sb("node", [P, NODES, TAB]), sb("last_node", [P, TAB])
            first_edge, degree, clamped, loops = sb("first_edge", [P, NODES]), sb("degree", [P, NODES]), sb("clamped", [P, NODES]), sb("loops", [P, 2], I32)
            with ExitStack() as inner:
                tab, gat_w, att, part = (inner.enter_context(nc.sbuf_tensor(n, s, F32)) for n, s in (
                    ("tab", [P, GRAPHS, TAB]), ("gat_w", [P, TAB]), ("att", [P, 2, GAT]), ("att_part", [P, 2, GAT])))
                with nc.Block() as block:
                    loaded, made = sem("gat_loaded"), sem("gat_made")

                    @block.sync
                    def _(sp):
                        sp.dma_start(gat_w[:, 0:GAT], a["gat_w"]).then_inc(loaded, 16)
                        sp.dma_start(att[:, :, :], bass.AP(a["att"].tensor, 0, [[0, P], [1, 2 * GAT]]).rearrange("p (a c) -> p a c", a=2)).then_inc(loaded, 16)

                    @block.vector
                    def _(dve):
                        dve.wait_ge(loaded, 32)
                        dve.tensor_tensor(part[:, :, :], att[:, :, :], gat_w[:, 0:GAT].unsqueeze(1).to_broadcast([P, 2, GAT]), ALU.mult).then_inc(made, 1)
                        dve.wait_ge(made, 1)
                        dve.tensor_reduce(gat_w[:, GAT:TAB], part[:, :, :].rearrange("p a (h e) -> p (a h) e", h=HEADS), AX_X, ALU.add)

                project(nc, sem, "gat", x, rstd, shift, ident[:, :], gat_w[:, :], TAB, tab)
                prepare_nodes(nc, sem, tab, table_dram, node, last_node, ident[:, :], ones, wanted, found, counted[:, :],
                              first_edge, degree, clamped, loops)
            gather_edges(nc, sem, source_ids, table_dram[:, 0:TAB], edges_dram, loops)
            attend_edges(nc, sem, a, edges_dram, node, last_node, first_edge, degree, clamped, loops, gates, ident[:, :])
        renew_semaphores()
        experts1(nc, sem, a, x, rstd, shift, gates, ident[:, :], out)


_OUTS = [((GRAPHS, NODES, FEAT), "float32")]


def kernel(**inputs):
    import numpy as _np
    import concourse.bacc as _bacc
    from concourse import mybir as _mybir
    from concourse.bass_utils import run_bass_kernel_spmd as _run

    i = {k: _np.asarray(v) for k, v in inputs.items()}
    hc, hc1 = HC, HC1
    laid = {
        "x": i["x"].transpose(1, 0, 2),
        "adj": i["adj"].transpose(1, 0, 2).reshape(P, -1),
        "edges": i["L1_ffn_edge_index"],
        "gnn0_wT": i["L0_gnn_W"].T,
        "gnn0_a12": i["L0_gnn_a_12"],
        "gnn0_a": _np.concatenate([i["L0_gnn_a_1"], i["L0_gnn_a_2"]], 1),
        "gnn0_w1": i["L0_gnn_W_1"],
        "gnn0_w2": i["L0_gnn_W_2"],
        "gnn1_w": i["L1_gnn_W"],
        "gnn1_wT": i["L1_gnn_W"].T,
        "gnn1_aT": i["L1_gnn_a"].T,
        "gnn1_bias": i["L1_gnn_bias"],
        "gate_w": i["L0_ffn_gate_w"],
        "gate_b": i["L0_ffn_gate_b"],
        "w1": i["L0_ffn_w1"],
        "b1T": i["L0_ffn_b1"].reshape(EXPERTS, hc, P).transpose(0, 2, 1),
        "w2": i["L0_ffn_w2"].reshape(EXPERTS, hc, P, FEAT).transpose(0, 2, 1, 3),
        "b2": i["L0_ffn_b2"],
        "gat_w": i["L1_ffn_W_gat"],
        "att": _np.stack([i["L1_ffn_att_src"].reshape(-1), i["L1_ffn_att_dst"].reshape(-1)]),
        "gat_b": i["L1_ffn_b_gat"],
        "gamma": i["L1_ffn_ln_gamma"],
        "beta": i["L1_ffn_ln_beta"],
        "w1b": i["L1_ffn_W1"].transpose(1, 0, 2),
        "b1b": i["L1_ffn_b1"].reshape(TOP_EXPERTS, hc1, P).transpose(2, 0, 1).reshape(P, -1),
        "w2b": i["L1_ffn_W2"].reshape(TOP_EXPERTS, hc1, P, FEAT).transpose(2, 0, 1, 3).reshape(P, -1, FEAT),
        "b2b": i["L1_ffn_b2"],
    }
    nc = _bacc.Bacc("TRN2", target_bir_lowering=False, num_devices=1)
    arrays, args = {}, {}
    for name, a in laid.items():
        a = _np.ascontiguousarray(a)
        arrays[f"in_{name}_dram"] = a
        args[name] = nc.dram_tensor(f"in_{name}_dram", a.shape, _mybir.dt.from_np(a.dtype), kind="ExternalInput").ap()
    (shape, dtype), = _OUTS
    out = nc.dram_tensor("out_dram", (NODES, GRAPHS, FEAT), _mybir.dt.from_np(_np.dtype(dtype)), kind="ExternalOutput").ap()
    build(nc, args, out)
    r = _run(nc, [arrays], core_ids=[0])
    return _np.ascontiguousarray(_np.asarray(r.results[0]["out_dram"]).transpose(1, 0, 2))
```

```python
from contextlib import ExitStack

import concourse.bass as bass
from concourse import mybir

ALU = mybir.AluOpType
ACT = mybir.ActivationFunctionType
F32 = mybir.dt.float32
BF16 = mybir.dt.bfloat16
I32 = mybir.dt.int32
U32 = mybir.dt.uint32
AX_X = mybir.AxisListType.X

P = 128
GRAPHS = NODES = FEAT = 128
PER = 4
GROUPS = GRAPHS // PER
WIDE = PER * FEAT
EPS = 1e-5
SLOPE = 0.2
TOKENS = GRAPHS * NODES

EXPERTS = 8
HIDDEN = 512
HC = HIDDEN // P
CAPACITY = (5 * TOKENS + 4 * EXPERTS - 1) // (4 * EXPERTS)
SLOT_GROUPS = CAPACITY // WIDE

EDGES = 524288
COLS = EDGES // P
LOG_COLS = COLS.bit_length() - 1
LOG_EDGES = EDGES.bit_length() - 1
NODE_BIT = TOKENS
LOG_NODES = TOKENS.bit_length() - 1
KEY_INSIDE = 1 << 28
KEY_CLAMPED = 2 << 28
KEY_DROPPED = 3 << 28
FAN = 64
SEARCHES = 2 * NODES
PER_SEARCH = SEARCHES // GROUPS
HEADS = 4
TOP_EXPERTS = 4
GAT = HEADS * TOP_EXPERTS
ROW = GAT + HEADS
TAB = ROW + HEADS
WINDOW = 24
EDGE_TILES = 8
EDGE_STEP = EDGE_TILES * P
ADJ_SLOTS = 4
ADJ_PART = COLS // ADJ_SLOTS
ADJ_PARTS = GRAPHS * NODES // ADJ_PART
STATS_AT_A_TIME = -(-GRAPHS // (2 * (LOG_EDGES - LOG_COLS)))
CLEAR = 2560
HIDDEN1 = 256
HC1 = HIDDEN1 // P
BIG = 1e30


def ge(engine, semaphore, value):
    if isinstance(value, int) and value <= 0:
        return
    engine.wait_ge(semaphore, value)


def across(ap, n):
    return bass.AP(ap.tensor, 0, [[0, P], [1, n]])


def pipeline(engine, first, step, total=GROUPS, after=0):
    for n in range(first, 4):
        step(n, n % 4)
    with engine.Fori(1, total // 4 - 1) as turn:
        for u in range(4):
            step(turn * 4 + u, u)
    for n in range(total - 4, total + after):
        step(n, n % 4)


def live(n, total=GROUPS):
    return not isinstance(n, int) or 0 <= n < total


def sort_edges(nc, sem, edge_index, x_dram, adj, x, stats, masked, keys_dram, coarse_dram, starts, counted, source_ids, ident, row_id, clear):
    HALF = COLS // 2
    BLOCKS = COLS // P
    with ExitStack() as ctx:
        ping = ctx.enter_context(nc.sbuf_tensor("sort_ping", [P, COLS], F32))
        pong = ctx.enter_context(nc.sbuf_tensor("sort_pong", [P, COLS], F32))
        sense = ctx.enter_context(nc.sbuf_tensor("sort_sense", [P, 14], F32))
        bits = ctx.enter_context(nc.sbuf_tensor("sort_bits", [P, 8], I32))
        small = ctx.enter_context(nc.sbuf_tensor("sort_small", [P, 2 * FAN], F32))
        zeros = ctx.enter_context(nc.sbuf_tensor("zeros", [P, CLEAR], F32))
        zeroed, cleared = sem("zeroed"), sem("tables_cleared")
        adjacent = ctx.enter_context(nc.sbuf_tensor("adjacent", [P, ADJ_SLOTS, ADJ_PART], I32))
        x_in, key_made, adj_used = sem("x_in"), sem("key_made"), sem("adj_used")
        adj_in = [sem(f"adj_in{c}") for c in range(ADJ_SLOTS)]
        turned = ctx.enter_context(nc.psum_tensor("sort_turned", [P, 8, 512], F32))
        edges_in, made, half_ready = sem("edges_in"), sem("sort_step"), sem("half_ready")
        half_turned, half_copied, keys_out = sem("half_turned"), sem("half_copied"), sem("keys_out")
        sorted_s, coarse_s, starts_turned, starts_s = sem("sorted"), sem("coarse"), sem("starts_turned"), sem("starts")
        turns = [(k, back, h) for k in range(LOG_COLS + 1, LOG_EDGES + 1) for back in (0, 1) for h in (0, 1)]
        source = ping[:, :].bitcast(I32)
        target = pong[:, :].bitcast(I32)
        from_to = {}
        block = ctx.enter_context(nc.Block())

        @block.sync
        def _(sp):
            sp.dma_start(source, edge_index[0, :].rearrange("(p f) -> p f", p=P)).then_inc(edges_in, 16)
            sp.dma_start(target, edge_index[1, :].rearrange("(p f) -> p f", p=P)).then_inc(edges_in, 16)
            sp.dma_start(x[:, :, :], x_dram).then_inc(x_in, 16)
            sp.wait_ge(key_made, 1)
            for c in range(ADJ_PARTS):
                ge(sp, adj_used, c - ADJ_SLOTS + 1)
                sp.dma_start(adjacent[:, c % ADJ_SLOTS, :], adj[:, c * ADJ_PART:(c + 1) * ADJ_PART]).then_inc(adj_in[c % ADJ_SLOTS], 16)
            sp.wait_ge(zeroed, 1)
            sent = 0
            for table in clear:
                flat = table.rearrange("(p r) d -> p (r d)", p=P)
                for c in range(0, flat.shape[1], CLEAR):
                    width = min(CLEAR, flat.shape[1] - c)
                    sp.dma_start(flat[:, c:c + width], zeros[:, 0:width]).then_inc(cleared, 16)
                    sent += 16
            sp.wait_ge(cleared, sent)

        @block.vector
        def _(dve):
            steps = [0]

            def step(ins):
                ins.then_inc(made, 1)
                steps[0] += 1

            def join():
                dve.wait_ge(made, steps[0])

            def link(ins):
                step(ins)
                join()

            for b in range(7):
                step(dve.tensor_scalar(bits[:, b:b + 1], row_id, b, 1, ALU.logical_shift_right, ALU.bitwise_and))
            join()
            link(dve.tensor_scalar(sense[:, 0:7], bits[:, 0:7], -2.0, 1.0, ALU.mult, ALU.add))
            step(dve.tensor_tensor(sense[:, 7:13], sense[:, 0:6], sense[:, 1:7], ALU.mult))
            step(dve.tensor_copy(sense[:, 13:14], sense[:, 6:7]))
            join()
            dve.wait_ge(edges_in, 32)
            part = source_ids[:, 0:COLS].bitcast(I32)
            key = adjacent[:, :, :].rearrange("p c f -> p (c f)")
            beyond = NODE_BIT
            inner = NODE_BIT - 1
            link(dve.tensor_scalar(part, target, inner, LOG_NODES, ALU.bitwise_and, ALU.logical_shift_left))
            link(dve.scalar_tensor_tensor(key, source, inner, part, ALU.bitwise_and, ALU.bitwise_or))
            link(dve.tensor_tensor(part, source, target, ALU.bitwise_or))
            link(dve.tensor_scalar(part, part, beyond, 15, ALU.bitwise_and, ALU.logical_shift_left))
            link(dve.tensor_tensor(key, key, part, ALU.bitwise_or))
            link(dve.scalar_tensor_tensor(part, source, beyond, target, ALU.bitwise_xor, ALU.bitwise_or))
            link(dve.tensor_scalar(part, part, beyond, 14, ALU.bitwise_and, ALU.logical_shift_left))
            link(dve.tensor_tensor(source, key, part, ALU.bitwise_or))
            dve.tensor_copy(bits[:, 7:8], bits[:, 0:1]).then_inc(key_made, 1)
            graph = [0]

            def some_stats():
                if graph[0] == 0:
                    dve.wait_ge(x_in, 16)
                for b in range(graph[0], min(graph[0] + STATS_AT_A_TIME, GRAPHS)):
                    dve.bn_stats(stats[:, b, :], x[:, b, :])
                graph[0] += STATS_AT_A_TIME

            def both_ways(k, j, a, b):
                c, m, n = 1 << j, 1 << (k - 1 - j), COLS >> (k + 1)
                va = a[:, :].rearrange("p (n d m t c) -> p n d m t c", n=n, d=2, m=m, t=2, c=c)
                vb = b[:, :].rearrange("p (n d m t c) -> p n d m t c", n=n, d=2, m=m, t=2, c=c)
                for d in (0, 1):
                    ops = (ALU.max, ALU.min) if d else (ALU.min, ALU.max)
                    for t in (0, 1):
                        step(dve.tensor_tensor(vb[:, :, d, :, t, :], va[:, :, d, :, 0, :], va[:, :, d, :, 1, :], ops[t]))
                join()

            def upwards(a, b, c):
                va = a.rearrange("p (m t c) -> p m t c", t=2, c=c)
                vb = b.rearrange("p (m t c) -> p m t c", t=2, c=c)
                for t, op in ((0, ALU.min), (1, ALU.max)):
                    step(dve.tensor_tensor(vb[:, :, t, :], va[:, :, 0, :], va[:, :, 1, :], op))
                join()

            a, b = ping, pong
            for k in range(1, LOG_COLS):
                for j in range(k - 1, -1, -1):
                    both_ways(k, j, a, b)
                    a, b = b, a
            n = 0
            for k in range(LOG_COLS, LOG_EDGES + 1):
                change = k - LOG_COLS if k == LOG_COLS else 7 + k - LOG_COLS - 1
                link(dve.tensor_scalar(b[:, :], a[:, :], sense[:, change:change + 1], None, ALU.mult))
                a, b = b, a
                if k > LOG_COLS:
                    from_to[n] = from_to[n + 1] = (a, b)
                    dve.tensor_copy(bits[:, 7:8], bits[:, 0:1]).then_inc(half_ready, 2)
                    some_stats()
                    a, b = b, a
                    for h in (0, 1):
                        cols = slice(h * HALF, (h + 1) * HALF)
                        dve.wait_ge(half_copied, n + h + 1)
                        c, d = a, b
                        for j in range(k - 1, LOG_COLS - 1, -1):
                            upwards(c[:, cols], d[:, cols], 1 << (j - LOG_COLS))
                            c, d = d, c
                        from_to[n + 2 + h] = (c, d)
                        dve.tensor_copy(bits[:, 7:8], bits[:, 0:1]).then_inc(half_ready, 1)
                    a, b = d, c
                    n += 4
                    some_stats()
                    dve.wait_ge(half_copied, n)
                for j in range(LOG_COLS - 1, -1, -1):
                    upwards(a[:, :], b[:, :], 1 << j)
                    a, b = b, a
            from_to["sorted"] = from_to[n] = from_to[n + 1] = (a, b)
            link(dve.tensor_copy(small[:, 0:FAN], a[:, 0:COLS:FAN]))
            dve.tensor_copy(bits[:, 7:8], bits[:, 0:1]).then_inc(sorted_s, 1)
            link(dve.tensor_scalar(bits[:, 6:7], row_id, 0, KEY_DROPPED, ALU.bitwise_and, ALU.bitwise_or))
            link(dve.tensor_scalar(pong[:, :] if a is ping else ping[:, :], a[:, :], bits[:, 6:7].bitcast(F32), None, ALU.is_lt))
            link(dve.tensor_reduce(counted, (pong if a is ping else ping)[:, :], AX_X, ALU.add))
            dve.tensor_copy(bits[:, 7:8], bits[:, 0:1]).then_inc(half_ready, 2)
            dve.wait_ge(starts_turned, 1)
            link(dve.tensor_copy(starts[:, :], turned[:, 0, 0:P]))
            dve.tensor_copy(bits[:, 7:8], bits[:, 0:1]).then_inc(starts_s, 1)
            dve.wait_ge(half_copied, n + 2)
            tiles = (pong if a is ping else ping)[:, :].bitcast(U32)
            link(dve.tensor_scalar(source_ids[:, 0:COLS].rearrange("q (p b) -> q b p", b=BLOCKS),
                                   tiles.rearrange("q (b p) -> q b p", p=P), NODE_BIT - 1, None, ALU.bitwise_and))

        @block.tensor
        def _(pe):
            total = len(turns)
            for n in range(total + 2):
                if n == total:
                    pe.wait_ge(sorted_s, 1)
                    pe.wait_ge(half_copied, total)
                    pe.transpose(turned[:, 0, 0:P], from_to["sorted"][0][:, 0:1].to_broadcast([P, P]), ident).then_inc(starts_turned, 1)
                    pe.wait_ge(starts_s, 1)
                pe.wait_ge(half_ready, n + 1 if n % 4 else n + 2)
                ge(pe, half_copied, n - 1)
                h = n % 2
                for blk in range(h * BLOCKS // 2, (h + 1) * BLOCKS // 2):
                    last = pe.transpose(turned[:, blk // 4, (blk % 4) * P:(blk % 4 + 1) * P],
                                        from_to[n][0][:, blk * P:(blk + 1) * P], ident)
                last.then_inc(half_turned, 1)

        @block.scalar
        def _(act):
            for n in range(len(turns) + 2):
                act.wait_ge(half_turned, n + 1)
                for bank in range(4 * (n % 2), 4 * (n % 2) + 4):
                    last = act.activation(from_to[n][1][:, bank * 512:bank * 512 + 512], turned[:, bank, :], ACT.Copy)
                last.then_inc(half_copied, 1)

        @block.gpsimd
        def _(pool):
            pool.memset(zeros[:, :], 0.0).then_inc(zeroed, 1)
            flat = masked[:, :, :].rearrange("p b j -> p (b j)")
            for c in range(ADJ_PARTS):
                pool.wait_ge(adj_in[c % ADJ_SLOTS], 16 * (c // ADJ_SLOTS + 1))
                pool.tensor_scalar(flat[:, c * ADJ_PART:(c + 1) * ADJ_PART], adjacent[:, c % ADJ_SLOTS, :], 0, None, ALU.is_le).then_inc(adj_used, 1)
            pool.wait_ge(sorted_s, 1)
            pool.dma_start(keys_dram.rearrange("(p b) f -> p (b f)", p=P), from_to["sorted"][0][:, :]).then_inc(keys_out, 16)
            pool.dma_start(coarse_dram, small[:, 0:FAN]).then_inc(keys_out, 16)
            pool.wait_ge(keys_out, 32)


def finish_norm(nc, sem, stats, scratch, rstd, shift, tag):
    made, rooted = sem(f"norm_step_{tag}"), sem(f"norm_root_{tag}")
    even, odd = stats[:, :, 1], stats[:, :, 4]
    with nc.Block() as block:
        @block.vector
        def _(dve):
            steps = [0]

            def link(ins):
                ins.then_inc(made, 1)
                steps[0] += 1
                dve.wait_ge(made, steps[0])

            link(dve.tensor_tensor(scratch[:, 0, :], even, odd, ALU.subtract))
            link(dve.scalar_tensor_tensor(scratch[:, 1, :], scratch[:, 0, :], 0.25, scratch[:, 0, :], ALU.mult, ALU.mult))
            link(dve.tensor_tensor(scratch[:, 0, :], stats[:, :, 2], stats[:, :, 5], ALU.add))
            link(dve.scalar_tensor_tensor(scratch[:, 2, :], scratch[:, 0, :], 1.0 / FEAT, scratch[:, 1, :], ALU.mult, ALU.add))
            link(dve.tensor_scalar(scratch[:, 2, :], scratch[:, 2, :], EPS, None, ALU.add))
            dve.wait_ge(rooted, 1)
            link(dve.reciprocal(rstd[:, :], scratch[:, 1, :]))
            link(dve.tensor_tensor(scratch[:, 0, :], even, odd, ALU.add))
            link(dve.scalar_tensor_tensor(shift[:, :], scratch[:, 0, :], -0.5, rstd[:, :], ALU.mult, ALU.mult))

        @block.scalar
        def _(act):
            act.wait_ge(made, 5)
            act.activation(scratch[:, 1, :], scratch[:, 2, :], ACT.Sqrt).then_inc(rooted, 1)


def normalise(act, out, x, rstd, shift, g):
    for u in range(PER):
        b = g * PER + u
        last = act.activation(out[:, u, :], x[:, bass.ds(b, 1), :].rearrange("p o f -> p (o f)"), ACT.Identity,
                              bias=shift[:, bass.ds(b, 1)], scale=rstd[:, bass.ds(b, 1)])
    return last


def graph_attention(nc, sem, layer, x, masked, stats, rstd, shift, ident, w, search):
    first = layer == 0
    fill = -9e15 if first else -1e12
    with ExitStack() as ctx:
        def sb(name, shape, dt=F32):
            return ctx.enter_context(nc.sbuf_tensor(f"{name}{layer}", shape, dt))

        def bank(name):
            return ctx.enter_context(nc.psum_tensor(f"{name}{layer}", [P, PER, P], F32))

        def s(name):
            return sem(f"g{layer}_{name}")

        feat = sb("feat", [P, 2, PER, FEAT])
        featT = sb("featT", [P, 4, PER, NODES])
        right = sb("right", [P, 4, PER, FEAT])
        queries = sb("queries", [P, 2, PER, NODES])
        low = sb("low", [P, PER, NODES])
        score = sb("score", [P, PER, NODES])
        probs = sb("probs", [P, 2, PER, NODES])
        probsT = sb("probsT", [P, PER, NODES])
        row = sb("row", [P, 3, PER])
        under = sb("under", [P, PER, FEAT])
        grown = sb("grown", [P, PER, FEAT])
        summed = sb("summed", [P, PER, FEAT])
        chosen = sb("chosen", [P, 2, PER_SEARCH], U32)
        fetched = sb("fetched", [P, 2, PER_SEARCH, FAN])
        before = sb("before", [P, PER_SEARCH, FAN])
        b_featT, b_queries, b_right, b_probsT = map(bank, ("b_featT", "b_queries", "b_right", "b_probsT"))
        b_score, b_out = (ctx.enter_context(nc.psum_tensor(f"{n}{layer}", [P, 2, PER, P], F32)) for n in ("b_score", "b_out"))
        normed, turned, featT_s, asked, queries_s, righted, right_s = map(
            s, ("normed", "turned", "featT", "asked", "queries", "righted", "right"))
        scored, low_s, score_s, shifted, exped, probs_s, probs_turned, probsT_s, out_s = map(
            s, ("scored", "low", "score", "shifted", "exped", "probs", "probs_turned", "probsT", "out"))
        under_s, grown_s, out_read, updated, stats_s = map(s, ("under", "grown", "out_read", "updated", "stats"))
        chain_b, chain_d, chain_s, begun = s("chain_b"), s("chain_d"), s("chain_s"), s("begun")
        chosen_s, fetched_s, looked = s("chosen"), (s("fetched_even"), s("fetched_odd")), s("looked")
        table, row_ids, wanted, counts = search
        block = ctx.enter_context(nc.Block())

        @block.scalar
        def _(act):
            def step(n, u):
                m, b, a, f = n - 1, n + 2, n + 3, n + 4
                if live(n):
                    act.wait_ge(probs_turned, n + 1)
                    ge(act, out_s, n)
                    act.activation(probsT[:, :, :], b_probsT[:, :, :], ACT.Copy).then_inc(probsT_s, 1)
                if live(b):
                    act.wait_ge(scored, b + 1)
                    ge(act, score_s, b)
                    act.activation(low[:, :, :], b_score[:, (u + 2) % 2, :, :], ACT.Copy, scale=SLOPE).then_inc(low_s, 1)
                if live(a):
                    act.wait_ge(turned, a + 1)
                    ge(act, out_s, a - 3)
                    act.activation(featT[:, (u + 3) % 4, :, :], b_featT[:, :, :], ACT.Copy).then_inc(featT_s, 1)
                if live(m) and first:
                    act.wait_ge(under_s, m + 1)
                    ge(act, out_read, m)
                    act.activation(grown[:, :, :], under[:, :, :], ACT.Exp).then_inc(grown_s, 1)
                if live(f):
                    ge(act, turned, f - 1)
                    normalise(act, feat[:, (u + 4) % 2, :, :], x, rstd, shift, f).then_inc(normed, 1)
                if live(b):
                    act.wait_ge(shifted, b + 1)
                    ge(act, probs_turned, b - 1)
                    act.activation(probs[:, (u + 2) % 2, :, :], score[:, :, :], ACT.Exp).then_inc(exped, 1)
                if live(a) and first:
                    act.wait_ge(asked, a + 1)
                    ge(act, scored, a - 1)
                    act.activation(queries[:, (u + 3) % 2, :, :], b_queries[:, :, :], ACT.Identity, bias=w["key_side"]).then_inc(queries_s, 1)
                    act.wait_ge(righted, a + 1)
                    ge(act, out_s, a - 3)
                    act.activation(right[:, (u + 3) % 4, :, :], b_right[:, :, :], ACT.Copy).then_inc(right_s, 1)

            pipeline(act, -4, step, after=1)

        @block.tensor
        def _(pe):
            def step(n, u):
                b, a = n + 2, n + 3
                if live(n):
                    pe.wait_ge(probs_s, n + 1)
                    ge(pe, probsT_s, n)
                    for v in range(PER):
                        last = pe.transpose(b_probsT[:, v, :], probs[:, u % 2, v, :], ident)
                    last.then_inc(probs_turned, 1)
                if live(b):
                    f = featT[:, (u + 2) % 4, :, :]
                    ge(pe, score_s, b - 1)
                    if first:
                        pe.wait_ge(queries_s, b + 1)
                    else:
                        pe.wait_ge(featT_s, b + 1)
                    for v in range(PER):
                        pe.matmul(b_score[:, (u + 2) % 2, v, :], queries[:, (u + 2) % 2, v, :] if first else w["key_side"], f[:, v, :],
                                  start=True, stop=False)
                        last = pe.matmul(b_score[:, (u + 2) % 2, v, :], f[:, v, :], w["query_side"], start=False, stop=True)
                    last.then_inc(scored, 1)
                if live(a):
                    pe.wait_ge(normed, a + 1)
                    ge(pe, featT_s, a)
                    for v in range(PER):
                        last = pe.transpose(b_featT[:, v, :], feat[:, (u + 3) % 2, v, :], ident)
                    last.then_inc(turned, 1)
                if live(n):
                    pe.wait_ge(probsT_s, n + 1)
                    pe.wait_ge(right_s, n + 1)
                    ge(pe, out_read, n - 1)
                    for v in range(PER):
                        if first:
                            pe.matmul(b_out[:, u % 2, v, :], featT[:, u, v, :], w["own"], start=True, stop=False)
                        last = pe.matmul(b_out[:, u % 2, v, :], probsT[:, v, :], right[:, u, v, :], start=not first, stop=True)
                    last.then_inc(out_s, 1)
                if live(a):
                    f = featT[:, (u + 3) % 4, :, :]
                    pe.wait_ge(featT_s, a + 1)
                    if first:
                        ge(pe, queries_s, a)
                        pe.matmul(b_queries[:, :, :], w["bilinear"], f, start=True, stop=True).then_inc(asked, 1)
                    ge(pe, right_s, a)
                    for v in range(PER):
                        last = pe.matmul(b_right[:, v, :], f[:, v, :], w["other"], start=True, stop=True)
                    last.then_inc(righted, 1)

            pipeline(pe, -3, step)

        @block.vector
        def _(dve):
            def step(n, u):
                m, d, b, a = n - 1, n + 1, n + 2, n + 3
                if live(d):
                    p = probs[:, (u + 1) % 2, :, :]
                    dve.wait_ge(exped, d + 1)
                    dve.tensor_reduce(row[:, 1, :], p, AX_X, ALU.add).then_inc(chain_d, 1)
                    dve.wait_ge(chain_d, d * 2 + 1)
                    dve.reciprocal(row[:, 2, :], row[:, 1, :]).then_inc(chain_d, 1)
                    dve.wait_ge(chain_d, d * 2 + 2)
                    dve.tensor_tensor(p, p, row[:, 2, :].unsqueeze(2).to_broadcast([P, PER, NODES]), ALU.mult).then_inc(probs_s, 1)
                if live(m) and first:
                    dve.wait_ge(out_s, m + 1)
                    ge(dve, grown_s, m)
                    dve.tensor_scalar(under[:, :, :], b_out[:, (u + 1) % 2, :, :], 0.0, None, ALU.min).then_inc(under_s, 1)
                if live(b):
                    dve.wait_ge(low_s, b + 1)
                    ge(dve, exped, b)
                    dve.tensor_tensor(score[:, :, :], b_score[:, (u + 2) % 2, :, :], low[:, :, :], ALU.max).then_inc(score_s, 1)
                    dve.wait_ge(score_s, b + 1)
                    dve.scalar_tensor_tensor(score[:, :, :], masked[:, bass.ds(b * PER, PER), :], fill, score[:, :, :],
                                             ALU.mult, ALU.add).then_inc(chain_b, 1)
                    dve.wait_ge(chain_b, b * 2 + 1)
                    dve.tensor_reduce(row[:, 0, :], score[:, :, :], AX_X, ALU.max).then_inc(chain_b, 1)
                    dve.wait_ge(chain_b, b * 2 + 2)
                    dve.tensor_tensor(score[:, :, :], score[:, :, :], row[:, 0, :].unsqueeze(2).to_broadcast([P, PER, NODES]),
                                      ALU.subtract).then_inc(shifted, 1)
                if live(m):
                    mine = x[:, bass.ds(m * PER, PER), :]
                    if first:
                        dve.wait_ge(grown_s, m + 1)
                        dve.scalar_tensor_tensor(summed[:, :, :], b_out[:, (u + 1) % 2, :, :], 0.0, grown[:, :, :],
                                                 ALU.max, ALU.add).then_inc(out_read, 1)
                        dve.wait_ge(out_read, m + 1)
                        dve.scalar_tensor_tensor(mine, summed[:, :, :], -1.0, mine, ALU.add, ALU.add).then_inc(updated, 1)
                    else:
                        dve.wait_ge(out_s, m + 1)
                        dve.tensor_tensor(mine, b_out[:, (u + 1) % 2, :, :], mine, ALU.add).then_inc(out_read, 1)
                if live(a) and not first:
                    dve.wait_ge(righted, a + 1)
                    ge(dve, out_s, a - 3)
                    dve.tensor_tensor(right[:, (u + 3) % 4, :, :], b_right[:, :, :],
                                      w["bias"].unsqueeze(1).to_broadcast([P, PER, FEAT]), ALU.add).then_inc(right_s, 1)
                if live(m):
                    dve.wait_ge(updated if first else out_read, m + 1)
                    for v in range(PER):
                        q = m * PER + v
                        dve.bn_stats(stats[:, bass.ds(q, 1), :].rearrange("p o s -> p (o s)"),
                                     x[:, bass.ds(q, 1), :].rearrange("p o f -> p (o f)"))
                if live(n):
                    dve.wait_ge(fetched_s[u % 2], (n - u % 2) * (8 * PER_SEARCH) + 16 * PER_SEARCH)
                    dve.tensor_tensor(before[:, :, :], fetched[:, u % 2, :, :],
                                      wanted[:, bass.ds(n * PER_SEARCH, PER_SEARCH)].unsqueeze(2).to_broadcast([P, PER_SEARCH, FAN]),
                                      ALU.is_lt).then_inc(chain_s, 1)
                    dve.wait_ge(chain_s, n + 1)
                    dve.tensor_reduce(counts[:, bass.ds(n * PER_SEARCH, PER_SEARCH)], before[:, :, :], AX_X, ALU.add).then_inc(looked, 1)
                    dve.wait_ge(looked, n + 1)

            pipeline(dve, -3, step, after=1)

        @block.gpsimd
        def _(pool):
            def step(n, u):
                if not isinstance(n, int) or n >= 2:
                    pool.wait_ge(looked, n - 1)
                pool.tensor_copy(chosen[:, u % 2, :], row_ids[:, bass.ds(n * PER_SEARCH, PER_SEARCH)]).then_inc(chosen_s, 1)
                pool.wait_ge(chosen_s, n + 1)
                pool.sem_inc(begun, 1)
                for c in range(PER_SEARCH):
                    pool.indirect_dma_start(fetched[:, u % 2, c, :], None, table,
                                            bass.IndirectOffsetOnAxis(chosen[:, u % 2, c:c + 1], 0)).then_inc(fetched_s[u % 2], 16)

            pipeline(pool, 0, step)


def project(nc, sem, tag, x, rstd, shift, ident, weight, cols, into):
    with ExitStack() as ctx:
        feat = ctx.enter_context(nc.sbuf_tensor(f"feat_{tag}", [P, 2, PER, FEAT], F32))
        featT = ctx.enter_context(nc.sbuf_tensor(f"featT_{tag}", [P, 2, PER, NODES], F32))
        b_featT = ctx.enter_context(nc.psum_tensor(f"b_featT_{tag}", [P, 2, PER, P], F32))
        b_out = ctx.enter_context(nc.psum_tensor(f"b_out_{tag}", [P, 2, PER, P], F32))
        normed, turned, featT_s, projected, kept = (sem(f"{tag}_{n}") for n in ("normed", "turned", "featT", "projected", "kept"))
        block = ctx.enter_context(nc.Block())

        @block.scalar
        def _(act):
            def step(n, u):
                a, f = n + 1, n + 2
                if live(a):
                    act.wait_ge(turned, a + 1)
                    ge(act, projected, a - 1)
                    act.activation(featT[:, (u + 1) % 2, :, :], b_featT[:, (u + 1) % 2, :, :], ACT.Copy).then_inc(featT_s, 1)
                if live(f):
                    ge(act, turned, f - 1)
                    normalise(act, feat[:, u % 2, :, :], x, rstd, shift, f).then_inc(normed, 1)

            pipeline(act, -2, step)

        @block.tensor
        def _(pe):
            def step(n, u):
                a = n + 1
                if live(a):
                    pe.wait_ge(normed, a + 1)
                    ge(pe, featT_s, a - 1)
                    for v in range(PER):
                        last = pe.transpose(b_featT[:, (u + 1) % 2, v, :], feat[:, (u + 1) % 2, v, :], ident)
                    last.then_inc(turned, 1)
                if live(n):
                    pe.wait_ge(featT_s, n + 1)
                    ge(pe, kept, n - 1)
                    for v in range(PER):
                        last = pe.matmul(b_out[:, u % 2, v, 0:cols], featT[:, u % 2, v, :], weight, start=True, stop=True)
                    last.then_inc(projected, 1)

            pipeline(pe, -1, step)

        @block.vector
        def _(dve):
            def step(n, u):
                dve.wait_ge(projected, n + 1)
                dve.tensor_scalar(into[:, bass.ds(n * PER, PER), :], b_out[:, u % 2, :, 0:cols], 1.0, None, ALU.mult).then_inc(kept, 1)

            pipeline(dve, 0, step)


def experts0(nc, sem, a, x, stats, rstd, shift, ident, ones, upto, slots_dram, rows_dram):
    with ExitStack() as outer:
        def kp(name, shape, dt=F32):
            return outer.enter_context(nc.sbuf_tensor(name, shape, dt))

        send = kp("send", [P, GRAPHS], U32)
        fetch = kp("fetch", [P, GRAPHS], U32)
        weight = kp("gate_weight", [P, GRAPHS])

        with ExitStack() as ctx:
            def sb(name, shape, dt=F32):
                return ctx.enter_context(nc.sbuf_tensor(name, shape, dt))

            gate_w, gate_b, logits = sb("gate_w", [P, EXPERTS]), sb("gate_b", [P, EXPERTS]), sb("gate_logits", [P, GRAPHS, EXPERTS])
            loaded = sem("gate_loaded")
            with nc.Block() as block:
                @block.sync
                def _(sp):
                    sp.dma_start(gate_w[:, :], a["gate_w"]).then_inc(loaded, 16)
                    sp.dma_start(gate_b[:, :], across(a["gate_b"], EXPERTS)).then_inc(loaded, 16)
                    sp.wait_ge(loaded, 32)
            project(nc, sem, "gate", x, rstd, shift, ident, gate_w[:, :], EXPERTS, logits)

            grown, chosen, tot, scan, work = (sb(n, [P, GRAPHS, EXPERTS]) for n in ("gate_grown", "gate_chosen", "gate_tot", "gate_scan", "gate_work"))
            best, prob, pos, base, kept = (sb(n, [P, GRAPHS]) for n in ("gate_best", "gate_prob", "gate_pos", "gate_base", "gate_kept"))
            order_i, order = sb("order_i", [P, 2, EXPERTS], I32), sb("order", [P, 2, EXPERTS])
            incl = ctx.enter_context(nc.psum_tensor("gate_incl", [P, GRAPHS, EXPERTS], F32))
            total = ctx.enter_context(nc.psum_tensor("gate_total", [P, GRAPHS, EXPERTS], F32))
            made, exped, ranked, ordered = sem("route_step"), sem("route_exp"), sem("route_ranked"), sem("route_order")
            block = ctx.enter_context(nc.Block())

            def wide(ap):
                return ap.unsqueeze(2).to_broadcast([P, GRAPHS, EXPERTS])

            def each(ap):
                return ap.unsqueeze(1).to_broadcast([P, GRAPHS, EXPERTS])

            @block.gpsimd
            def _(pool):
                pool.iota(order_i[:, 0, :], [[-1, EXPERTS]], base=EXPERTS, channel_multiplier=0).then_inc(ordered, 1)
                pool.iota(order_i[:, 1, :], [[CAPACITY, EXPERTS]], base=0, channel_multiplier=0).then_inc(ordered, 1)

            @block.vector
            def _(dve):
                n = [0]

                def link(ins):
                    ins.then_inc(made, 1)
                    n[0] += 1
                    dve.wait_ge(made, n[0])

                dve.wait_ge(ordered, 2)
                link(dve.tensor_copy(order[:, :, :], order_i[:, :, :]))
                L = logits[:, :, :]
                link(dve.tensor_tensor(L, L, each(gate_b[:, :]), ALU.add))
                link(dve.tensor_reduce(best[:, :], L, AX_X, ALU.max))
                link(dve.tensor_tensor(work[:, :, :], L, wide(best[:, :]), ALU.subtract))
                link(dve.tensor_tensor(chosen[:, :, :], L, wide(best[:, :]), ALU.is_equal))
                link(dve.tensor_tensor(chosen[:, :, :], chosen[:, :, :], each(order[:, 0, :]), ALU.mult))
                link(dve.tensor_reduce(pos[:, :], chosen[:, :, :], AX_X, ALU.max))
                link(dve.tensor_tensor(chosen[:, :, :], chosen[:, :, :], wide(pos[:, :]), ALU.is_equal))
                dve.wait_ge(exped, 1)
                link(dve.tensor_reduce(pos[:, :], grown[:, :, :], AX_X, ALU.add))
                link(dve.reciprocal(prob[:, :], pos[:, :]))
                link(dve.tensor_tensor(work[:, :, :], chosen[:, :, :], each(order[:, 1, :]), ALU.mult))
                link(dve.tensor_reduce(base[:, :], work[:, :, :], AX_X, ALU.add))
                dve.wait_ge(ranked, 4)
                link(dve.tensor_copy(tot[:, :, :], total[:, :, :]))
                for e in range(EXPERTS):
                    link(dve.tensor_tensor_scan(scan[:, :, e], ones[:, :], tot[:, :, e], 0.0, ALU.mult, ALU.add))
                link(dve.tensor_tensor(scan[:, :, :], scan[:, :, :], tot[:, :, :], ALU.subtract))
                link(dve.tensor_tensor(scan[:, :, :], incl[:, :, :], scan[:, :, :], ALU.add))
                link(dve.tensor_tensor(scan[:, :, :], scan[:, :, :], chosen[:, :, :], ALU.mult))
                link(dve.tensor_reduce(pos[:, :], scan[:, :, :], AX_X, ALU.add))
                link(dve.tensor_scalar(pos[:, :], pos[:, :], -1.0, None, ALU.add))
                link(dve.tensor_scalar(kept[:, :], pos[:, :], float(CAPACITY), None, ALU.is_lt))
                link(dve.scalar_tensor_tensor(base[:, :], pos[:, :], float(CAPACITY - 1), base[:, :], ALU.min, ALU.add))
                link(dve.tensor_copy(fetch[:, :], base[:, :]))
                link(dve.tensor_tensor(weight[:, :], prob[:, :], kept[:, :], ALU.mult))
                link(dve.tensor_scalar(kept[:, :], kept[:, :], -float(1 << 20), float(1 << 20), ALU.mult, ALU.add))
                link(dve.tensor_tensor(base[:, :], base[:, :], kept[:, :], ALU.add))
                link(dve.tensor_copy(send[:, :], base[:, :]))

            @block.scalar
            def _(act):
                act.wait_ge(made, 4)
                act.activation(grown[:, :, :], work[:, :, :], ACT.Exp).then_inc(exped, 1)

            @block.tensor
            def _(pe):
                pe.wait_ge(made, 8)
                half = GRAPHS // 2
                for lhs, to in ((upto, incl), (ones, total)):
                    for h in (0, 1):
                        cols = slice(h * half, (h + 1) * half)
                        pe.matmul(to[:, cols, :], lhs[:, :], chosen[:, cols, :], start=True, stop=True).then_inc(ranked, 1)

        with ExitStack() as ctx:
            feat = ctx.enter_context(nc.sbuf_tensor("sent_feat", [P, 2, PER, FEAT], F32))
            ids = ctx.enter_context(nc.sbuf_tensor("sent_ids", [P, 2, PER], U32))
            normed, ids_s, paced = sem("sent_normed"), sem("sent_ids_s"), sem("sent_paced")
            sent = (sem("sent_even"), sem("sent_odd"))
            block = ctx.enter_context(nc.Block())

            @block.scalar
            def _(act):
                def step(n, u):
                    if not isinstance(n, int) or n >= 2:
                        act.wait_ge(sent[u % 2], (n - u % 2) * (8 * PER))
                    normalise(act, feat[:, u % 2, :, :], x, rstd, shift, n).then_inc(normed, 1)

                pipeline(act, 0, step)

            @block.gpsimd
            def _(pool):
                def step(n, u):
                    if not isinstance(n, int) or n >= 2:
                        pool.wait_ge(sent[u % 2], (n - u % 2) * (8 * PER))
                    pool.tensor_copy(ids[:, u % 2, :], send[:, bass.ds(n * PER, PER)]).then_inc(ids_s, 1)
                    pool.wait_ge(ids_s, n + 1)
                    pool.wait_ge(normed, n + 1)
                    pool.sem_inc(paced, 1)
                    for v in range(PER):
                        pool.indirect_dma_start(slots_dram, bass.IndirectOffsetOnAxis(ids[:, u % 2, v:v + 1], 0),
                                                feat[:, u % 2, v, :], None, bounds_check=EXPERTS * CAPACITY - 1,
                                                oob_is_err=False).then_inc(sent[u % 2], 16)

                pipeline(pool, 0, step)
                for s in sent:
                    pool.wait_ge(s, 8 * PER * GROUPS)

        with ExitStack() as ctx:
            def sb(name, shape, dt=F32):
                return ctx.enter_context(nc.sbuf_tensor(name, shape, dt))

            w1, w2 = sb("w1", [P, 2, HIDDEN]), sb("w2", [P, 2, HC, FEAT])
            b1, b2 = sb("b1", [P, 2, HC]), sb("b2", [P, 2, FEAT])
            rows, rowsT = sb("rows", [P, 2, PER, FEAT]), sb("rowsT", [P, 2, WIDE])
            hid, res = sb("hid", [P, 2, HC, WIDE]), sb("res", [P, 2, PER, FEAT])
            b_rowsT = ctx.enter_context(nc.psum_tensor("b_rowsT", [P, PER, P], F32))
            b_hid = ctx.enter_context(nc.psum_tensor("b_hid", [P, HC, WIDE], F32))
            b_res = ctx.enter_context(nc.psum_tensor("b_res", [P, 2, PER, P], F32))
            w_in = (sem("x0_w_even"), sem("x0_w_odd"))
            rows_in = (sem("x0_rows_even"), sem("x0_rows_odd"))
            turned, rowsT_s, hid_mm, hid_act, hid_dve, res_mm, res_s = (sem(f"x0_{n}") for n in (
                "turned", "rowsT", "hid_mm", "hid_act", "hid_dve", "res_mm", "res"))
            res_out = (sem("x0_out_even"), sem("x0_out_odd"))
            block = ctx.enter_context(nc.Block())
            STEPS = EXPERTS * SLOT_GROUPS
            TURN = 2 * SLOT_GROUPS
            slots_v = slots_dram.rearrange("(k p r) d -> k p r d", p=P, r=PER)
            rows_v = rows_dram.rearrange("(k p r) d -> k p r d", p=P, r=PER)

            def turns(engine, first, step):
                for n in range(first, TURN):
                    step(n, n % TURN)
                with engine.Fori(1, STEPS // TURN - 1) as turn:
                    for u in range(TURN):
                        step(turn * TURN + u, u)
                for n in range(STEPS - TURN, STEPS):
                    step(n, n % TURN)

            def there(n):
                return not isinstance(n, int) or 0 <= n < STEPS

            @block.sync
            def _(sp):
                def load(n, u):
                    ge(sp, turned, n - 1)
                    sp.dma_start(rows[:, u % 2, :, :], slots_v[bass.ds(n, 1)].rearrange("o p r d -> p (o r) d")).then_inc(rows_in[u % 2], 16)

                def store(n, u):
                    sp.wait_ge(res_s, n + 1)
                    sp.dma_start(rows_v[bass.ds(n, 1)].rearrange("o p r d -> p (o r) d"), res[:, u % 2, :, :]).then_inc(res_out[u % 2], 16)

                def step(n, u):
                    if there(n + 2):
                        load(n + 2, (u + 2) % TURN)
                    if there(n):
                        store(n, u)

                turns(sp, -2, step)
                for s in res_out:
                    sp.wait_ge(s, 8 * STEPS)

            @block.gpsimd
            def _(pool):
                def load(e, h):
                    for to, of in ((w1[:, h, :], a["w1"]), (w2[:, h, :, :], a["w2"]), (b1[:, h, :], a["b1T"])):
                        pool.dma_start(to, of[e]).then_inc(w_in[h], 16)
                    pool.dma_start(b2[:, h, :], bass.AP(a["b2"].tensor, e * FEAT, [[0, P], [1, FEAT]])).then_inc(w_in[h], 16)

                for e in range(EXPERTS):
                    if e >= 2:
                        pool.wait_ge(res_s, (e - 1) * SLOT_GROUPS)
                    load(e, e % 2)

            @block.tensor
            def _(pe):
                def step(n, u, pair):
                    m = n + 2
                    if there(m):
                        pe.wait_ge(rows_in[u % 2], (m - u % 2) * 8 + 16)
                        ge(pe, rowsT_s, m)
                        for r in range(PER):
                            last = pe.transpose(b_rowsT[:, r, :], rows[:, u % 2, r, :], ident)
                        last.then_inc(turned, 1)
                    m, mu = n + 1, (u + 1) % TURN
                    if there(m):
                        h = mu // SLOT_GROUPS
                        pe.wait_ge(w_in[h], (pair + (1 if u == TURN - 1 else 0)) * 64 + 64)
                        pe.wait_ge(rowsT_s, m + 1)
                        ge(pe, hid_act, m)
                        ge(pe, hid_dve, m)
                        for c in range(HC):
                            last = pe.matmul(b_hid[:, c, :], w1[:, h, c * P:(c + 1) * P], rowsT[:, (u + 1) % 2, :], start=True, stop=True)
                        last.then_inc(hid_mm, 1)
                    if there(n):
                        pe.wait_ge(hid_act, n + 1)
                        pe.wait_ge(hid_dve, n + 1)
                        ge(pe, res_s, n - 1)
                        h = u // SLOT_GROUPS
                        for r in range(PER):
                            for c in range(HC):
                                last = pe.matmul(b_res[:, u % 2, r, :], hid[:, u % 2, c, r * P:(r + 1) * P], w2[:, h, c, :],
                                                 start=(c == 0), stop=(c == HC - 1))
                        last.then_inc(res_mm, 1)

                for n in range(-2, TURN):
                    step(n, n % TURN, n // TURN)
                with pe.Fori(1, STEPS // TURN - 1) as turn:
                    for u in range(TURN):
                        step(turn * TURN + u, u, turn)
                for n in range(STEPS - TURN, STEPS):
                    step(n, n % TURN, n // TURN)

            @block.scalar
            def _(act):
                def step(n, u):
                    m = n + 1
                    if there(m):
                        act.wait_ge(turned, m + 1)
                        ge(act, hid_mm, m - 1)
                        act.activation(rowsT[:, (u + 1) % 2, :], b_rowsT[:, :, :].rearrange("p r i -> p (r i)"), ACT.Copy).then_inc(rowsT_s, 1)
                    if there(n):
                        act.wait_ge(hid_mm, n + 1)
                        ge(act, res_mm, n - 1)
                        h = u // SLOT_GROUPS
                        for c in (0, 1):
                            last = act.activation(hid[:, u % 2, c, :], b_hid[:, c, :], ACT.Relu, bias=b1[:, h, c:c + 1])
                        last.then_inc(hid_act, 1)

                turns(act, -1, step)

            @block.vector
            def _(dve):
                def step(n, u):
                    m, mu = n + 1, (u + 1) % TURN
                    if there(m):
                        dve.wait_ge(hid_mm, m + 1)
                        ge(dve, res_mm, m - 1)
                        h = mu // SLOT_GROUPS
                        for c in (2, 3):
                            last = dve.tensor_scalar(hid[:, (u + 1) % 2, c, :], b_hid[:, c, :], b1[:, h, c:c + 1], 0.0, ALU.add, ALU.max)
                        last.then_inc(hid_dve, 1)
                    if there(n):
                        h = u // SLOT_GROUPS
                        dve.wait_ge(res_mm, n + 1)
                        if not isinstance(n, int) or n >= 2:
                            dve.wait_ge(res_out[u % 2], (n - u % 2) * 8)
                        dve.tensor_tensor(res[:, u % 2, :, :], b_res[:, u % 2, :, :],
                                          b2[:, h, :].unsqueeze(1).to_broadcast([P, PER, FEAT]), ALU.add).then_inc(res_s, 1)

                turns(dve, -1, step)

        with ExitStack() as ctx:
            got = ctx.enter_context(nc.sbuf_tensor("got", [P, 2, PER, FEAT], F32))
            ids = ctx.enter_context(nc.sbuf_tensor("got_ids", [P, 2, PER], U32))
            ids_s, paced, added = sem("got_ids_s"), sem("got_paced"), sem("got_added")
            came = (sem("got_even"), sem("got_odd"))
            block = ctx.enter_context(nc.Block())

            @block.gpsimd
            def _(pool):
                def step(n, u):
                    if not isinstance(n, int) or n >= 2:
                        pool.wait_ge(added, n - 1)
                    pool.tensor_copy(ids[:, u % 2, :], fetch[:, bass.ds(n * PER, PER)]).then_inc(ids_s, 1)
                    pool.wait_ge(ids_s, n + 1)
                    pool.sem_inc(paced, 1)
                    for v in range(PER):
                        pool.indirect_dma_start(got[:, u % 2, v, :], None, rows_dram,
                                                bass.IndirectOffsetOnAxis(ids[:, u % 2, v:v + 1], 0)).then_inc(came[u % 2], 16)

                pipeline(pool, 0, step)

            @block.vector
            def _(dve):
                def step(n, u):
                    dve.wait_ge(came[u % 2], (n - u % 2) * (8 * PER) + 16 * PER)
                    for v in range(PER):
                        q = n * PER + v
                        mine = x[:, bass.ds(q, 1), :].rearrange("p o f -> p (o f)")
                        last = dve.scalar_tensor_tensor(mine, got[:, u % 2, v, :], weight[:, bass.ds(q, 1)], mine, ALU.mult, ALU.add)
                    last.then_inc(added, 1)
                    dve.wait_ge(added, n + 1)
                    for v in range(PER):
                        q = n * PER + v
                        dve.bn_stats(stats[:, bass.ds(q, 1), :].rearrange("p o s -> p (o s)"),
                                     x[:, bass.ds(q, 1), :].rearrange("p o f -> p (o f)"))

                pipeline(dve, 0, step)


def prepare_nodes(nc, sem, tab, table_dram, node, last_node, ident, ones, wanted, found, counted, first_edge, degree, clamped, loops):
    with ExitStack() as ctx:
        def sb(name, shape, dt=F32):
            return ctx.enter_context(nc.sbuf_tensor(name, shape, dt))

        beside, at_end, total_at_end = sb("beside", [P, P]), sb("at_end", [P, P]), sb("total_at_end", [P, P])
        ends, most, flag = sb("ends", [P, 2]), sb("most", [P, 1]), sb("most_row", [P, 4])
        ps = ctx.enter_context(nc.psum_tensor("ends_ps", [P, 512], F32))
        wrote, read, drawn, made, shifted, turned = (sem(f"nodes_{n}") for n in ("wrote", "read", "drawn", "made", "shifted", "turned"))
        block = ctx.enter_context(nc.Block())

        @block.sync
        def _(sp):
            sp.dma_start(table_dram.rearrange("(b i) c -> i b c", i=NODES), tab[:, :, :]).then_inc(wrote, 16)
            sp.wait_ge(wrote, 16)
            sp.dma_start(node[:, :, :], table_dram.rearrange("(b i) c -> b i c", i=NODES)).then_inc(read, 16)
            sp.dma_start(last_node[:, :], bass.AP(table_dram.tensor, (TOKENS - 1) * TAB, [[0, P], [1, TAB]])).then_inc(read, 16)
            sp.wait_ge(read, 32)

        @block.gpsimd
        def _(pool):
            pool.affine_select(out=total_at_end[:, :], in_=ones[:, :], compare_op=ALU.is_ge, fill=0.0, base=-(P - 1),
                               pattern=[[1, P]], channel_multiplier=0).then_inc(drawn, 1)
            pool.memset(beside[:, :], 0.0).then_inc(drawn, 1)
            pool.wait_ge(drawn, 2)
            pool.affine_select(out=beside[:, :], in_=beside[:, :], compare_op=ALU.not_equal, fill=1.0, base=-1,
                               pattern=[[-1, P]], channel_multiplier=1).then_inc(drawn, 1)
            pool.affine_select(out=at_end[:, :], in_=total_at_end[:, :], compare_op=ALU.is_ge, fill=0.0, base=0,
                               pattern=[[0, P]], channel_multiplier=-1).then_inc(drawn, 1)

        @block.tensor
        def _(pe):
            pe.wait_ge(drawn, 4)
            pe.matmul(ps[:, 0:1], beside[:, :], found[:, 0, 0:1], start=True, stop=False)
            pe.matmul(ps[:, 0:1], at_end[:, :], found[:, 0, NODES:NODES + 1], start=False, stop=True)
            pe.matmul(ps[:, 1:2], beside[:, :], found[:, 0, NODES:NODES + 1], start=True, stop=False)
            pe.matmul(ps[:, 1:2], total_at_end[:, :], counted, start=False, stop=True).then_inc(shifted, 1)
            pe.wait_ge(made, 6)
            pe.transpose(ps[:, 128:256], most[:, :].to_broadcast([P, P]), ident).then_inc(turned, 1)

        @block.vector
        def _(dve):
            n = [0]

            def link(ins):
                ins.then_inc(made, 1)
                n[0] += 1
                dve.wait_ge(made, n[0])

            dve.wait_ge(shifted, 1)
            link(dve.tensor_copy(ends[:, :], ps[:, 0:2]))
            for c, to in ((0, degree), (1, clamped)):
                s = found[:, 0, c * NODES:(c + 1) * NODES]
                link(dve.tensor_tensor(to[:, 0:NODES - 1], s[:, 1:NODES], s[:, 0:NODES - 1], ALU.subtract))
                link(dve.tensor_tensor(to[:, NODES - 1:NODES], ends[:, c:c + 1], s[:, NODES - 1:NODES], ALU.subtract))
            link(dve.tensor_reduce(most[:, :], degree[:, :], AX_X, ALU.max))
            link(dve.tensor_copy(first_edge[:, :], found[:, 0, 0:NODES]))
            dve.wait_ge(turned, 1)
            link(dve.tensor_reduce(flag[:, 0:1], ps[:, 128:256], AX_X, ALU.max))
            link(dve.tensor_scalar(flag[:, 0:1], flag[:, 0:1], 1.0, None, ALU.max))
            link(dve.tensor_scalar(flag[:, 1:2], found[:, 0, NODES:NODES + 1], float(WINDOW + EDGE_STEP), None, ALU.add))
            link(dve.tensor_copy(loops[:, 0:2], flag[:, 0:2]))
            link(dve.tensor_scalar(loops[:, 1:2], loops[:, 1:2], EDGE_STEP.bit_length() - 1, None, ALU.logical_shift_right))


def gather_edges_and_experts1(nc, sem, a, x, rstd, shift, source_ids, table_dram, edges_dram, results_dram, loops, ident):
    E = TOP_EXPERTS
    with ExitStack() as ctx:
        def sb(name, shape, dt=F32):
            return ctx.enter_context(nc.sbuf_tensor(name, shape, dt))

        ids, rows = sb("edge_ids", [P, 2, EDGE_TILES], U32), sb("edge_rows", [P, 2, EDGE_TILES, ROW])
        ids_s, paced, freed = sem("edge_ids_s"), sem("edge_paced"), sem("edge_freed")
        came = (sem("edge_rows_even"), sem("edge_rows_odd"))
        gone = (sem("edge_out_even"), sem("edge_out_odd"))
        out_v = edges_dram.rearrange("(s c q) w -> s q c w", c=EDGE_TILES, q=P)
        w1, b1 = sb("x1_w1", [P, E, HIDDEN1]), sb("x1_b1", [P, E * HC1])
        w2, b2 = sb("x1_w2", [P, E * HC1, FEAT]), sb("x1_b2", [P, E, FEAT])
        feat, featT = sb("x1_feat", [P, 2, PER, FEAT]), sb("x1_featT", [P, 2, WIDE])
        hid, res = sb("x1_hid", [P, 2, HC1, WIDE]), sb("x1_res", [P, 2, PER, FEAT])
        b_featT = ctx.enter_context(nc.psum_tensor("x1_b_featT", [P, PER, P], F32))
        b_hid = ctx.enter_context(nc.psum_tensor("x1_b_hid", [P, 2, HC1, WIDE], F32))
        b_res = ctx.enter_context(nc.psum_tensor("x1_b_res", [P, 2, PER, P], F32))
        loaded, normed, turned, featT_s, hid_mm, hid_s, res_mm, res_s = (sem(f"x1_{n}") for n in (
            "loaded", "normed", "turned", "featT", "hid_mm", "hid", "res_mm", "res"))
        stored = (sem("x1_stored_even"), sem("x1_stored_odd"))
        block = ctx.enter_context(nc.Block())

        def turns(engine):
            return (engine.value_load(loops[0:1, 1:2], min_val=1, max_val=EDGES // EDGE_STEP + 1) + 1) // 2

        @block.gpsimd
        def _(pool):
            with pool.Fori(0, turns(pool)) as turn:
                for u in (0, 1):
                    n = turn * 2 + u
                    pool.wait_ge(freed, n + 1)
                    pool.tensor_copy(ids[:, u, :], source_ids[:, bass.ds(n * EDGE_TILES, EDGE_TILES)]).then_inc(ids_s, 1)
                    pool.wait_ge(ids_s, n + 1)
                    pool.sem_inc(paced, 1)
                    for c in range(EDGE_TILES):
                        pool.indirect_dma_start(rows[:, u, c, :], None, table_dram,
                                                bass.IndirectOffsetOnAxis(ids[:, u, c:c + 1], 0)).then_inc(came[u], 16)

        @block.sync
        def _(sp):
            for to, of in ((w1[:, :, :], a["w1b"]), (b1[:, :], a["b1b"]), (w2[:, :, :], a["w2b"]),
                           (b2[:, :, :].rearrange("p e d -> p (e d)"), across(a["b2b"], E * FEAT))):
                sp.dma_start(to, of).then_inc(loaded, 16)
            sp.sem_inc(freed, 2)
            with sp.Fori(0, turns(sp)) as turn:
                for u in (0, 1):
                    n = turn * 2 + u
                    sp.wait_ge(came[u], turn * (16 * EDGE_TILES) + 16 * EDGE_TILES)
                    sp.dma_start(out_v[bass.ds(n, 1)].rearrange("o q c w -> q (o c) w"), rows[:, u, :, :]).then_inc(gone[u], 16)
                    sp.wait_ge(gone[u], turn * 16 + 16)
                    sp.sem_inc(freed, 1)

        @block.scalar
        def _(act):
            def store(n, e):
                act.wait_ge(res_s, n * E + e + 1)
                at = n * E + e
                act.dma_start(results_dram[bass.ds(at, 1)].rearrange("o p d -> p (o d)"),
                              res[:, e % 2, :, :].rearrange("p v d -> p (v d)")).then_inc(stored[e % 2], 16)

            def step(n, u):
                if live(n + 1):
                    m = n + 1
                    act.wait_ge(turned, m + 1)
                    ge(act, hid_mm, (m - 1) * E)
                    act.activation(featT[:, (u + 1) % 2, :], b_featT[:, :, :].rearrange("p v i -> p (v i)"), ACT.Copy).then_inc(featT_s, 1)
                if live(n):
                    for e in range(E):
                        act.wait_ge(hid_mm, n * E + e + 1)
                        ge(act, res_mm, n * E + e - 1)
                        for c in range(HC1):
                            last = act.activation(hid[:, e % 2, c, :], b_hid[:, e % 2, c, :], ACT.Gelu, bias=b1[:, e * HC1 + c:e * HC1 + c + 1])
                        last.then_inc(hid_s, 1)
                        if e >= 2:
                            store(n, e - 2)
                        elif live(n - 1):
                            store(n - 1, e + E - 2)
                if live(n + 2):
                    ge(act, turned, n + 1)
                    normalise(act, feat[:, u % 2, :, :], x, rstd, shift, n + 2).then_inc(normed, 1)

            act.wait_ge(loaded, 64)
            pipeline(act, -2, step)
            for e in (E - 2, E - 1):
                store(GROUPS - 1, e)
            for s in stored:
                act.wait_ge(s, 8 * E * GROUPS)

        @block.tensor
        def _(pe):
            def hidden(n, u, e):
                pe.wait_ge(featT_s, n + 1)
                ge(pe, hid_s, n * E + e - 1)
                for c in range(HC1):
                    last = pe.matmul(b_hid[:, e % 2, c, :], w1[:, e, c * P:(c + 1) * P], featT[:, u % 2, :], start=True, stop=True)
                last.then_inc(hid_mm, 1)

            def result(n, u, e):
                ge(pe, res_s, n * E + e - 1)
                pe.wait_ge(hid_s, n * E + e + 1)
                for v in range(PER):
                    cols = slice(v * P, (v + 1) * P)
                    for c in range(HC1):
                        last = pe.matmul(b_res[:, e % 2, v, :], hid[:, e % 2, c, cols], w2[:, e * HC1 + c, :], start=(c == 0), stop=(c == HC1 - 1))
                last.then_inc(res_mm, 1)

            def step(n, u):
                if live(n + 1):
                    m = n + 1
                    pe.wait_ge(normed, m + 1)
                    ge(pe, featT_s, m)
                    for v in range(PER):
                        last = pe.transpose(b_featT[:, v, :], feat[:, (u + 1) % 2, v, :], ident)
                    last.then_inc(turned, 1)
                if live(n):
                    hidden(n, u, 0)
                    for e in range(1, E):
                        hidden(n, u, e)
                        result(n, u, e - 1)
                    result(n, u, E - 1)

            pe.wait_ge(loaded, 64)
            pipeline(pe, -1, step)

        @block.vector
        def _(dve):
            def step(n, u):
                for e in range(E):
                    dve.wait_ge(res_mm, n * E + e + 1)
                    if e >= 2:
                        dve.wait_ge(stored[e % 2], n * (8 * E) + 16 * (e // 2))
                    elif not isinstance(n, int) or n > 0:
                        dve.wait_ge(stored[e % 2], n * (8 * E))
                    dve.tensor_tensor(res[:, e % 2, :, :], b_res[:, e % 2, :, :],
                                      b2[:, e, :].unsqueeze(1).to_broadcast([P, PER, FEAT]), ALU.add).then_inc(res_s, 1)

            dve.wait_ge(loaded, 64)
            pipeline(dve, 0, step)


def attend_edges(nc, sem, a, edges_dram, node, last_node, first_edge, degree, clamped, loops, gates, ident):
    HALL = NODES * HEADS
    with ExitStack() as ctx:
        def sb(name, shape, dt=F32):
            return ctx.enter_context(nc.sbuf_tensor(name, shape, dt))

        top, total = sb("top", [P, NODES, HEADS]), sb("total", [P, NODES, HEADS])
        acc = sb("acc", [P, NODES, GAT])
        self_w, clamp_w = sb("self_w", [P, NODES, HEADS]), sb("clamp_w", [P, NODES, HEADS])
        wide = sb("wide", [P, NODES, GAT])
        left = sb("left", [P, NODES])
        order_i, order = sb("window_order_i", [P, WINDOW], I32), sb("window_order", [P, WINDOW])
        made, exped, drawn = sem("attend_step"), sem("attend_exp"), sem("attend_drawn")

        def heads(ap):
            return ap.unsqueeze(2).to_broadcast([P, NODES, HEADS])

        with nc.Block() as block:
            @block.gpsimd
            def _(pool):
                pool.iota(order_i[:, :], [[1, WINDOW]], base=0, channel_multiplier=0).then_inc(drawn, 1)

            @block.vector
            def _(dve):
                n = [0]

                def link(ins):
                    ins.then_inc(made, 1)
                    n[0] += 1
                    dve.wait_ge(made, n[0])

                S, C = self_w[:, :, :], clamp_w[:, :, :]
                to = node[:, :, ROW:TAB]
                link(dve.tensor_tensor(S, node[:, :, GAT:ROW], to, ALU.add))
                link(dve.scalar_tensor_tensor(S, S, SLOPE, S, ALU.mult, ALU.max))
                link(dve.tensor_tensor(C, to, last_node[:, GAT:ROW].unsqueeze(1).to_broadcast([P, NODES, HEADS]), ALU.add))
                link(dve.scalar_tensor_tensor(C, C, SLOPE, C, ALU.mult, ALU.max))
                link(dve.tensor_scalar(left[:, :], clamped[:, :], 0.0, -BIG, ALU.is_equal, ALU.mult))
                link(dve.tensor_tensor(C, C, heads(left[:, :]), ALU.add))
                link(dve.tensor_tensor(top[:, :, :], S, C, ALU.max))
                link(dve.tensor_tensor(S, S, top[:, :, :], ALU.subtract))
                link(dve.tensor_tensor(C, C, top[:, :, :], ALU.subtract))
                dve.wait_ge(exped, 2)
                link(dve.tensor_tensor(C, C, heads(clamped[:, :]), ALU.mult))
                link(dve.tensor_tensor(total[:, :, :], S, C, ALU.add))
                rows_h = node[:, :, 0:GAT].rearrange("p n (h e) -> p n h e", h=HEADS)
                acc_h = acc[:, :, :].rearrange("p n (h e) -> p n h e", h=HEADS)
                wide_h = wide[:, :, :].rearrange("p n (h e) -> p n h e", h=HEADS)
                link(dve.tensor_tensor(acc_h, rows_h, S.unsqueeze(3).to_broadcast([P, NODES, HEADS, TOP_EXPERTS]), ALU.mult))
                last_h = last_node[:, 0:GAT].rearrange("p (h e) -> p h e", h=HEADS)
                link(dve.tensor_tensor(wide_h, last_h.unsqueeze(1).to_broadcast([P, NODES, HEADS, TOP_EXPERTS]),
                                       C.unsqueeze(3).to_broadcast([P, NODES, HEADS, TOP_EXPERTS]), ALU.mult))
                link(dve.tensor_tensor(acc[:, :, :], acc[:, :, :], wide[:, :, :], ALU.add))
                link(dve.tensor_copy(left[:, :], degree[:, :]))
                dve.wait_ge(drawn, 1)
                link(dve.tensor_copy(order[:, :], order_i[:, :]))

            @block.scalar
            def _(act):
                act.wait_ge(made, 9)
                act.activation(self_w[:, :, :], self_w[:, :, :], ACT.Exp).then_inc(exped, 1)
                act.activation(clamp_w[:, :, :], clamp_w[:, :, :], ACT.Exp).then_inc(exped, 1)

        with ExitStack() as inner:
            def sb(name, shape, dt=F32):
                return inner.enter_context(nc.sbuf_tensor(name, shape, dt))

            win = sb("win", [P, 2, PER, WINDOW * ROW])
            ids = sb("win_ids", [P, 2, PER], U32)
            sc, low = sb("win_score", [P, 2, PER, WINDOW, HEADS]), sb("win_low", [P, PER * WINDOW * HEADS])
            hide = sb("win_hide", [P, PER, WINDOW])
            newtop, fade = sb("win_top", [P, 2, PER, HEADS]), sb("win_fade", [P, 2, PER, HEADS])
            msg, got = sb("win_msg", [P, PER, WINDOW, GAT]), sb("win_got", [P, PER, GAT])
            sums, adv = sb("win_sums", [P, PER, HEADS]), sb("win_adv", [P, PER])
            ids_s, paced, exp_s, scored, used, chain, advanced = (sem(f"win_{n}") for n in ("ids_s", "paced", "exp", "scored", "used", "chain", "advanced"))
            came = (sem("win_even"), sem("win_odd"))
            block = inner.enter_context(nc.Block())
            FULL = [P, PER, WINDOW, HEADS]

            def rounds(engine):
                return (engine.value_load(loops[0:1, 0:1], min_val=1, max_val=EDGES) + (WINDOW - 1)) // WINDOW

            @block.gpsimd
            def _(pool):
                with pool.Fori(0, rounds(pool)) as r:
                    with pool.Fori(0, GROUPS // 2) as turn:
                        for u in (0, 1):
                            g = turn * 2 + u
                            n = r * GROUPS + g
                            pool.wait_ge(used, n + 1)
                            pool.tensor_copy(ids[:, u, :], first_edge[:, bass.ds(g * PER, PER)]).then_inc(ids_s, 1)
                            pool.wait_ge(ids_s, n + 1)
                            pool.sem_inc(paced, 1)
                            for v in range(PER):
                                pool.indirect_dma_start(win[:, u, v, :], None, edges_dram,
                                                        bass.IndirectOffsetOnAxis(ids[:, u, v:v + 1], 0)).then_inc(came[u], 16)

            @block.scalar
            def _(act):
                with act.Fori(0, rounds(act)) as r:
                    with act.Fori(0, GROUPS // 2) as turn:
                        for u in (0, 1):
                            n = r * GROUPS + turn * 2 + u
                            act.wait_ge(scored, n + 1)
                            act.activation(fade[:, u, :, :], fade[:, u, :, :], ACT.Exp).then_inc(exp_s, 1)
                            act.activation(sc[:, u, :, :, :], sc[:, u, :, :, :], ACT.Exp).then_inc(exp_s, 1)

            @block.vector
            def _(dve):
                def look(g, n, u, r):
                    at = n * 12
                    mine = bass.ds(g * PER, PER)
                    w = win[:, u, :, :].rearrange("p t (k c) -> p t k c", c=ROW)
                    s = sc[:, u, :, :, :]
                    flat = s.rearrange("p t k h -> p (t k h)")
                    dve.wait_ge(came[u], (n - u) * (8 * PER) + 16 * PER)
                    dve.tensor_tensor(s, w[:, :, :, GAT:ROW], node[:, mine, ROW:TAB].unsqueeze(2).to_broadcast(FULL), ALU.add).then_inc(chain, 1)
                    dve.tensor_tensor(hide[:, :, :], order[:, :].unsqueeze(1).to_broadcast([P, PER, WINDOW]),
                                      left[:, mine].unsqueeze(2).to_broadcast([P, PER, WINDOW]), ALU.is_ge).then_inc(chain, 1)
                    dve.wait_ge(chain, at + 2)
                    dve.tensor_scalar(hide[:, :, :], hide[:, :, :], -BIG, None, ALU.mult).then_inc(chain, 1)
                    dve.scalar_tensor_tensor(flat, flat, SLOPE, flat, ALU.mult, ALU.max).then_inc(chain, 1)
                    dve.wait_ge(chain, at + 4)
                    dve.tensor_tensor(s, s, hide[:, :, :].unsqueeze(3).to_broadcast(FULL), ALU.add).then_inc(chain, 1)
                    dve.wait_ge(chain, at + 5)
                    dve.tensor_reduce(newtop[:, u, :, :], s.rearrange("p t k h -> p t h k"), AX_X, ALU.max).then_inc(chain, 1)
                    dve.wait_ge(chain, at + 6)
                    dve.tensor_tensor(newtop[:, u, :, :], newtop[:, u, :, :], top[:, mine, :], ALU.max).then_inc(chain, 1)
                    dve.wait_ge(chain, at + 7)
                    dve.tensor_tensor(fade[:, u, :, :], top[:, mine, :], newtop[:, u, :, :], ALU.subtract).then_inc(chain, 1)
                    dve.tensor_tensor(s, s, newtop[:, u, :, :].unsqueeze(2).to_broadcast(FULL), ALU.subtract).then_inc(chain, 1)
                    dve.wait_ge(chain, at + 9)
                    dve.tensor_scalar(top[:, mine, :], newtop[:, u, :, :], 1.0, None, ALU.mult).then_inc(scored, 1)
                    dve.tensor_scalar(left[:, mine], left[:, mine], -float(WINDOW), None, ALU.add).then_inc(chain, 1)
                    dve.wait_ge(chain, at + 10)
                    dve.tensor_scalar(adv[:, :], left[:, mine], 0.0, float(WINDOW), ALU.is_gt, ALU.mult).then_inc(chain, 1)
                    dve.wait_ge(chain, at + 11)
                    dve.tensor_tensor(first_edge[:, mine], first_edge[:, mine], adv[:, :], ALU.add).then_inc(chain, 1)

                def gather(g, n, u):
                    at = n * 6
                    mine = bass.ds(g * PER, PER)
                    w = win[:, u, :, :].rearrange("p t (k c) -> p (t k) c", c=ROW)
                    s = sc[:, u, :, :, :]
                    dve.wait_ge(exp_s, n * 2 + 2)
                    dve.tensor_reduce(sums[:, :, :], s.rearrange("p t k h -> p t h k"), AX_X, ALU.add).then_inc(advanced, 1)
                    dve.tensor_tensor(total[:, mine, :], total[:, mine, :], fade[:, u, :, :], ALU.mult).then_inc(advanced, 1)
                    dve.tensor_tensor(msg[:, :, :, :].rearrange("p t k (h e) -> p (t k) h e", h=HEADS),
                                      w[:, :, 0:GAT].rearrange("p k (h e) -> p k h e", h=HEADS),
                                      s.rearrange("p t k h -> p (t k) h").unsqueeze(3).to_broadcast([P, PER * WINDOW, HEADS, TOP_EXPERTS]),
                                      ALU.mult).then_inc(used, 1)
                    a4 = acc[:, mine, :].rearrange("p t (h e) -> p t h e", h=HEADS)
                    dve.tensor_tensor(a4, a4, fade[:, u, :, :].unsqueeze(3).to_broadcast([P, PER, HEADS, TOP_EXPERTS]), ALU.mult).then_inc(advanced, 1)
                    dve.wait_ge(advanced, at + 3)
                    dve.tensor_tensor(total[:, mine, :], total[:, mine, :], sums[:, :, :], ALU.add).then_inc(advanced, 1)
                    dve.wait_ge(used, n + 3)
                    dve.tensor_reduce(got[:, :, :], msg[:, :, :, :].rearrange("p t k c -> p t c k"), AX_X, ALU.add).then_inc(advanced, 1)
                    dve.wait_ge(advanced, at + 5)
                    dve.tensor_tensor(acc[:, mine, :], acc[:, mine, :], got[:, :, :], ALU.add).then_inc(advanced, 1)

                dve.tensor_copy(adv[:, 0:1], left[:, 0:1]).then_inc(used, 2)
                with dve.Fori(0, rounds(dve)) as r:
                    with dve.Fori(0, GROUPS // 2) as turn:
                        g = turn * 2
                        n = r * GROUPS + g
                        look(g, n, 0, r)
                        look(g + 1, n + 1, 1, r)
                        gather(g, n, 0)
                        gather(g + 1, n + 1, 1)

        with ExitStack() as inner:
            def sb(name, shape, dt=F32):
                return inner.enter_context(nc.sbuf_tensor(name, shape, dt))

            gat_b, gamma, beta = sb("gat_b", [P, GAT]), sb("gat_gamma", [P, GAT]), sb("gat_beta", [P, GAT])
            mean, var, root = sb("gat_mean", [P, NODES]), sb("gat_var", [P, NODES]), sb("gat_root", [P, NODES])
            s4, one, two, val = (sb(n, [P, NODES, TOP_EXPERTS]) for n in ("s4", "one", "two", "val"))
            first, second, w1, w2 = (sb(n, [P, NODES]) for n in ("first_best", "second_best", "first_w", "second_w"))
            pref_i, pref = sb("pref_i", [P, TOP_EXPERTS], I32), sb("pref", [P, TOP_EXPERTS])
            ps = inner.enter_context(nc.psum_tensor("gates_ps", [P, TOP_EXPERTS, P], F32))
            loaded, made, act_s, drawn, turned = (sem(f"top_{n}") for n in ("loaded", "made", "act", "drawn", "turned"))
            block = inner.enter_context(nc.Block())

            @block.sync
            def _(sp):
                for to, of in ((gat_b, "gat_b"), (gamma, "gamma"), (beta, "beta")):
                    sp.dma_start(to[:, :], across(a[of], GAT)).then_inc(loaded, 16)

            @block.gpsimd
            def _(pool):
                pool.iota(pref_i[:, :], [[-1, TOP_EXPERTS]], base=TOP_EXPERTS, channel_multiplier=0).then_inc(drawn, 1)

            marks = {}

            @block.vector
            def _(dve):
                n = [0]

                def link(ins, mark=None):
                    ins.then_inc(made, 1)
                    n[0] += 1
                    dve.wait_ge(made, n[0])
                    if mark:
                        marks[mark] = n[0]

                def nodes16(ap):
                    return ap.unsqueeze(2).to_broadcast([P, NODES, GAT])

                def each16(ap):
                    return ap.unsqueeze(1).to_broadcast([P, NODES, GAT])

                def nodes4(ap):
                    return ap.unsqueeze(2).to_broadcast([P, NODES, TOP_EXPERTS])

                A, B = acc[:, :, :], wide[:, :, :]
                link(dve.tensor_scalar(total[:, :, :], total[:, :, :], 1e-16, None, ALU.add))
                link(dve.reciprocal(total[:, :, :], total[:, :, :]))
                A4 = A.rearrange("p n (h e) -> p n h e", h=HEADS)
                link(dve.tensor_tensor(A4, A4, total[:, :, :].unsqueeze(3).to_broadcast([P, NODES, HEADS, TOP_EXPERTS]), ALU.mult))
                dve.wait_ge(loaded, 48)
                link(dve.tensor_tensor(A, A, each16(gat_b[:, :]), ALU.add))
                link(dve.tensor_reduce(mean[:, :], A, AX_X, ALU.add))
                link(dve.tensor_scalar(mean[:, :], mean[:, :], 1.0 / GAT, None, ALU.mult))
                link(dve.tensor_tensor(A, A, nodes16(mean[:, :]), ALU.subtract))
                link(dve.tensor_tensor(B, A, A, ALU.mult))
                link(dve.tensor_reduce(var[:, :], B, AX_X, ALU.add))
                link(dve.tensor_scalar(var[:, :], var[:, :], 1.0 / GAT, EPS, ALU.mult, ALU.add), "var")
                dve.wait_ge(act_s, 1)
                link(dve.reciprocal(var[:, :], root[:, :]))
                link(dve.tensor_tensor(A, A, nodes16(var[:, :]), ALU.mult))
                link(dve.tensor_tensor(A, A, each16(gamma[:, :]), ALU.mult))
                link(dve.tensor_tensor(A, A, each16(beta[:, :]), ALU.add))
                link(dve.tensor_reduce(s4[:, :, :], A.rearrange("p n (h e) -> p n e h", h=HEADS), AX_X, ALU.add))
                link(dve.tensor_scalar(s4[:, :, :], s4[:, :, :], 1.0 / HEADS, None, ALU.mult))
                dve.wait_ge(drawn, 1)
                link(dve.tensor_copy(pref[:, :], pref_i[:, :]))
                pref4 = pref[:, :].unsqueeze(1).to_broadcast([P, NODES, TOP_EXPERTS])
                for best, hot in ((first, one), (second, two)):
                    link(dve.tensor_reduce(best[:, :], s4[:, :, :], AX_X, ALU.max))
                    link(dve.tensor_tensor(val[:, :, :], s4[:, :, :], nodes4(best[:, :]), ALU.is_equal))
                    link(dve.tensor_tensor(val[:, :, :], val[:, :, :], pref4, ALU.mult))
                    link(dve.tensor_reduce(w1[:, :], val[:, :, :], AX_X, ALU.max))
                    link(dve.tensor_tensor(hot[:, :, :], val[:, :, :], nodes4(w1[:, :]), ALU.is_equal))
                    if hot is one:
                        link(dve.scalar_tensor_tensor(s4[:, :, :], one[:, :, :], -BIG, s4[:, :, :], ALU.mult, ALU.add))
                link(dve.tensor_tensor(w2[:, :], second[:, :], first[:, :], ALU.subtract), "gap")
                dve.wait_ge(act_s, 2)
                link(dve.tensor_scalar(w1[:, :], w2[:, :], 1.0, None, ALU.add))
                link(dve.reciprocal(w1[:, :], w1[:, :]))
                link(dve.tensor_tensor(w2[:, :], w2[:, :], w1[:, :], ALU.mult))
                link(dve.tensor_tensor(one[:, :, :], one[:, :, :], nodes4(w1[:, :]), ALU.mult))
                link(dve.tensor_tensor(two[:, :, :], two[:, :, :], nodes4(w2[:, :]), ALU.mult))
                link(dve.tensor_tensor(one[:, :, :], one[:, :, :], two[:, :, :], ALU.add), "gates")
                dve.wait_ge(turned, 1)
                link(dve.tensor_copy(gates[:, :, :].rearrange("i b e -> i e b"), ps[:, :, :]))

            @block.scalar
            def _(act):
                act.wait_ge(made, marks["var"])
                act.activation(root[:, :], var[:, :], ACT.Sqrt).then_inc(act_s, 1)
                act.wait_ge(made, marks["gap"])
                act.activation(w2[:, :], w2[:, :], ACT.Exp).then_inc(act_s, 1)

            @block.tensor
            def _(pe):
                pe.wait_ge(made, marks["gates"])
                for e in range(TOP_EXPERTS):
                    last = pe.transpose(ps[:, e, :], one[:, :, e], ident)
                last.then_inc(turned, 1)


def combine_experts1(nc, sem, x, gates, results_dram, out):
    E, AHEAD = TOP_EXPERTS, 4
    with ExitStack() as ctx:
        got = ctx.enter_context(nc.sbuf_tensor("x1_got", [P, AHEAD, E, PER, FEAT], F32))
        came = [sem(f"x1_came{k}") for k in range(AHEAD)]
        added, gone = sem("x1_added"), sem("x1_out")
        block = ctx.enter_context(nc.Block())
        results_v = results_dram.rearrange("(g e) p d -> g p e d", e=E)

        @block.sync
        def _(sp):
            def step(n, u):
                ge(sp, added, (n - AHEAD + 1) * E)
                sp.dma_start(got[:, u, :, :, :].rearrange("p e v d -> p e (v d)"),
                             results_v[bass.ds(n, 1)].rearrange("o p e d -> p (o e) d")).then_inc(came[u], 16)

            pipeline(sp, 0, step)

        @block.vector
        def _(dve):
            def step(n, u):
                dve.wait_ge(came[u], (n - u) * 4 + 16)
                for e in range(E):
                    ge(dve, added, n * E + e)
                    for v in range(PER):
                        q = n * PER + v
                        mine = x[:, bass.ds(q, 1), :].rearrange("p o f -> p (o f)")
                        last = dve.scalar_tensor_tensor(mine, got[:, u, e, v, :], gates[:, bass.ds(q, 1), e:e + 1].rearrange("p o e -> p (o e)"),
                                                        mine, ALU.mult, ALU.add)
                    last.then_inc(added, 1)

            pipeline(dve, 0, step)

        @block.scalar
        def _(act):
            def step(n, u):
                act.wait_ge(added, n * E + E)
                act.dma_start(out[:, bass.ds(n * PER, PER), :], x[:, bass.ds(n * PER, PER), :]).then_inc(gone, 16)

            pipeline(act, 0, step)
            act.wait_ge(gone, 16 * GROUPS)


def build(nc, a, out):
    keys_dram = nc.dram_tensor("keys", (EDGES // FAN, FAN), F32).ap()
    slots_dram = nc.dram_tensor("slots", (EXPERTS * CAPACITY, FEAT), F32).ap()
    rows_dram = nc.dram_tensor("slot_results", (EXPERTS * CAPACITY, FEAT), F32).ap()
    table_dram = nc.dram_tensor("node_table", (TOKENS, TAB), F32).ap()
    edges_dram = nc.dram_tensor("edge_table", (EDGES + 2 * EDGE_STEP, ROW), F32).ap()
    results_dram = nc.dram_tensor("expert_results", (GROUPS * TOP_EXPERTS, P, WIDE), F32).ap()
    coarse_dram = nc.dram_tensor("coarse", (P * COLS // FAN // FAN, FAN), F32).ap()
    with ExitStack() as top:
        in_use = []

        def sem(name):
            in_use.append(nc.alloc_semaphore(name))
            return in_use[-1]

        def renew_semaphores():
            nc.all_engine_barrier()
            nc.clear_and_free_semaphores(in_use)
            in_use.clear()
            nc.all_engine_barrier()

        def keep(name, shape, dt=F32):
            return top.enter_context(nc.sbuf_tensor(name, shape, dt))

        x = keep("x", [P, GRAPHS, FEAT])
        stats = keep("stats", [P, GRAPHS, 6])
        rstd = keep("rstd", [P, GRAPHS])
        shift = keep("shift", [P, GRAPHS])
        scratch = keep("scratch", [P, 3, P])
        ident = keep("ident", [P, P])
        ones = keep("ones", [P, P])
        upto = keep("upto", [P, P])
        row_id = keep("row_id", [P, 1], I32)
        source_ids = keep("source_ids", [P, COLS + 2 * EDGE_TILES], U32)
        wanted = keep("wanted", [P, SEARCHES])
        starts = keep("starts", [P, P])
        counted = keep("counted", [P, 1])
        row_ids = keep("row_ids", [P, SEARCHES], U32)
        counts = keep("counts", [P, SEARCHES])
        found = keep("found", [P, 2, SEARCHES])
        W = {n: keep(n, [P, k]) for n, k in (("bilinear", P), ("key_col", 1), ("query_row0", P), ("own", P), ("other0", P),
                                             ("query_row1", P), ("key_row1", P), ("other1", P), ("bias1", P))}

        with ExitStack() as ctx:
            def sb(name, shape, dt=F32):
                return ctx.enter_context(nc.sbuf_tensor(name, shape, dt))

            w0T, a12, cols0, w1, cols1 = sb("w0T", [P, P]), sb("a12", [P, P]), sb("cols0", [P, 2]), sb("w1g", [P, P]), sb("cols1", [P, 2])
            m1 = sb("m1", [P, P])
            vec = sb("vec", [P, 4])
            ps = ctx.enter_context(nc.psum_tensor("setup_ps", [P, 2, 512], F32))
            loaded, drawn, prod, made = sem("loaded"), sem("drawn"), sem("setup_product"), sem("setup_step")
            block = ctx.enter_context(nc.Block())

            @block.sync
            def _(sp):
                for to, of in ((w0T, a["gnn0_wT"]), (a12, a["gnn0_a12"]), (cols0, a["gnn0_a"]), (w1, a["gnn1_w"]), (cols1, a["gnn1_aT"]),
                               (W["own"], a["gnn0_w1"]), (W["other0"], a["gnn0_w2"]), (W["other1"], a["gnn1_wT"]), (W["bias1"], across(a["gnn1_bias"], P))):
                    sp.dma_start(to[:, :], of).then_inc(loaded, 16)

            @block.gpsimd
            def _(pool):
                pool.memset(ident[:, :], 0.0).then_inc(drawn, 1)
                pool.memset(ones[:, :], 1.0).then_inc(drawn, 1)
                pool.memset(source_ids[:, COLS:], 0).then_inc(drawn, 1)
                pool.iota(row_id[:, :], [[0, 1]], base=0, channel_multiplier=1).then_inc(drawn, 1)
                for c, base in enumerate((KEY_INSIDE, KEY_CLAMPED)):
                    pool.iota(wanted[:, c * NODES:(c + 1) * NODES].bitcast(I32), [[1 << LOG_NODES, NODES]], base=base,
                              channel_multiplier=NODES << LOG_NODES).then_inc(drawn, 1)
                pool.wait_ge(drawn, 6)
                pool.affine_select(out=ident[:, :], in_=ident[:, :], compare_op=ALU.not_equal, fill=1.0, base=0,
                                   pattern=[[-1, P]], channel_multiplier=1).then_inc(drawn, 1)
                pool.affine_select(out=upto[:, :], in_=ones[:, :], compare_op=ALU.is_ge, fill=0.0, base=0,
                                   pattern=[[1, P]], channel_multiplier=-1).then_inc(drawn, 1)
                pool.wait_ge(drawn, 8)

            @block.tensor
            def _(pe):
                pe.wait_ge(loaded, 144)
                pe.matmul(ps[:, 0, 0:P], a12[:, :], w0T[:, :], start=True, stop=True).then_inc(prod, 1)
                pe.matmul(ps[:, 0, 128:130], w0T[:, :], cols0[:, :], start=True, stop=True).then_inc(prod, 1)
                pe.matmul(ps[:, 0, 130:132], w1[:, :], cols1[:, :], start=True, stop=True).then_inc(prod, 1)
                pe.wait_ge(made, 1)
                pe.matmul(ps[:, 1, 0:P], m1[:, :], w0T[:, :], start=True, stop=True).then_inc(prod, 1)

            @block.vector
            def _(dve):
                dve.wait_ge(prod, 3)
                dve.tensor_copy(m1[:, :], ps[:, 0, 0:P]).then_inc(made, 1)
                dve.tensor_copy(vec[:, :], ps[:, 0, 128:132]).then_inc(made, 1)
                dve.wait_ge(made, 2)
                dve.tensor_copy(W["key_col"][:, :], vec[:, 0:1])
                dve.tensor_copy(W["query_row0"][:, :], vec[:, 1:2].to_broadcast([P, P]))
                dve.tensor_copy(W["query_row1"][:, :], vec[:, 2:3].to_broadcast([P, P]))
                dve.tensor_copy(W["key_row1"][:, :], vec[:, 3:4].to_broadcast([P, P]))
                dve.wait_ge(prod, 4)
                dve.tensor_copy(W["bilinear"][:, :], ps[:, 1, 0:P])

        masked_ctx = top.enter_context(ExitStack())
        masked = masked_ctx.enter_context(nc.sbuf_tensor("masked", [P, GRAPHS, NODES], BF16))
        sort_edges(nc, sem, a["edges"], a["x"], a["adj"], x, stats, masked, keys_dram, coarse_dram, starts, counted[:, :], source_ids, ident[:, :], row_id[:, :],
                   (slots_dram, edges_dram))

        def descend(level, base_in, base_out):
            made = sem(f"descend_{level}")
            with ExitStack() as ctx:
                lower = ctx.enter_context(nc.sbuf_tensor(f"lower_{level}", [P, SEARCHES], F32))
                tmp = ctx.enter_context(nc.sbuf_tensor(f"firsts_before_{level}", [P, 64, P], BF16))
                block = ctx.enter_context(nc.Block())

                @block.vector
                def _(dve):
                    n = [0]

                    def link(ins):
                        ins.then_inc(made, 1)
                        n[0] += 1
                        dve.wait_ge(made, n[0])

                    if level == 1:
                        for c in range(0, SEARCHES, 64):
                            link(dve.tensor_tensor(tmp[:, :, :], starts[:, :].unsqueeze(1).to_broadcast([P, 64, P]),
                                                   wanted[:, c:c + 64].unsqueeze(2).to_broadcast([P, 64, P]), ALU.is_lt))
                            link(dve.tensor_reduce(counts[:, c:c + 64], tmp[:, :, :], AX_X, ALU.add))
                    if level < 3:
                        link(dve.tensor_scalar(lower[:, :], counts[:, :], -1.0, 0.0, ALU.add, ALU.max))
                    else:
                        link(dve.tensor_copy(lower[:, :], counts[:, :]))
                    if level > 1:
                        link(dve.scalar_tensor_tensor(base_out, base_in, float(FAN), lower[:, :], ALU.mult, ALU.add))
                    else:
                        link(dve.tensor_copy(base_out, lower[:, :]))
                    if level < 3:
                        link(dve.tensor_copy(row_ids[:, :], base_out))

        descend(1, None, found[:, 0, :])
        finish_norm(nc, sem, stats, scratch, rstd, shift, "gnn0")
        graph_attention(nc, sem, 0, x, masked, stats, rstd, shift, ident[:, :],
                        {"bilinear": W["bilinear"][:, :], "key_side": W["key_col"][:, :], "query_side": W["query_row0"][:, :],
                         "own": W["own"][:, :], "other": W["other0"][:, :]},
                        (coarse_dram, row_ids, wanted, counts))
        descend(2, found[:, 0, :], found[:, 1, :])
        renew_semaphores()
        finish_norm(nc, sem, stats, scratch, rstd, shift, "x0")
        experts0(nc, sem, a, x, stats, rstd, shift, ident[:, :], ones, upto, slots_dram, rows_dram)
        renew_semaphores()
        finish_norm(nc, sem, stats, scratch, rstd, shift, "gnn1")
        graph_attention(nc, sem, 1, x, masked, stats, rstd, shift, ident[:, :],
                        {"key_side": W["key_row1"][:, :], "query_side": W["query_row1"][:, :],
                         "bias": W["bias1"][:, :], "other": W["other1"][:, :]},
                        (keys_dram, row_ids, wanted, counts))
        descend(3, found[:, 1, :], found[:, 0, :])
        masked_ctx.close()
        renew_semaphores()
        finish_norm(nc, sem, stats, scratch, rstd, shift, "gat")
        gates = keep("gates", [P, GRAPHS, TOP_EXPERTS])
        with ExitStack() as ctx:
            def sb(name, shape, dt=F32):
                return ctx.enter_context(nc.sbuf_tensor(name, shape, dt))

            node, last_node = sb("node", [P, NODES, TAB]), sb("last_node", [P, TAB])
            first_edge, degree, clamped, loops = sb("first_edge", [P, NODES]), sb("degree", [P, NODES]), sb("clamped", [P, NODES]), sb("loops", [P, 2], I32)
            with ExitStack() as inner:
                tab, gat_w, att, part = (inner.enter_context(nc.sbuf_tensor(n, s, F32)) for n, s in (
                    ("tab", [P, GRAPHS, TAB]), ("gat_w", [P, TAB]), ("att", [P, 2, GAT]), ("att_part", [P, 2, GAT])))
                with nc.Block() as block:
                    loaded, made = sem("gat_loaded"), sem("gat_made")

                    @block.sync
                    def _(sp):
                        sp.dma_start(gat_w[:, 0:GAT], a["gat_w"]).then_inc(loaded, 16)
                        sp.dma_start(att[:, :, :], bass.AP(a["att"].tensor, 0, [[0, P], [1, 2 * GAT]]).rearrange("p (a c) -> p a c", a=2)).then_inc(loaded, 16)

                    @block.vector
                    def _(dve):
                        dve.wait_ge(loaded, 32)
                        dve.tensor_tensor(part[:, :, :], att[:, :, :], gat_w[:, 0:GAT].unsqueeze(1).to_broadcast([P, 2, GAT]), ALU.mult).then_inc(made, 1)
                        dve.wait_ge(made, 1)
                        dve.tensor_reduce(gat_w[:, GAT:TAB], part[:, :, :].rearrange("p a (h e) -> p (a h) e", h=HEADS), AX_X, ALU.add)

                project(nc, sem, "gat", x, rstd, shift, ident[:, :], gat_w[:, :], TAB, tab)
                prepare_nodes(nc, sem, tab, table_dram, node, last_node, ident[:, :], ones, wanted, found, counted[:, :],
                              first_edge, degree, clamped, loops)
            gather_edges_and_experts1(nc, sem, a, x, rstd, shift, source_ids, table_dram[:, 0:TAB], edges_dram, results_dram,
                                      loops, ident[:, :])
            attend_edges(nc, sem, a, edges_dram, node, last_node, first_edge, degree, clamped, loops, gates, ident[:, :])
        renew_semaphores()
        combine_experts1(nc, sem, x, gates, results_dram, out)


_OUTS = [((GRAPHS, NODES, FEAT), "float32")]


def kernel(**inputs):
    import numpy as _np
    import concourse.bacc as _bacc
    from concourse import mybir as _mybir
    from concourse.bass_utils import run_bass_kernel_spmd as _run

    i = {k: _np.asarray(v) for k, v in inputs.items()}
    hc, hc1 = HC, HC1
    laid = {
        "x": i["x"].transpose(1, 0, 2),
        "adj": i["adj"].transpose(1, 0, 2).reshape(P, -1),
        "edges": i["L1_ffn_edge_index"],
        "gnn0_wT": i["L0_gnn_W"].T,
        "gnn0_a12": i["L0_gnn_a_12"],
        "gnn0_a": _np.concatenate([i["L0_gnn_a_1"], i["L0_gnn_a_2"]], 1),
        "gnn0_w1": i["L0_gnn_W_1"],
        "gnn0_w2": i["L0_gnn_W_2"],
        "gnn1_w": i["L1_gnn_W"],
        "gnn1_wT": i["L1_gnn_W"].T,
        "gnn1_aT": i["L1_gnn_a"].T,
        "gnn1_bias": i["L1_gnn_bias"],
        "gate_w": i["L0_ffn_gate_w"],
        "gate_b": i["L0_ffn_gate_b"],
        "w1": i["L0_ffn_w1"],
        "b1T": i["L0_ffn_b1"].reshape(EXPERTS, hc, P).transpose(0, 2, 1),
        "w2": i["L0_ffn_w2"].reshape(EXPERTS, hc, P, FEAT).transpose(0, 2, 1, 3),
        "b2": i["L0_ffn_b2"],
        "gat_w": i["L1_ffn_W_gat"],
        "att": _np.stack([i["L1_ffn_att_src"].reshape(-1), i["L1_ffn_att_dst"].reshape(-1)]),
        "gat_b": i["L1_ffn_b_gat"],
        "gamma": i["L1_ffn_ln_gamma"],
        "beta": i["L1_ffn_ln_beta"],
        "w1b": i["L1_ffn_W1"].transpose(1, 0, 2),
        "b1b": i["L1_ffn_b1"].reshape(TOP_EXPERTS, hc1, P).transpose(2, 0, 1).reshape(P, -1),
        "w2b": i["L1_ffn_W2"].reshape(TOP_EXPERTS, hc1, P, FEAT).transpose(2, 0, 1, 3).reshape(P, -1, FEAT),
        "b2b": i["L1_ffn_b2"],
    }
    nc = _bacc.Bacc("TRN2", target_bir_lowering=False, num_devices=1)
    arrays, args = {}, {}
    for name, a in laid.items():
        a = _np.ascontiguousarray(a)
        arrays[f"in_{name}_dram"] = a
        args[name] = nc.dram_tensor(f"in_{name}_dram", a.shape, _mybir.dt.from_np(a.dtype), kind="ExternalInput").ap()
    (shape, dtype), = _OUTS
    out = nc.dram_tensor("out_dram", (NODES, GRAPHS, FEAT), _mybir.dt.from_np(_np.dtype(dtype)), kind="ExternalOutput").ap()
    build(nc, args, out)
    r = _run(nc, [arrays], core_ids=[0])
    return _np.ascontiguousarray(_np.asarray(r.results[0]["out_dram"]).transpose(1, 0, 2))
```
